# Optimizing a Trainium2 kernel written in Bass

```python
import numpy as np
import jax
import jax.numpy as jnp

def _softmax(x, axis=-1):
    return jax.nn.softmax(x, axis=axis)

def _gelu(x):
    return jax.nn.gelu(x, approximate=True)

def _silu(x):
    return jax.nn.silu(x)

def _sigmoid(x):
    return jax.nn.sigmoid(x)

def _layernorm(x, axis=-1, eps=1e-05):
    m = jnp.mean(x, axis=axis, keepdims=True)
    v = jnp.var(x, axis=axis, keepdims=True)
    return (x - m) / jnp.sqrt(v + eps)

def _scatter_add(tgt, idx, src, axis=0):
    return tgt.at[idx].add(src)

def _segment_sum(src, seg, n):
    return jax.ops.segment_sum(src, seg, n)
kernel_name = 'mk_gps_d1_gnn_r8_e6e532'

def setup_inputs(seed: int=0):
    np.random.seed(seed)
    _w = jnp.asarray

    def _rec_inputs():
        import jax
        import jax.numpy as jnp
        _gk = jax.random.key(seed)
        x = -0.0002117 + 1 * jax.random.normal(jax.random.fold_in(_gk, 1), (6250, 512), jnp.float32)
        src = jax.random.randint(jax.random.fold_in(_gk, 2), (100000,), 0, 6250, jnp.int32)
        dst = jnp.minimum((6250 * jax.random.uniform(jax.random.fold_in(_gk, 3), (100000,)) ** 2.0).astype(jnp.int32), 49999)
        _o = jnp.argsort(dst, stable=True)
        src = src[_o]
        dst = dst[_o]
        return (x, src, dst)
    x, src, dst = _rec_inputs()

    def _L0_gnn_setup():
        import jax, jax.numpy as jnp
        import numpy as np
        N_NODES = 6250
        N_EDGES = 50000
        IN_DIM = 512
        OUT_DIM = 512
        key = jax.random.key(seed)
        k1, k2, k3, k4 = jax.random.split(key, 4)
        x = jax.random.normal(k1, (N_NODES, IN_DIM), dtype=jnp.float32)
        edge_index = jax.random.randint(k2, (2, N_EDGES), 0, N_NODES, dtype=jnp.int64)
        W = jax.random.normal(k3, (OUT_DIM, IN_DIM), dtype=jnp.float32) / np.sqrt(IN_DIM)
        b = jax.random.normal(k4, (OUT_DIM,), dtype=jnp.float32) * 0.01
        return {'x': x, 'edge_index': edge_index, 'W': W, 'b': b}
    _L0_gnn_all = _L0_gnn_setup()
    _L0_gnn_in = {k: v for k, v in _L0_gnn_all.items() if k in ('W', 'b')}
    del _L0_gnn_all

    def _L0_mix_setup():
        import jax, jax.numpy as jnp
        import numpy as np
        DIM = 512
        HEADS = 8
        DIM_HEAD = 64
        INNER = HEADS * DIM_HEAD
        EPS = 1e-05

        def _per_head_layernorm(t, gamma, beta):
            mu = jnp.mean(t, axis=-1, keepdims=True)
            var = jnp.mean(jnp.square(t - mu), axis=-1, keepdims=True)
            t_hat = (t - mu) * jax.lax.rsqrt(var + EPS)
            return t_hat * gamma[None, :, None, :] + beta[None, :, None, :]
        key = jax.random.key(seed)
        ks = jax.random.split(key, 6)
        x = jax.random.normal(ks[0], (4, 1024, DIM), dtype=jnp.float32)
        std_qkv = 0.0001 * np.sqrt(2.0 / (3 * INNER + DIM))
        W_qkv = jax.random.normal(ks[1], (3 * INNER, DIM), dtype=jnp.float32) * std_qkv
        gamma_K = jnp.ones((HEADS, DIM_HEAD), dtype=jnp.float32)
        beta_K = jnp.zeros((HEADS, DIM_HEAD), dtype=jnp.float32)
        gamma_V = jnp.ones((HEADS, DIM_HEAD), dtype=jnp.float32)
        beta_V = jnp.zeros((HEADS, DIM_HEAD), dtype=jnp.float32)
        std_out = np.sqrt(1.0 / INNER)
        W_out = jax.random.uniform(ks[2], (DIM, INNER), dtype=jnp.float32, minval=-std_out, maxval=std_out)
        b_out = jax.random.uniform(ks[3], (DIM,), dtype=jnp.float32, minval=-std_out, maxval=std_out)
        return {'x': x, 'W_qkv': W_qkv, 'gamma_K': gamma_K, 'beta_K': beta_K, 'gamma_V': gamma_V, 'beta_V': beta_V, 'W_out': W_out, 'b_out': b_out}
    _L0_mix_all = _L0_mix_setup()
    _L0_mix_in = {k: v for k, v in _L0_mix_all.items() if k in ('W_qkv', 'gamma_K', 'beta_K', 'gamma_V', 'beta_V', 'W_out', 'b_out')}
    del _L0_mix_all

    def _L0_ffn_setup():
        import jax, jax.numpy as jnp
        import numpy as np
        D, H, E, K = (512, 256, 8, 2)
        EPS = 1e-05

        def _ln(x, g, b):
            m = jnp.mean(x, axis=-1, keepdims=True)
            v = jnp.var(x, axis=-1, keepdims=True)
            return (x - m) * jax.lax.rsqrt(v + EPS) * g + b
        key = jax.random.key(seed)
        ks = jax.random.split(key, 12)
        s = 0.02
        return {'x': jax.random.normal(ks[0], (2, 256, D), jnp.float32), 'Wg1': jax.random.normal(ks[1], (D, 2 * E), jnp.float32) * s, 'bg1': jnp.zeros((2 * E,), jnp.float32), 'Wg2': jax.random.normal(ks[2], (2 * E, E), jnp.float32) * s, 'bg2': jnp.zeros((E,), jnp.float32), 'W1': jax.random.normal(ks[3], (E, D, H), jnp.float32) * s, 'b1': jnp.zeros((E, H), jnp.float32), 'g1': jnp.ones((E, H), jnp.float32), 'be1': jnp.zeros((E, H), jnp.float32), 'W2': jax.random.normal(ks[4], (E, H, H), jnp.float32) * s, 'b2': jnp.zeros((E, H), jnp.float32), 'g2': jnp.ones((E, H), jnp.float32), 'be2': jnp.zeros((E, H), jnp.float32), 'W3': jax.random.normal(ks[5], (E, H, D), jnp.float32) * s, 'b3': jnp.zeros((E, D), jnp.float32)}
    _L0_ffn_all = _L0_ffn_setup()
    _L0_ffn_in = {k: v for k, v in _L0_ffn_all.items() if k in ('Wg1', 'bg1', 'Wg2', 'bg2', 'W1', 'b1', 'g1', 'be1', 'W2', 'b2', 'g2', 'be2', 'W3', 'b3')}
    del _L0_ffn_all
    return {'x': x, 'src': src, 'dst': dst, 'L0_gnn_W': _L0_gnn_in['W'], 'L0_gnn_b': _L0_gnn_in['b'], 'L0_mix_W_qkv': _L0_mix_in['W_qkv'], 'L0_mix_gamma_K': _L0_mix_in['gamma_K'], 'L0_mix_beta_K': _L0_mix_in['beta_K'], 'L0_mix_gamma_V': _L0_mix_in['gamma_V'], 'L0_mix_beta_V': _L0_mix_in['beta_V'], 'L0_mix_W_out': _L0_mix_in['W_out'], 'L0_mix_b_out': _L0_mix_in['b_out'], 'L0_ffn_Wg1': _L0_ffn_in['Wg1'], 'L0_ffn_bg1': _L0_ffn_in['bg1'], 'L0_ffn_Wg2': _L0_ffn_in['Wg2'], 'L0_ffn_bg2': _L0_ffn_in['bg2'], 'L0_ffn_W1': _L0_ffn_in['W1'], 'L0_ffn_b1': _L0_ffn_in['b1'], 'L0_ffn_g1': _L0_ffn_in['g1'], 'L0_ffn_be1': _L0_ffn_in['be1'], 'L0_ffn_W2': _L0_ffn_in['W2'], 'L0_ffn_b2': _L0_ffn_in['b2'], 'L0_ffn_g2': _L0_ffn_in['g2'], 'L0_ffn_be2': _L0_ffn_in['be2'], 'L0_ffn_W3': _L0_ffn_in['W3'], 'L0_ffn_b3': _L0_ffn_in['b3']}

def reference(x, src, dst, L0_gnn_W, L0_gnn_b, L0_mix_W_qkv, L0_mix_gamma_K, L0_mix_beta_K, L0_mix_gamma_V, L0_mix_beta_V, L0_mix_W_out, L0_mix_b_out, L0_ffn_Wg1, L0_ffn_bg1, L0_ffn_Wg2, L0_ffn_bg2, L0_ffn_W1, L0_ffn_b1, L0_ffn_g1, L0_ffn_be1, L0_ffn_W2, L0_ffn_b2, L0_ffn_g2, L0_ffn_be2, L0_ffn_W3, L0_ffn_b3):
    import jax
    import jax.numpy as jnp

    def _L0_gnn_ref(x, edge_index, W, b):
        import jax, jax.numpy as jnp
        import numpy as np
        N_NODES = 6250
        N_EDGES = 50000
        IN_DIM = 512
        OUT_DIM = 512
        n = x.shape[0]
        loops = jnp.arange(n, dtype=edge_index.dtype)
        row = jnp.concatenate([edge_index[0], loops])
        col = jnp.concatenate([edge_index[1], loops])
        deg = jax.ops.segment_sum(jnp.ones(row.shape[0], dtype=x.dtype), row, num_segments=n)
        dis = jax.lax.rsqrt(deg)
        norm = dis[row] * dis[col]
        h = x @ W.T + b
        out = jax.ops.segment_sum(norm[:, None] * h[row], col, num_segments=n)
        return jax.nn.relu(out)

    def _L0_mix_ref(x, W_qkv, gamma_K, beta_K, gamma_V, beta_V, W_out, b_out):
        import jax, jax.numpy as jnp
        import numpy as np
        DIM = 512
        HEADS = 8
        DIM_HEAD = 64
        INNER = HEADS * DIM_HEAD
        EPS = 1e-05

        def _per_head_layernorm(t, gamma, beta):
            mu = jnp.mean(t, axis=-1, keepdims=True)
            var = jnp.mean(jnp.square(t - mu), axis=-1, keepdims=True)
            t_hat = (t - mu) * jax.lax.rsqrt(var + EPS)
            return t_hat * gamma[None, :, None, :] + beta[None, :, None, :]
        b, n, _ = x.shape
        qkv = jnp.einsum('bnd,ed->bne', x, W_qkv)
        q, k, v = jnp.split(qkv, 3, axis=-1)

        def to_heads(t):
            return t.reshape(b, n, HEADS, DIM_HEAD).transpose(0, 2, 1, 3)
        q, k, v = (to_heads(q), to_heads(k), to_heads(v))
        k = _per_head_layernorm(k, gamma_K, beta_K)
        v = _per_head_layernorm(v, gamma_V, beta_V)
        p_attn = jnp.einsum('bhnk,bhnv->bhkv', k, v) / n
        out = jnp.einsum('bhnk,bhkv->bhnv', q, p_attn)
        out = out.transpose(0, 2, 1, 3).reshape(b, n, INNER)
        return jnp.einsum('bne,de->bnd', out, W_out) + b_out

    def _L0_ffn_ref(x, Wg1, bg1, Wg2, bg2, W1, b1, g1, be1, W2, b2, g2, be2, W3, b3):
        import jax, jax.numpy as jnp
        import numpy as np
        D, H, E, K = (512, 256, 8, 2)
        EPS = 1e-05

        def _ln(x, g, b):
            m = jnp.mean(x, axis=-1, keepdims=True)
            v = jnp.var(x, axis=-1, keepdims=True)
            return (x - m) * jax.lax.rsqrt(v + EPS) * g + b
        B, S, d = x.shape
        t = x.reshape(-1, d)
        logits = jax.nn.gelu(t @ Wg1 + bg1, approximate=False) @ Wg2 + bg2
        gates_full = jax.nn.softmax(logits, axis=-1)
        topv, topi = jax.lax.top_k(gates_full, K)
        topv = topv / jnp.sum(topv, axis=-1, keepdims=True)
        cw = jnp.sum(jax.nn.one_hot(topi, E, dtype=t.dtype) * topv[..., None], axis=1)
        h = jnp.einsum('td,edh->eth', t, W1) + b1[:, None, :]
        h = jax.nn.gelu(_ln(h, g1[:, None, :], be1[:, None, :]), approximate=False)
        h = jnp.einsum('eth,ehg->etg', h, W2) + b2[:, None, :]
        h = jax.nn.gelu(_ln(h, g2[:, None, :], be2[:, None, :]), approximate=False)
        o = jnp.einsum('eth,eho->eto', h, W3) + b3[:, None, :]
        out = jnp.einsum('te,eto->to', cw, o)
        return out.reshape(B, S, -1)
    edge_index = jnp.stack([src, dst])
    xn = _layernorm(x, axis=-1)
    x = x + _L0_gnn_ref(xn, edge_index, L0_gnn_W, L0_gnn_b) + _L0_mix_ref(xn[None], L0_mix_W_qkv, L0_mix_gamma_K, L0_mix_beta_K, L0_mix_gamma_V, L0_mix_beta_V, L0_mix_W_out, L0_mix_b_out)[0]
    x = x + _L0_ffn_ref(_layernorm(x, axis=-1)[None], L0_ffn_Wg1, L0_ffn_bg1, L0_ffn_Wg2, L0_ffn_bg2, L0_ffn_W1, L0_ffn_b1, L0_ffn_g1, L0_ffn_be1, L0_ffn_W2, L0_ffn_b2, L0_ffn_g2, L0_ffn_be2, L0_ffn_W3, L0_ffn_b3)[0]
    return x

_drawn_inputs = setup_inputs


def setup_inputs(seed=0):
    import zlib

    import numpy as np

    out = dict(_drawn_inputs(seed))
    spreads = {'L0_mix_gamma_K': (1.0, 0.6),
     'L0_mix_beta_K': (0.0, 2.0),
     'L0_mix_gamma_V': (1.0, 0.6),
     'L0_mix_beta_V': (0.0, 2.0),
     'L0_ffn_bg1': (0.0, 0.1),
     'L0_ffn_bg2': (0.0, 0.1),
     'L0_ffn_b1': (0.0, 0.292),
     'L0_ffn_g1': (1.0, 0.561),
     'L0_ffn_be1': (0.0, 0.545),
     'L0_ffn_b2': (0.0, 0.1),
     'L0_ffn_g2': (1.0, 0.6),
     'L0_ffn_be2': (0.0, 0.552),
     'L0_ffn_b3': (0.0, 0.1)}
    factors = {'L0_gnn_b': 4.543, 'L0_mix_W_qkv': 25.741, 'L0_mix_W_out': 25.292, 'L0_mix_b_out': 3.043}
    for name, (base, spread) in spreads.items():
        noise = np.random.default_rng([zlib.crc32(name.encode()), seed]).standard_normal(out[name].shape)
        drawn = base * np.exp(spread * noise) if base else spread * noise
        out[name] = jnp.asarray(drawn.astype(out[name].dtype))
    for name, factor in factors.items():
        out[name] = (out[name] * factor).astype(out[name].dtype)
    return out
```

```python
from contextlib import ExitStack

import concourse.bass as bass
import numpy as np
from concourse import mybir

P = 128
D = 512
KD = D // P
HEADS = 8
DH = 64
H2 = 256
EXPERTS = 8
GATE = 16
EPS = 1e-5

F32 = mybir.dt.float32
F16 = mybir.dt.float16
I32 = mybir.dt.int32
ALU = mybir.AluOpType
ACT = mybir.ActivationFunctionType
AX = mybir.AxisListType

SUPER = 8
TABLE_SCALE = 2.0 ** 10
LOW_SCALE = 2.0 ** 11


class Chain:

    def __init__(self, engine, sem, start=0):
        self.engine, self.sem, self.start, self.n = engine, sem, start, 0

    def mark(self, ins):
        ins.then_inc(self.sem, 1)
        self.n += 1

    def wait(self):
        self.engine.wait_ge(self.sem, self.start + self.n)

    def then(self, ins):
        self.mark(ins)
        self.wait()


def shapes(n_nodes, n_edges):
    s = lambda: None
    s.nodes = n_nodes
    s.tiles = -(-n_nodes // P)
    s.last = n_nodes - (s.tiles - 1) * P
    s.per_tile = -(-n_edges // P // s.tiles)
    s.chunks = s.per_tile * s.tiles
    s.supers = s.chunks // SUPER
    s.slot_tiles = (2 * s.tiles * P) // P + EXPERTS
    s.group = 7
    assert s.tiles % s.group == 0 and s.chunks % SUPER == 0 and s.supers == 2 * s.tiles
    return s


def allocate(nc, ctx, stage, lasting=None):
    sb = lambda name, shape, dt=F32: ctx.enter_context(nc.sbuf_tensor(f"{stage}_{name}", shape, dt))
    ps = lambda name, shape, dt=F32: ctx.enter_context(nc.psum_tensor(f"{stage}_{name}", shape, dt))
    sem = lambda name: (lasting or ctx).enter_context(nc.semaphore(f"{stage}_{name}"))
    return sb, ps, sem


def at(i, n=1):
    return bass.ds(i, n)


def by_pairs(engine, tiles, body):
    body(0, 0, True)
    body(1, 1, True)
    with engine.Fori(1, tiles // 2) as pair:
        body(2 * pair, 0, False)
        body(2 * pair + 1, 1, False)
    body(tiles - 1, 0, False)


def moments(v, step, stats, mean, var, half):
    step.mark(v.tensor_tensor(mean[:], stats[:, :, 1], stats[:, :, 4], ALU.add))
    step.mark(v.tensor_tensor(half[:], stats[:, :, 1], stats[:, :, 4], ALU.subtract))
    step.then(v.tensor_tensor(var[:], stats[:, :, 2], stats[:, :, 5], ALU.add))
    step.mark(v.tensor_scalar(mean[:], mean[:], 0.5, None, ALU.mult))
    step.mark(v.scalar_tensor_tensor(half[:], half[:], 0.25, half[:], ALU.mult, ALU.mult))
    step.then(v.tensor_scalar(var[:], var[:], 1.0 / D, None, ALU.mult))
    step.then(v.tensor_tensor(var[:], var[:], half[:], ALU.add))


def refine_root(v, step, r, a, spare):
    step.then(v.tensor_tensor(spare, r, r, ALU.mult))
    step.then(v.tensor_tensor(spare, spare, a, ALU.mult))
    step.then(v.tensor_scalar(spare, spare, -0.5, 1.5, ALU.mult, ALU.add))
    step.then(v.tensor_tensor(r, r, spare, ALU.mult))


def prepare_edges(nc, s, t, dram):
    with ExitStack() as ctx:
        sb, ps, sem = allocate(nc, ctx, "prepare_edges", t.lasting)
        T, C, U = s.tiles, s.chunks, s.supers
        low = sb("src_low_int", [P, C], I32)
        high = sb("src_high_int", [P, C], I32)
        dst_int = sb("dst_int", [P, C], I32)
        low_f = sb("src_low", [P, C])
        high_f = sb("src_high", [P, C])
        hot_low = sb("hot_low", [P, 2, s.per_tile, P], F16)
        hot_high = sb("hot_high", [P, 2, s.per_tile, T], F16)
        gap = sb("gap", [P, 2, s.per_tile, T], F16)
        gap2 = sb("gap2", [P, s.per_tile, T], F16)
        stats = sb("stats", [P, T, 6])
        var = sb("var", [P, T])
        half = sb("half", [P, T])
        ends = sb("ends", [U, 2])
        ends_int = sb("ends_int", [U, 2], I32)
        ends_block = sb("ends_block", [U, 2], I32)
        span = sb("span", [U, 5])
        deg = sb("deg", [P, T])
        root = sb("root", [P, T])
        sd = sb("sd", [P, T])
        upper = sb("upper", [P, P])
        zero = sb("zero", [P, P], F16)
        ps_dst = ps("ps_dst", [P, SUPER * P])
        ps_deg = ps("ps_deg", [P, 512])
        ps_rows = ps("ps_rows", [P, 512])

        load_small = sem("load_small")
        load_x = sem("load_x")
        split = sem("split")
        low_ready = sem("low_ready")
        gap_ready = sem("gap_ready")
        gap_squared = sem("gap_squared")
        high_ready = sem("high_ready")
        hot_used = sem("hot_used")
        dst_turned = sem("dst_turned")
        dve = sem("dve_steps")
        bn = sem("bn_steps")
        rows_in = sem("rows_in")
        rows_out = sem("rows_out")
        zeroed = sem("zeroed")
        deg_done = sem("deg_done")
        roots_in = sem("roots_in")
        roots_out = sem("roots_out")

        with nc.Block() as block:

            @block.sync
            def _(sp):
                sp.dma_start(t.src[:], dram["src"]).then_inc(load_small, 16)
                sp.dma_start(dst_int[:], dram["dst"]).then_inc(load_small, 16)
                sp.dma_start(t.ident[:], dram["ident"]).then_inc(load_small, 16)
                sp.dma_start(upper[:], dram["upper"]).then_inc(load_small, 16)
                sp.dma_start(t.iota[:], dram["iota"]).then_inc(load_small, 16)
                sp.dma_start(t.neg_block[:], dram["neg_block"]).then_inc(load_small, 16)
                xv = dram["x"].rearrange("(t p) d -> p t d", p=P)
                def load(g):
                    sp.dma_start(t.acc[:, at(g * s.group, s.group), :],
                                 xv[:, at(g * s.group, s.group), :]).then_inc(load_x, 16)

                load(0)
                with sp.Fori(1, T // s.group) as g:
                    sp.wait_ge(load_x, g * 16)
                    load(g)

            @block.gpsimd
            def _(pool):
                pool.memset(zero[:], 0.0).then_inc(zeroed, 1)
                pool.wait_ge(load_small, 96)
                pool.wait_ge(split, 4)
                shape = [P, s.per_tile, T]
                blocks = t.iota[:, 0:T].unsqueeze(1).to_broadcast(shape)

                def gaps(i, slot, first):
                    if not first:
                        pool.wait_ge(gap_squared, i - 1)
                    pool.tensor_tensor(gap[:, slot], high_f[:, at(i * s.per_tile, s.per_tile)].unsqueeze(2).to_broadcast(shape),
                                       blocks, ALU.subtract).then_inc(gap_ready, 1)

                gaps(0, 0, True)
                gaps(1, 1, True)
                with pool.Fori(1, T // 2) as pair:
                    i = 2 * pair
                    gaps(i, 0, False)
                    gaps(i + 1, 1, False)
                gaps(T - 1, 0, False)

            @block.vector
            def _(v):
                v.wait_ge(load_small, 96)
                v.tensor_copy(t.dst[:], dst_int[:]).then_inc(split, 1)
                v.tensor_single_scalar(high[:], t.src[:], 7, op=ALU.logical_shift_right).then_inc(split, 1)
                v.tensor_single_scalar(low[:], t.src[:], P - 1, op=ALU.bitwise_and).then_inc(split, 1)
                v.wait_ge(split, 3)
                v.tensor_copy(high_f[:], high[:]).then_inc(split, 1)
                v.tensor_copy(low_f[:], low[:]).then_inc(split, 1)
                v.wait_ge(split, 5)

                step = Chain(v, dve)
                v.wait_ge(dst_turned, 1)
                step.mark(v.tensor_reduce(ends[:, 0:1], ps_dst[0:U, :], AX.X, ALU.max))
                step.then(v.tensor_reduce(ends[:, 1:2], ps_dst[0:U, :], AX.X, ALU.min))
                step.then(v.tensor_copy(ends_int[:], ends[:]))
                step.then(v.tensor_single_scalar(ends_block[:], ends_int[:], 7, op=ALU.logical_shift_right))
                step.then(v.tensor_copy(span[:, 0:2], ends_block[:]))
                step.mark(v.tensor_scalar(span[:, 4:5], span[:, 1:2], -1.0, float(T), ALU.mult, ALU.add))
                step.then(v.tensor_scalar(span[:, 3:4], span[:, 0:1], 1.0, None, ALU.add))
                v.tensor_tensor(span[:, 2:3], span[:, 0:1], span[:, 1:2], ALU.subtract).then_inc(rows_in, 1)
                v.wait_ge(rows_out, 1)
                v.tensor_copy(t.visits[:], ps_rows[0:1, 0:3 * U])

                def low_hots(i, slot, first):
                    if not first:
                        v.wait_ge(hot_used, i - 1)
                    for c in range(s.per_tile):
                        hot = v.tensor_scalar(hot_low[:, slot, c, :], t.iota[:], low_f[:, at(i * s.per_tile + c)],
                                              None, ALU.is_equal)
                    hot.then_inc(low_ready, 1)

                low_hots(0, 0, True)
                low_hots(1, 1, True)
                with v.Fori(1, T // 2) as pair:
                    i = 2 * pair
                    low_hots(i, 0, False)
                    low_hots(i + 1, 1, False)
                low_hots(T - 1, 0, False)

                with v.Fori(0, T // s.group) as g:
                    v.wait_ge(load_x, g * 16 + 16)
                    for j in range(s.group):
                        v.bn_stats(stats[:, at(g * s.group + j)].squeeze(1),
                                   t.acc[:, at(g * s.group + j)].squeeze(1)).then_inc(bn, 1)
                v.wait_ge(bn, T)
                step = Chain(v, dve, step.n)
                moments(v, step, stats, t.mean, var, half)
                step.then(v.tensor_scalar(var[:], var[:], EPS, None, ALU.add))
                v.wait_ge(deg_done, 1)
                step.then(v.tensor_scalar(deg[:], ps_deg[:, 0:T], 1.0, None, ALU.add))
                v.sem_inc(roots_in, 1)
                v.wait_ge(roots_out, 2)
                step.mark(v.reciprocal(t.rstd[:], sd[:]))
                step.then(v.reciprocal(t.dis[:], root[:]))
                refine_root(v, step, t.rstd[:], var[:], sd[:])
                refine_root(v, step, t.dis[:], deg[:], root[:])
                v.tensor_scalar(t.dis_table[:], t.dis[:], TABLE_SCALE, None, ALU.mult)
                v.tensor_scalar(t.dis_back[:], t.dis[:], 1.0 / TABLE_SCALE, None, ALU.mult)

            @block.scalar
            def _(a):
                def high_hots(i, slot, first):
                    a.wait_ge(gap_ready, i + 1)
                    if not (first and slot == 0):
                        a.wait_ge(high_ready, i)
                    a.activation(gap2[:], gap[:, slot], ACT.Square).then_inc(gap_squared, 1)
                    a.wait_ge(gap_squared, i + 1)
                    if not first:
                        a.wait_ge(hot_used, i - 1)
                    a.activation(hot_high[:, slot], gap2[:], ACT.Relu, bias=1.0, scale=-1.0).then_inc(high_ready, 1)

                high_hots(0, 0, True)
                high_hots(1, 1, True)
                with a.Fori(1, T // 2) as pair:
                    i = 2 * pair
                    high_hots(i, 0, False)
                    high_hots(i + 1, 1, False)
                high_hots(T - 1, 0, False)
                a.wait_ge(roots_in, 1)
                a.activation(root[:], deg[:], ACT.Sqrt).then_inc(roots_out, 1)
                a.activation(sd[:], var[:], ACT.Sqrt).then_inc(roots_out, 1)

            @block.tensor
            def _(pe):
                pe.wait_ge(load_small, 96)
                pe.wait_ge(split, 1)
                for k in range(SUPER):
                    turn = pe.transpose(ps_dst[0:U, k * P:(k + 1) * P], t.dst[:, k::SUPER], t.ident[:])
                turn.then_inc(dst_turned, 1)
                pe.wait_ge(rows_in, 1)
                for n, column, square, start, stop in ((0, 1, t.ident, True, True), (1, 3, t.ident, True, True),
                                                       (2, 4, t.ident, True, False), (2, 2, upper, False, True)):
                    mm = pe.matmul(ps_rows[0:1, n * U:(n + 1) * U], span[:, column:column + 1], square[0:U, 0:U],
                                   start=start, stop=stop)
                mm.then_inc(rows_out, 1)
                pe.wait_ge(zeroed, 1)
                pe.matmul(ps_deg[:, 0:T], zero[:], t.iota[:, 0:T], start=True, stop=True)

                def count(i, slot):
                    pe.wait_ge(high_ready, i + 1)
                    pe.wait_ge(low_ready, i + 1)
                    for c in range(s.per_tile):
                        mm = pe.matmul(ps_deg[:, 0:T], hot_low[:, slot, c, :], hot_high[:, slot, c, :],
                                       start=False, stop=True, skip_group_check=True)
                    mm.then_inc(hot_used, 1)

                with pe.Fori(0, T // 2) as pair:
                    i = 2 * pair
                    count(i, 0)
                    count(i + 1, 1)
                count(T - 1, 0)
                pe.wait_ge(hot_used, T)
                pe.sem_inc(deg_done, 1)


def prepare_table(nc, s, t, dram):
    with ExitStack() as ctx:
        sb, ps, sem = allocate(nc, ctx, "prepare_table", t.lasting)
        T = s.tiles
        xn = sb("xn", [P, 2, D])
        xt = sb("xt", [P, 2, D])
        rest = sb("rest", [P, 2, D])
        halves = sb("halves", [P, 2, 2 * D], F16)
        ps_xt = [ps(f"ps_xt{i}", [P, D]) for i in range(2)]
        xn_ready = sem("xn_ready")
        turned = sem("turned")
        xt_ready = sem("xt_ready")
        scaled = sem("scaled")
        high_ready = sem("high_ready")
        rest_ready = sem("rest_ready")
        low_ready = sem("low_ready")
        xt_stored = [sem(f"xt_stored{i}") for i in range(2)]
        table_stored = [sem(f"table_stored{i}") for i in range(2)]
        table = dram["table"].rearrange("(t p) d -> t p d", p=P)

        def stores_before(i, slot):
            return 8 * (i - slot)

        with nc.Block() as block:

            @block.vector
            def _(v):
                def normalize(i, slot, first):
                    if not first:
                        v.wait_ge(turned, i - 1)
                        v.wait_ge(scaled, i - 1)
                    v.tensor_scalar(xn[:, slot], t.acc[:, at(i), :].squeeze(1), t.mean[:, at(i)], t.rstd[:, at(i)],
                                    ALU.subtract, ALU.mult).then_inc(xn_ready, 1)

                def halve(i, slot, first):
                    v.wait_ge(scaled, i + 1)
                    if not first:
                        v.wait_ge(table_stored[slot], stores_before(i, slot))
                    v.tensor_scalar(halves[:, slot, 0:D], t.acc[:, at(i), :].squeeze(1), 1.0, None,
                                    ALU.mult).then_inc(high_ready, 1)
                    v.wait_ge(high_ready, i + 1)
                    if not first:
                        v.wait_ge(low_ready, i - 1)
                    v.tensor_tensor(rest[:, slot], t.acc[:, at(i), :].squeeze(1), halves[:, slot, 0:D],
                                    ALU.subtract).then_inc(rest_ready, 1)

                normalize(0, 0, True)
                normalize(1, 1, True)
                halve(0, 0, True)
                normalize(2, 0, False)
                halve(1, 1, True)
                with v.Fori(1, T // 2) as pair:
                    i = 2 * pair
                    normalize(i + 1, 1, False)
                    halve(i, 0, False)
                    normalize(i + 2, 0, False)
                    halve(i + 1, 1, False)
                halve(T - 1, 0, False)

            @block.gpsimd
            def _(pool):
                def low(i, slot, first):
                    pool.wait_ge(rest_ready, i + 1)
                    if not first:
                        pool.wait_ge(table_stored[slot], stores_before(i, slot))
                    pool.sem_inc(held, 1)
                    pool.tensor_scalar(halves[:, slot, D:2 * D], rest[:, slot], LOW_SCALE, 1.0, ALU.mult,
                                       ALU.mult).then_inc(low_ready, 1)

                held = sem("held")
                by_pairs(pool, T, low)

            @block.scalar
            def _(a):
                def evacuate(i, slot, first):
                    a.wait_ge(xn_ready, i + 1)
                    a.activation(t.acc[:, at(i), :].squeeze(1), xn[:, slot], ACT.Identity,
                                 bias=t.dis_col(i, 0), scale=t.dis_col(i, 0)).then_inc(scaled, 1)
                    a.wait_ge(turned, i + 1)
                    if not first:
                        a.wait_ge(xt_stored[slot], stores_before(i, slot))
                    a.copy(xt[:, slot], ps_xt[slot][:]).then_inc(xt_ready, 1)

                by_pairs(a, T, evacuate)

            @block.tensor
            def _(pe):
                def turn(i, slot, first):
                    pe.wait_ge(xn_ready, i + 1)
                    if not first:
                        pe.wait_ge(xt_ready, i - 1)
                    for k in range(KD):
                        tr = pe.transpose(ps_xt[slot][:, k * P:(k + 1) * P], xn[:, slot, k * P:(k + 1) * P], t.ident[:])
                    tr.then_inc(turned, 1)

                by_pairs(pe, T, turn)

            @block.sync
            def _(sp):
                def store(i, slot, first):
                    sp.wait_ge(xt_ready, i + 1)
                    sp.dma_start(dram["xt"][at(i)].squeeze(0), xt[:, slot]).then_inc(xt_stored[slot], 16)
                    sp.wait_ge(low_ready, i + 1)
                    sp.dma_start(table[at(i)].squeeze(0), halves[:, slot]).then_inc(table_stored[slot], 16)

                by_pairs(sp, T, store)
                for slot, n in ((0, T // 2 + 1), (1, T // 2)):
                    sp.wait_ge(xt_stored[slot], 16 * n)
                    sp.wait_ge(table_stored[slot], 16 * n)


def aggregate(nc, s, t, dram):
    with ExitStack() as ctx:
        sb, ps, sem = allocate(nc, ctx, "aggregate", t.lasting)
        T, U = s.tiles, s.supers
        RING = 2 * SUPER
        rows = sb("rows", [P, RING, 2 * D], F16)
        index = sb("index", [P, 2, SUPER], I32)
        offsets = sb("offsets", [P, 3, SUPER])
        hot = sb("hot", [P, 3, SUPER, P], F16)
        hot_small = sb("hot_small", [P, 3, SUPER, P], F16)
        zero = sb("zero", [P, P])
        w = sb("w_kv", [P, KD, 2 * D])
        sums = sb("w_sums", [P, KD, 2 * HEADS])
        affine = sb("affine", [P, 4, D])
        xt = sb("xt_kv", [P, 2, D])
        square = sb("square", [P, 2, D])
        var = sb("var_kv", [P, 2, HEADS])
        rstd = sb("rstd_kv", [P, 2, HEADS])
        spare = sb("spare_kv", [P, HEADS])
        kv = sb("kv", [P, 2, 2, D])
        ps_sum = [ps("ps_sum0", [P, D]), ps("ps_sum1", [P, D]), ps("ps_sum2", [P, D])]
        ps_kv = [ps("ps_k", [P, D]), ps("ps_v", [P, D])]
        ps_p = ps("ps_p", [P, D])

        gathered = [sem(f"gathered{i}") for i in range(RING)]
        index_ready = sem("index_ready")
        go = sem("go")
        super_used = sem("super_used")
        placed, further_placed = sem("placed"), sem("further_placed")
        hot_ready, further_hot = sem("hot_ready"), sem("further_hot")
        small_ready, further_small = sem("small_ready"), sem("further_small")
        summed, further_summed = sem("summed"), sem("further_summed")
        added, further_added = sem("added"), sem("further_added")
        load_w = sem("load_w")
        w_ready = sem("w_ready")
        zeroed = sem("zeroed")
        loaded_xt = [sem(f"loaded_xt{i}") for i in range(2)]
        projected = [sem("projected_k"), sem("projected_v")]
        squared = [sem("squared_k"), sem("squared_v")]
        var_ready = [sem("var_ready_k"), sem("var_ready_v")]
        rooted = [sem("rooted_k"), sem("rooted_v")]
        kv_steps = [sem("kv_steps_k"), sem("kv_steps_v")]
        emptied = [sem("emptied_k"), sem("emptied_v")]
        normalized = [sem("normalized_k"), sem("normalized_v")]
        correlated = sem("correlated")
        w_steps = sem("w_steps")

        def span_of(engine, u):
            first, end, offset = (engine.value_load(t.visits[0:1, at(k * U + u)], min_val=lo, max_val=hi)
                                  for k, lo, hi in ((0, 0, T - 1), (1, 1, T), (2, 1, T * U + T)))
            return first, end, offset

        with nc.Block() as block:

            @block.sync
            def _(sp):
                sp.dma_start(w[:], dram["w_kv"].rearrange("(k p) n -> p k n", p=P)).then_inc(load_w, 16)
                for n, name in enumerate(("gamma_k", "beta_k", "gamma_v", "beta_v")):
                    sp.dma_start(affine[:, n], dram[name].partition_broadcast(P)).then_inc(load_w, 16)

                def load(i, slot, first):
                    if not first:
                        sp.wait_ge(projected[1], i - 1)
                    sp.dma_start(xt[:, slot], dram["xt"][at(i)].squeeze(0)).then_inc(loaded_xt[slot], 16)

                load(0, 0, True)
                load(1, 1, True)
                with sp.Fori(1, T // 2) as pair:
                    load(2 * pair, 0, False)
                    load(2 * pair + 1, 1, False)
                load(T - 1, 0, False)

            @block.gpsimd
            def _(pool):
                pool.memset(zero[:], 0.0).then_inc(zeroed, 1)

                def gather(u, half, first):
                    if not first:
                        pool.wait_ge(super_used, u - 1)
                        pool.sem_inc(go, 1)
                    pool.tensor_copy(index[:, half], t.src[:, at(u * SUPER, SUPER)]).then_inc(index_ready, 1)
                    pool.wait_ge(index_ready, u + 1)
                    pool.sem_inc(go, 1)
                    for k in range(SUPER):
                        slot = half * SUPER + k
                        pool.indirect_dma_start(
                            rows[:, slot], None, dram["table"],
                            bass.IndirectOffsetOnAxis(ap=index[:, half, k:k + 1], axis=0)).then_inc(gathered[slot], 16)

                gather(0, 0, True)
                gather(1, 1, True)
                with pool.Fori(1, T) as i:
                    gather(2 * i, 0, False)
                    gather(2 * i + 1, 1, False)

            @block.vector
            def _(v):
                v.sem_inc(further_placed, T + 1)
                v.sem_inc(further_hot, T + 1)
                v.sem_inc(further_added, T + 1)
                v.wait_ge(load_w, 80)
                step = Chain(v, w_steps)
                grouped = w[:].rearrange("p k (h e) -> p k h e", e=DH)
                step.then(v.tensor_reduce(sums[:], grouped, AX.X, ALU.add))
                step.then(v.tensor_scalar(sums[:], sums[:], 1.0 / DH, None, ALU.mult))
                v.tensor_tensor(grouped, grouped, sums[:].unsqueeze(3).to_broadcast([P, KD, 2 * HEADS, DH]),
                                ALU.subtract).then_inc(w_ready, 1)

                def make_hots(u, b, buffer, done, ready, n):
                    v.tensor_scalar(offsets[:, buffer], t.dst[:, at(u * SUPER, SUPER)], t.neg_block[:, at(b)], None,
                                    ALU.add).then_inc(done, 1)
                    v.wait_ge(done, n + 1)
                    shape = [P, SUPER, P]
                    v.tensor_tensor(hot[:, buffer], t.iota[:].unsqueeze(1).to_broadcast(shape),
                                    offsets[:, buffer].unsqueeze(2).to_broadcast(shape), ALU.is_equal).then_inc(ready, 1)

                def first_hots(u, parity, opening=False):
                    first, _, _ = span_of(v, u)
                    if not opening:
                        v.wait_ge(summed, u - 1)
                    make_hots(u, first, parity, placed, hot_ready, u)

                def add_visits(u, parity):
                    first, end, offset = span_of(v, u)
                    acc = t.acc[:, at(first)].squeeze(1)
                    v.wait_ge(summed, u + 1)
                    v.wait_ge(further_added, offset + first + 1)
                    if not isinstance(u, int) or u > 0:
                        v.wait_ge(added, u)
                    v.tensor_tensor(acc, ps_sum[parity][:], acc, ALU.add).then_inc(added, 1)
                    with v.If(first + 1 < end), v.Fori(first + 1, end) as b:
                        n = offset + b
                        v.wait_ge(further_summed, n)
                        make_hots(u, b, 2, further_placed, further_hot, n)
                        acc = t.acc[:, at(b)].squeeze(1)
                        v.wait_ge(further_summed, n + 1)
                        v.wait_ge(further_added, n)
                        v.wait_ge(added, u + 1)
                        v.tensor_tensor(acc, ps_sum[2][:], acc, ALU.add).then_inc(further_added, 1)

                def post(i, slot, kind, first):
                    per_head = [P, HEADS, DH]
                    v.wait_ge(squared[kind], i + 1)
                    step = Chain(v, kv_steps[kind], 6 * i)
                    step.then(v.tensor_reduce(var[:, kind], square[:, kind].rearrange("p (h e) -> p h e", e=DH), AX.X, ALU.add))
                    v.tensor_scalar(var[:, kind], var[:, kind], 1.0 / DH, EPS, ALU.mult, ALU.add).then_inc(var_ready[kind], 1)
                    out = kv[:, kind, slot]
                    if not first:
                        v.wait_ge(correlated, i - 1)
                    v.tensor_tensor(out, ps_kv[kind][:], affine[:, 2 * kind], ALU.mult).then_inc(emptied[kind], 1)
                    v.wait_ge(var_ready[kind], i + 1)
                    v.wait_ge(rooted[kind], i + 1)
                    step.then(v.reciprocal(rstd[:, kind], rstd[:, kind]))
                    refine_root(v, step, rstd[:, kind], var[:, kind], spare[:])
                    v.wait_ge(emptied[kind], i + 1)
                    heads = out.rearrange("p (h e) -> p h e", e=DH)
                    v.tensor_tensor(heads, heads, rstd[:, kind].unsqueeze(2).to_broadcast(per_head),
                                    ALU.mult).then_inc(normalized[kind], 1)
                    v.wait_ge(normalized[kind], 2 * i + 1)
                    v.tensor_tensor(out, out, affine[:, 2 * kind + 1], ALU.add).then_inc(normalized[kind], 1)

                def beside(i, slot, last=False):
                    number = i if isinstance(i, int) else T
                    first_hots(2 * i + 1, 1, number == 0)
                    add_visits(2 * i, 0)
                    if number > 0:
                        post(i - 1, 1 - slot, 1, number < 3)
                    if not last:
                        first_hots(2 * i + 2, 0)
                    add_visits(2 * i + 1, 1)
                    post(i, slot, 0, number < 2)

                first_hots(0, 0, True)
                for i in range(3):
                    beside(i, i % 2)
                with v.Fori(1, T // 2 - 1) as pair:
                    beside(2 * pair + 1, 1)
                    beside(2 * pair + 2, 0)
                beside(T - 2, 1)
                beside(T - 1, 0, True)
                post(T - 1, 0, 1, False)
                v.memset(t.p[:], 0.0).then_inc(zeroed, 1)
                v.wait_ge(zeroed, 2)
                v.wait_ge(correlated, T)
                for head in range(HEADS):
                    rows = slice(head % 2 * DH, head % 2 * DH + DH)
                    cols = slice(head * DH, head * DH + DH)
                    v.tensor_scalar(t.p[rows, cols], ps_p[rows, cols], 1.0 / s.nodes, None, ALU.mult)

            @block.scalar
            def _(a):
                def first_small(u, parity):
                    a.wait_ge(hot_ready, u + 1)
                    a.activation(hot_small[:, parity], hot[:, parity], ACT.Copy, scale=1.0 / LOW_SCALE).then_inc(small_ready, 1)

                def further_smalls(u):
                    first, end, offset = span_of(a, u)
                    with a.If(first + 1 < end), a.Fori(first + 1, end) as b:
                        a.wait_ge(further_hot, offset + b + 1)
                        a.sem_inc(go, 1)
                        a.activation(hot_small[:, 2], hot[:, 2], ACT.Copy, scale=1.0 / LOW_SCALE).then_inc(further_small, 1)

                def squares(i, kind):
                    a.wait_ge(projected[kind], i + 1)
                    a.activation(square[:, kind], ps_kv[kind][:], ACT.Square).then_inc(squared[kind], 1)

                def root(i, kind):
                    a.wait_ge(var_ready[kind], i + 1)
                    a.activation(rstd[:, kind], var[:, kind], ACT.Sqrt).then_inc(rooted[kind], 1)

                def beside(i, opening=False, last=False):
                    first_small(2 * i + 1, 1)
                    further_smalls(2 * i)
                    squares(i, 0)
                    if not opening:
                        root(i - 1, 1)
                    if not last:
                        first_small(2 * i + 2, 0)
                    further_smalls(2 * i + 1)
                    squares(i, 1)
                    root(i, 0)

                a.sem_inc(further_small, T + 1)
                first_small(0, 0)
                beside(0, opening=True)
                with a.Fori(1, T - 1) as i:
                    beside(i)
                beside(T - 1, last=True)
                root(T - 1, 1)

            @block.tensor
            def _(pe):
                def products(bank, buffer, half, ready, small, n, done):
                    for part, (hots, signal) in enumerate(((hot, ready), (hot_small, small))):
                        pe.wait_ge(signal, n + 1)
                        for k in range(SUPER):
                            mm = pe.matmul(bank[:], hots[:, buffer, k], rows[:, half * SUPER + k, part * D:(part + 1) * D],
                                           start=part == 0 and k == 0, stop=part == 1 and k == SUPER - 1)
                    mm.then_inc(done, 1)

                def first_visit(u, i, half):
                    for k in range(SUPER):
                        pe.wait_ge(gathered[half * SUPER + k], (i + 1) * 16)
                    if not isinstance(u, int) or u > 1:
                        pe.wait_ge(added, u - 1)
                    products(ps_sum[half], half, half, hot_ready, small_ready, u, summed)

                def further_visits(u, half):
                    first, end, offset = span_of(pe, u)
                    with pe.If(first + 1 < end), pe.Fori(first + 1, end) as b:
                        n = offset + b
                        pe.wait_ge(further_added, n)
                        products(ps_sum[2], 2, half, further_hot, further_small, n, further_summed)
                    pe.wait_ge(summed, u + 1)
                    pe.wait_ge(further_summed, offset + end)
                    pe.sem_inc(super_used, 1)

                def project(i, slot, kind, first):
                    if kind == 0:
                        pe.wait_ge(loaded_xt[slot], 8 * (i - slot) + 16)
                    if not first:
                        pe.wait_ge(emptied[kind], i)
                    for k in range(KD):
                        mm = pe.matmul(ps_kv[kind][:], xt[:, slot, k * P:(k + 1) * P], w[:, k, kind * D:(kind + 1) * D],
                                       start=k == 0, stop=k == KD - 1)
                    mm.then_inc(projected[kind], 1)

                def correlate(i, slot, n=P):
                    pe.wait_ge(normalized[0], 2 * i + 2)
                    pe.wait_ge(normalized[1], 2 * i + 2)
                    for pair in range(HEADS // 2):
                        cols = slice(pair * P, (pair + 1) * P)
                        mm = pe.matmul(ps_p[:, cols], kv[0:n, 1, slot, cols], kv[0:n, 0, slot, cols],
                                       start=False, stop=True, skip_group_check=True)
                    mm.then_inc(correlated, 1)

                def beside(i, slot, first):
                    for half in range(2):
                        first_visit(2 * i + half, i, half)
                        project(i, slot, half, first)
                        further_visits(2 * i + half, half)
                    if not first:
                        correlate(i - 1, 1 - slot)

                pe.sem_inc(further_summed, T + 1)
                pe.wait_ge(zeroed, 1)
                pe.wait_ge(w_ready, 1)
                pe.matmul(ps_p[:], zero[:], w[:, 0, 0:D], start=True, stop=True)
                beside(0, 0, True)
                with pe.Fori(0, T // 2) as pair:
                    beside(2 * pair + 1, 1, False)
                    beside(2 * pair + 2, 0, False)
                correlate(T - 1, 0, s.last)


def fold(nc, s, t, dram):
    with ExitStack() as ctx:
        sb, ps, sem = allocate(nc, ctx, "fold", t.lasting)
        wq = sb("wq", [P, KD, D])
        wo = sb("wo", [P, KD, D])
        pw = sb("pw", [P, KD, D])
        ps_pw = [ps(f"ps_pw{i}", [P, D]) for i in range(KD)]
        ps_m = [ps(f"ps_m{i}", [P, D]) for i in range(KD)]
        loaded = sem("loaded")
        pw_done = sem("pw_done")
        pw_ready = sem("pw_ready")
        m_done = sem("m_done")

        with nc.Block() as block:

            @block.sync
            def _(sp):
                sp.dma_start(wo[:], dram["w_out"].rearrange("(k p) n -> p k n", p=P)).then_inc(loaded, 16)
                sp.dma_start(wq[:], dram["w_q"].rearrange("(k p) n -> p k n", p=P)).then_inc(loaded, 16)

            @block.tensor
            def _(pe):
                pe.wait_ge(loaded, 32)
                for j in range(KD):
                    pe.matmul(ps_pw[j][:], t.p[:, j * P:(j + 1) * P], wo[:, j], start=True, stop=True).then_inc(pw_done, 1)
                for m in range(KD):
                    for j in range(KD):
                        if m == 0:
                            pe.wait_ge(pw_ready, j + 1)
                        mm = pe.matmul(ps_m[m][:], wq[:, j, m * P:(m + 1) * P], pw[:, j], start=j == 0, stop=j == KD - 1)
                    mm.then_inc(m_done, 1)

            @block.vector
            def _(v):
                for j in range(KD):
                    v.wait_ge(pw_done, j + 1)
                    v.tensor_copy(pw[:, j], ps_pw[j][:]).then_inc(pw_ready, 1)
                for m in range(KD):
                    v.wait_ge(m_done, m + 1)
                    v.tensor_copy(t.m[:, m], ps_m[m][:])


def mix(nc, s, t, dram):
    with ExitStack() as ctx:
        sb, ps, sem = allocate(nc, ctx, "mix", t.lasting)
        T = s.tiles
        wg = sb("w_gnn", [P, KD, D])
        b_gnn = sb("b_gnn", [P, D])
        b_out = sb("b_out", [P, D])
        x = sb("x", [P, 2, D])
        xt = sb("xt", [P, 2, D])
        y = sb("y", [P, 2, D])
        yt = sb("yt", [P, 2, D])
        part = sb("part", [P, D])
        stats = sb("stats", [P, 2, 6])
        mean = sb("mean", [P, 2])
        weight = sb("weight", [P, 2])
        stats2 = sb("stats2", [P, T, 6])
        var = sb("var", [P, T])
        half = sb("half", [P, T])
        ps_yt = [ps(f"ps_yt{i}", [P, D]) for i in range(2)]
        ps_g = [ps(f"ps_g{i}", [P, D]) for i in range(2)]
        ps_a = [ps(f"ps_a{i}", [P, D]) for i in range(2)]
        load_w = sem("load_w")
        load_x = [sem(f"load_x{i}") for i in range(2)]
        load_xt = [sem(f"load_xt{i}") for i in range(2)]
        x_biased = sem("x_biased")
        stat_steps = sem("stat_steps")
        y_ready = sem("y_ready")
        turned = sem("turned")
        yt_ready = sem("yt_ready")
        g_done = sem("g_done")
        a_done = sem("a_done")
        sums = sem("sums")
        tail = sem("tail")
        root_in = sem("root_in")
        root_out = sem("root_out")

        with nc.Block() as block:

            @block.sync
            def _(sp):
                sp.dma_start(wg[:], dram["w_gnn"].rearrange("(k p) n -> p k n", p=P)).then_inc(load_w, 16)
                sp.dma_start(b_gnn[:], dram["b_gnn"].partition_broadcast(P)).then_inc(load_w, 16)
                sp.dma_start(b_out[:], dram["b_out"].partition_broadcast(P)).then_inc(load_w, 16)
                xv = dram["x"].rearrange("(t p) d -> t p d", p=P)

                def load(i, slot, first):
                    if not first:
                        sp.wait_ge(a_done, i - 1)
                    sp.dma_start(xt[:, slot], dram["xt"][at(i)].squeeze(0)).then_inc(load_xt[slot], 16)
                    if not first:
                        sp.wait_ge(sums, 3 * i - 3)
                    sp.dma_start(x[:, slot], xv[at(i)].squeeze(0)).then_inc(load_x[slot], 16)

                by_pairs(sp, T, load)

            @block.gpsimd
            def _(pool):
                pool.wait_ge(load_w, 48)

                def add_bias(i, slot, first):
                    pool.wait_ge(load_x[slot], 8 * (i - slot) + 16)
                    pool.tensor_tensor(x[:, slot], x[:, slot], b_out[:], ALU.add).then_inc(x_biased, 1)

                by_pairs(pool, T, add_bias)

            @block.vector
            def _(v):
                v.wait_ge(load_w, 48)

                def centre(i, slot, first):
                    step = Chain(v, stat_steps, 4 * i)
                    acc = t.acc[:, at(i)].squeeze(1)
                    step.then(v.bn_stats(stats[:, slot], acc))
                    step.then(v.tensor_tensor(mean[:, slot:slot + 1], stats[:, slot, 1:2], stats[:, slot, 4:5], ALU.add))
                    step.then(v.tensor_scalar(mean[:, slot:slot + 1], mean[:, slot:slot + 1], 0.5, None, ALU.mult))
                    step.mark(v.tensor_scalar(weight[:, slot:slot + 1], mean[:, slot:slot + 1], t.dis_back[:, at(i)], None,
                                              ALU.mult))
                    if not first:
                        v.wait_ge(turned, i - 1)
                    v.tensor_scalar(y[:, slot], acc, mean[:, slot:slot + 1], t.dis_back[:, at(i)], ALU.subtract,
                                    ALU.mult).then_inc(y_ready, 1)

                def add(i, slot, first):
                    v.wait_ge(g_done, i + 1)
                    v.wait_ge(stat_steps, 4 * i + 4)
                    if not (first and slot == 0):
                        v.wait_ge(sums, 3 * i)
                    v.scalar_tensor_tensor(part[:], b_gnn[:], weight[:, slot:slot + 1], ps_g[slot][:], ALU.mult,
                                           ALU.add).then_inc(sums, 1)
                    v.wait_ge(sums, 3 * i + 1)
                    v.wait_ge(a_done, i + 1)
                    v.scalar_tensor_tensor(part[:], part[:], 0.0, ps_a[slot][:], ALU.max, ALU.add).then_inc(sums, 1)
                    v.wait_ge(sums, 3 * i + 2)
                    v.wait_ge(x_biased, i + 1)
                    v.wait_ge(y_ready, i + 1)
                    v.tensor_tensor(t.acc[:, at(i)].squeeze(1), part[:], x[:, slot], ALU.add).then_inc(sums, 1)
                    v.wait_ge(sums, 3 * i + 3)
                    v.bn_stats(stats2[:, at(i)].squeeze(1), t.acc[:, at(i)].squeeze(1)).then_inc(tail, 1)

                centre(0, 0, True)
                centre(1, 1, True)
                add(0, 0, True)
                centre(2, 0, False)
                add(1, 1, True)
                with v.Fori(1, T // 2) as pair:
                    i = 2 * pair
                    centre(i + 1, 1, False)
                    add(i, 0, False)
                    centre(i + 2, 0, False)
                    add(i + 1, 1, False)
                add(T - 1, 0, False)
                v.wait_ge(tail, T)
                step = Chain(v, tail, T)
                moments(v, step, stats2, t.mean, var, half)
                step.then(v.tensor_scalar(var[:], var[:], EPS, None, ALU.add))
                v.sem_inc(root_in, 1)
                v.wait_ge(root_out, 1)
                step.then(v.reciprocal(t.rstd[:], half[:]))
                refine_root(v, step, t.rstd[:], var[:], half[:])

            @block.scalar
            def _(a):
                def evacuate(i, slot, first):
                    a.wait_ge(turned, i + 1)
                    if not first:
                        a.wait_ge(g_done, i - 1)
                    a.copy(yt[:, slot], ps_yt[slot][:]).then_inc(yt_ready, 1)

                by_pairs(a, T, evacuate)
                a.wait_ge(root_in, 1)
                a.activation(half[:], var[:], ACT.Sqrt).then_inc(root_out, 1)

            @block.tensor
            def _(pe):
                pe.wait_ge(load_w, 48)

                def turn(i, slot, first):
                    pe.wait_ge(y_ready, i + 1)
                    if not first:
                        pe.wait_ge(yt_ready, i - 1)
                    for k in range(KD):
                        tr = pe.transpose(ps_yt[slot][:, k * P:(k + 1) * P], y[:, slot, k * P:(k + 1) * P], t.ident[:])
                    tr.then_inc(turned, 1)

                def attention(i, slot, first):
                    pe.wait_ge(load_xt[slot], 8 * (i - slot) + 16)
                    if not first:
                        pe.wait_ge(sums, 3 * i - 4)
                    for k in range(KD):
                        mm = pe.matmul(ps_a[slot][:], xt[:, slot, k * P:(k + 1) * P], t.m[:, k], start=k == 0, stop=k == KD - 1)
                    mm.then_inc(a_done, 1)

                def gnn(i, slot, first):
                    pe.wait_ge(yt_ready, i + 1)
                    if not first:
                        pe.wait_ge(sums, 3 * i - 5)
                    for k in range(KD):
                        mm = pe.matmul(ps_g[slot][:], yt[:, slot, k * P:(k + 1) * P], wg[:, k], start=k == 0, stop=k == KD - 1)
                    mm.then_inc(g_done, 1)

                def tile(i, slot, first, more=True):
                    attention(i, slot, first)
                    if more:
                        turn(i + 1, 1 - slot, first and slot == 0)
                    gnn(i, slot, first)

                turn(0, 0, True)
                tile(0, 0, True)
                tile(1, 1, True)
                with pe.Fori(1, T // 2) as pair:
                    tile(2 * pair, 0, False)
                    tile(2 * pair + 1, 1, False)
                tile(T - 1, 0, False, False)


def gate_in(nc, s, t, dram):
    with ExitStack() as ctx:
        sb, ps, sem = allocate(nc, ctx, "gate_in", t.lasting)
        T = s.tiles
        w = sb("w", [P, KD, GATE])
        b = sb("b", [P, GATE])
        tok = sb("tok", [P, 2, D])
        tt = sb("tt", [P, 2, D])
        ps_t = [ps(f"ps_t{i}", [P, D]) for i in range(2)]
        ps_gate = [ps(f"ps_gate{i}", [P, D]) for i in range(2)]
        load_w = sem("load_w")
        tok_ready = sem("tok_ready")
        turned = sem("turned")
        tt_ready = sem("tt_ready")
        gated = sem("gated")
        gate_read = sem("gate_read")
        tok_stored = [sem(f"tok_stored{i}") for i in range(2)]
        x1_stored = sem("x1_stored")

        with nc.Block() as block:

            @block.sync
            def _(sp):
                sp.dma_start(w[:], dram["w_gate1"].rearrange("(k p) n -> p k n", p=P)).then_inc(load_w, 16)
                sp.dma_start(b[:], dram["b_gate1"].partition_broadcast(P)).then_inc(load_w, 16)
                sp.dma_start(dram["x1"].rearrange("(t p) d -> p t d", p=P), t.acc[:]).then_inc(x1_stored, 16)
                rows = dram["tok"].rearrange("(t p) d -> t p d", p=P)

                def store(i, slot, first):
                    sp.wait_ge(tok_ready, i + 1)
                    sp.dma_start(rows[at(i)].squeeze(0), tok[:, slot]).then_inc(tok_stored[slot], 16)

                by_pairs(sp, T, store)
                sp.wait_ge(x1_stored, 16)
                for slot, n in ((0, T // 2 + 1), (1, T // 2)):
                    sp.wait_ge(tok_stored[slot], 16 * n)

            @block.vector
            def _(v):
                v.wait_ge(load_w, 32)

                def normalize(i, slot, first):
                    if not first:
                        v.wait_ge(turned, i - 1)
                        v.wait_ge(tok_stored[slot], 8 * (i - slot))
                    v.tensor_scalar(tok[:, slot], t.acc[:, at(i)].squeeze(1), t.mean[:, at(i)], t.rstd[:, at(i)],
                                    ALU.subtract, ALU.mult).then_inc(tok_ready, 1)

                def keep(i, slot, first):
                    v.wait_ge(gated, i + 1)
                    v.tensor_tensor(t.gate[:, at(i)].squeeze(1), ps_gate[slot][:, 0:GATE], b[:], ALU.add).then_inc(gate_read, 1)

                normalize(0, 0, True)
                normalize(1, 1, True)
                keep(0, 0, True)
                normalize(2, 0, False)
                keep(1, 1, True)
                with v.Fori(1, T // 2) as pair:
                    i = 2 * pair
                    normalize(i + 1, 1, False)
                    keep(i, 0, False)
                    normalize(i + 2, 0, False)
                    keep(i + 1, 1, False)
                keep(T - 1, 0, False)

            @block.scalar
            def _(a):
                def evacuate(i, slot, first):
                    a.wait_ge(turned, i + 1)
                    if not first:
                        a.wait_ge(gated, i - 1)
                    a.copy(tt[:, slot], ps_t[slot][:]).then_inc(tt_ready, 1)

                by_pairs(a, T, evacuate)

            @block.tensor
            def _(pe):
                pe.wait_ge(load_w, 32)

                def turn(i, slot, first):
                    pe.wait_ge(tok_ready, i + 1)
                    if not first:
                        pe.wait_ge(tt_ready, i - 1)
                    for k in range(KD):
                        tr = pe.transpose(ps_t[slot][:, k * P:(k + 1) * P], tok[:, slot, k * P:(k + 1) * P], t.ident[:])
                    tr.then_inc(turned, 1)

                def gate(i, slot, first):
                    pe.wait_ge(tt_ready, i + 1)
                    if not first:
                        pe.wait_ge(gate_read, i - 1)
                    for k in range(KD):
                        mm = pe.matmul(ps_gate[slot][:, 0:GATE], tt[:, slot, k * P:(k + 1) * P], w[:, k], start=k == 0,
                                       stop=k == KD - 1)
                    mm.then_inc(gated, 1)

                def tile(i, slot, first, more=True):
                    if more:
                        turn(i + 1, 1 - slot, first and slot == 0)
                    gate(i, slot, first)

                turn(0, 0, True)
                tile(0, 0, True)
                tile(1, 1, True)
                with pe.Fori(1, T // 2) as pair:
                    tile(2 * pair, 0, False)
                    tile(2 * pair + 1, 1, False)
                tile(T - 1, 0, False, False)


def route(nc, s, t, dram):
    with ExitStack() as ctx:
        sb, ps, sem = allocate(nc, ctx, "route", t.lasting)
        T, E, S = s.tiles, EXPERTS, s.slot_tiles
        w = sb("w", [P, E, GATE])
        b = sb("b", [P, E])
        ids = sb("ids", [P, T])
        upper = sb("upper", [P, P])
        ones = sb("ones", [P, P])
        products = sb("products", [P, T, E, GATE])
        logits = sb("logits", [P, T, E])
        order = sb("order", [P, E])
        top = sb("top", [P, 2, T])
        same = sb("same", [P, T, E])
        pick = sb("pick", [P, T])
        hot = sb("hot", [P, 2, T, E])
        mask = sb("mask", [P, T, E])
        down = sb("down", [P, T])
        rank = sb("rank", [P, T, E])
        total = sb("total", [P, T, E])
        run = [sb("run0", [P, T, E]), sb("run1", [P, T, E])]
        count = sb("count", [P, E])
        count_int = sb("count_int", [P, 2, E], I32)
        tiles_of = sb("tiles_of", [P, E])
        ends = [sb("ends0", [P, E]), sb("ends1", [P, E])]
        base = sb("base", [P, E])
        slot = sb("slot", [P, T, 2])
        slot_low = sb("slot_low", [P, T, 2], I32)
        slot_high = sb("slot_high", [P, T, 2], I32)
        low = sb("low", [P, T, 2])
        high = sb("high", [P, T, 2])
        reached = sb("reached", [1, S, E])
        expert = sb("expert", [1, S])
        hot_low = sb("hot_low", [P, 2, P])
        hot_high = sb("hot_high", [P, 2, S])
        ps_rank = ps("ps_rank", [P, 512])
        ps_total = ps("ps_total", [P, 512])
        ps_list = ps("ps_list", [P, 512])
        loaded = sem("loaded")
        gelu = sem("gelu")
        steps = sem("steps")
        one = sem("one")
        exp_in = sem("exp_in")
        exp_out = sem("exp_out")
        masked = sem("masked")
        ranked = sem("ranked")
        hots = sem("hots")
        listed = sem("listed")
        opened = sem("opened")

        with nc.Block() as block:

            @block.sync
            def _(sp):
                sp.dma_start(w[:], dram["w_gate2"].partition_broadcast(P)).then_inc(loaded, 16)
                sp.dma_start(b[:], dram["b_gate2"].partition_broadcast(P)).then_inc(loaded, 16)
                sp.dma_start(ids[:], dram["ids"]).then_inc(loaded, 16)
                sp.dma_start(upper[:], dram["upper"]).then_inc(loaded, 16)

            @block.gpsimd
            def _(pool):
                pool.memset(ones[:], 1.0).then_inc(one, 1)

            @block.scalar
            def _(a):
                a.activation(t.gate[:], t.gate[:], ACT.Gelu).then_inc(gelu, 1)
                a.wait_ge(exp_in, 1)
                a.activation(down[:], down[:], ACT.Exp).then_inc(exp_out, 1)

            @block.vector
            def _(v):
                step = Chain(v, steps)
                over_t = lambda a: a.unsqueeze(1).to_broadcast([P, T, E])
                over_e = lambda a: a.unsqueeze(2).to_broadcast([P, T, E])
                v.wait_ge(loaded, 64)
                step.mark(v.tensor_scalar(order[:], t.iota[:, 0:E], -1.0, float(E), ALU.mult, ALU.add))
                v.wait_ge(gelu, 1)
                step.then(v.tensor_tensor(products[:], t.gate[:].unsqueeze(2).to_broadcast([P, T, E, GATE]),
                                          w[:].unsqueeze(1).to_broadcast([P, T, E, GATE]), ALU.mult))
                step.then(v.tensor_reduce(logits[:], products[:], AX.X, ALU.add))
                step.then(v.tensor_tensor(logits[:], logits[:], over_t(b[:]), ALU.add))
                for n in range(2):
                    step.then(v.tensor_reduce(top[:, n], logits[:], AX.X, ALU.max))
                    step.then(v.tensor_tensor(same[:], logits[:], over_e(top[:, n]), ALU.is_equal))
                    step.then(v.tensor_tensor(same[:], same[:], over_t(order[:]), ALU.mult))
                    step.then(v.tensor_reduce(pick[:], same[:], AX.X, ALU.max))
                    step.then(v.tensor_tensor(hot[:, n], over_t(order[:]), over_e(pick[:]), ALU.is_equal))
                    if n == 0:
                        step.then(v.scalar_tensor_tensor(logits[:], hot[:, 0], -3.0e38, logits[:], ALU.mult, ALU.add))
                step.then(v.tensor_tensor(down[:], top[:, 1], top[:, 0], ALU.subtract))
                v.sem_inc(exp_in, 1)
                step.then(v.tensor_tensor(mask[:], hot[:, 0], hot[:, 1], ALU.add))
                v.sem_inc(masked, 1)
                v.wait_ge(exp_out, 1)
                step.then(v.tensor_scalar(pick[:], down[:], 1.0, None, ALU.add))
                step.then(v.reciprocal(t.weight[:, :, 0], pick[:]))
                step.mark(v.tensor_tensor(t.weight[:, :, 1], t.weight[:, :, 0], down[:], ALU.mult))
                v.wait_ge(ranked, 1)
                step.mark(v.tensor_copy(rank[:], ps_rank[:, 0:T * E]))
                step.mark(v.tensor_copy(total[:], ps_total[:, 0:T * E]))
                step.then(v.tensor_copy(run[0][:], ps_total[:, 0:T * E]))
                now, shift = 0, 1
                while shift < T:
                    old, new = run[now], run[1 - now]
                    step.mark(v.tensor_copy(new[:, 0:shift], old[:, 0:shift]))
                    step.then(v.tensor_tensor(new[:, shift:], old[:, shift:], old[:, 0:T - shift], ALU.add))
                    now, shift = 1 - now, 2 * shift
                step.mark(v.tensor_copy(count_int[:, 0], run[now][:, T - 1]))
                step.then(v.tensor_tensor(rank[:], rank[:], run[now][:], ALU.add))
                step.then(v.tensor_tensor(rank[:], rank[:], total[:], ALU.subtract))
                step.then(v.tensor_scalar(count[:], count_int[:, 0], float(P - 1), None, ALU.add))
                step.then(v.tensor_copy(count_int[:, 0], count[:]))
                step.then(v.tensor_single_scalar(count_int[:, 1], count_int[:, 0], 7, op=ALU.logical_shift_right))
                step.mark(v.tensor_copy(tiles_of[:], count_int[:, 1]))
                step.then(v.tensor_copy(ends[0][:], count_int[:, 1]))
                now, shift = 0, 1
                while shift < E:
                    old, new = ends[now], ends[1 - now]
                    step.mark(v.tensor_copy(new[:, 0:shift], old[:, 0:shift]))
                    step.then(v.tensor_tensor(new[:, shift:], old[:, shift:], old[:, 0:E - shift], ALU.add))
                    now, shift = 1 - now, 2 * shift
                end = ends[now]
                step.then(v.tensor_tensor(base[:], end[:], tiles_of[:], ALU.subtract))
                step.then(v.tensor_scalar(base[:], base[:], float(P), None, ALU.mult))
                step.then(v.tensor_tensor(rank[:], rank[:], over_t(base[:]), ALU.add))
                for n in range(2):
                    step.then(v.tensor_tensor(same[:], hot[:, n], rank[:], ALU.mult))
                    step.then(v.tensor_reduce(slot[:, :, n], same[:], AX.X, ALU.add))
                step.then(v.tensor_copy(t.slot[:], slot[:]))
                step.mark(v.tensor_single_scalar(slot_low[:], t.slot[:], P - 1, op=ALU.bitwise_and))
                step.then(v.tensor_single_scalar(slot_high[:], t.slot[:], 7, op=ALU.logical_shift_right))
                step.mark(v.tensor_copy(low[:], slot_low[:]))
                step.mark(v.tensor_copy(high[:], slot_high[:]))
                steps_row = [1, S, E]
                step.then(v.tensor_tensor(reached[:], t.iota[0:1, 0:S].unsqueeze(2).to_broadcast(steps_row),
                                          end[0:1].unsqueeze(1).to_broadcast(steps_row), ALU.is_ge))
                step.then(v.tensor_reduce(expert[:], reached[:], AX.X, ALU.add))
                step.then(v.tensor_scalar(expert[:], expert[:], float(E - 1), None, ALU.min))
                step.then(v.tensor_copy(t.expert[:], expert[:]))

                def spot(i, first):
                    for n in range(2):
                        if not first:
                            v.wait_ge(listed, 2 * i + n - 1)
                        v.tensor_scalar(hot_low[:, n], t.iota[:], low[:, at(i), n], None, ALU.is_equal).then_inc(hots, 1)
                        v.tensor_scalar(hot_high[:, n], t.iota[:, 0:S], high[:, at(i), n], ids[:, at(i)], ALU.is_equal,
                                        ALU.mult).then_inc(hots, 1)

                spot(0, True)
                with v.Fori(1, T) as i:
                    spot(i, False)
                v.wait_ge(listed, 2 * T)
                v.tensor_copy(t.token[:], ps_list[:, 0:S])

            @block.tensor
            def _(pe):
                pe.wait_ge(loaded, 64)
                pe.wait_ge(one, 1)
                pe.wait_ge(masked, 1)
                pe.matmul(ps_rank[:, 0:T * E], upper[:], mask[:].rearrange("p t e -> p (t e)"), start=True, stop=True)
                pe.matmul(ps_total[:, 0:T * E], ones[:], mask[:].rearrange("p t e -> p (t e)"), start=True,
                          stop=True).then_inc(ranked, 1)

                def place(i, opening):
                    for n in range(2):
                        pe.wait_ge(hots, 4 * i + 2 * n + 2)
                        pe.matmul(ps_list[:, 0:S], hot_low[:, n], hot_high[:, n], start=opening and n == 0, stop=True,
                                  skip_group_check=True).then_inc(listed, 1)

                place(0, True)
                with pe.Fori(1, T) as i:
                    place(i, False)


def experts(nc, s, t, dram):
    with ExitStack() as ctx:
        sb, ps, sem = allocate(nc, ctx, "experts", t.lasting)
        E, N = EXPERTS, s.slot_tiles
        KH = H2 // P
        w = [sb("w1", [P, KD, E, H2]), sb("w2", [P, KH, E, H2]), sb("w3", [P, KH, E, D])]
        b = [sb("b1", [P, E, H2]), sb("b2", [P, E, H2]), sb("b3", [P, E, D])]
        affine = sb("affine", [P, 2, 2, KH, E])
        index = sb("index", [P, 2, 1], I32)
        rows = sb("rows", [P, 2, D])
        xt = sb("xt", [P, 2, D])
        h = [sb("h1", [P, H2]), sb("h2", [P, H2])]
        stats = sb("stats", [P, 2, 6])
        moment = sb("moment", [P, 2, 2])
        var = sb("var", [P, 2])
        power = sb("power", [P, 1])
        rstd = sb("rstd", [P, 2])
        v_ = [sb("v1", [P, H2]), sb("v2", [P, H2])]
        a_ = [sb("a1", [P, H2]), sb("a2", [P, H2])]
        o = sb("o", [P, 2, D])
        ps_t = [ps(f"ps_t{i}", [P, D]) for i in range(2)]
        ps_h = [ps(f"ps_h{i}", [P, D]) for i in range(2)]
        ps_u = [ps(f"ps_u{i}", [P, D]) for i in range(2)]
        ps_o = [ps(f"ps_o{i}", [P, D]) for i in range(2)]
        load_w = sem("load_w")
        indexed = sem("indexed")
        powered = sem("powered")
        go = sem("go")
        gathered = [sem(f"gathered{i}") for i in range(2)]
        turned = sem("turned")
        xt_ready = sem("xt_ready")
        h_done = [sem("h1_done"), sem("h2_done")]
        ln = [sem("ln1"), sem("ln2")]
        rooted = [sem("rooted1"), sem("rooted2")]
        v_ready = [sem("v1_ready"), sem("v2_ready")]
        u_done = [sem("u1_done"), sem("u2_done")]
        a_ready = [sem("a1_ready"), sem("a2_ready")]
        o_done = sem("o_done")
        o_ready = sem("o_ready")
        stored = [sem(f"stored{i}") for i in range(2)]

        def need(engine, semaphore, value):
            if not isinstance(value, int) or value > 0:
                engine.wait_ge(semaphore, value)

        def pipeline(engine, body):
            has = lambda i: not isinstance(i, int) or 0 <= i < N
            for i in range(-1, 4):
                body(i, i % 2, has)
            with engine.Fori(2, (N - 4) // 2) as pair:
                body(2 * pair, 0, lambda i: True)
                body(2 * pair + 1, 1, lambda i: True)
            for i in range(N - 4, N + 3):
                body(i, i % 2, has)

        def expert_of(engine, i):
            return engine.value_load(t.expert[0:1, at(i)], min_val=0, max_val=E - 1)

        with nc.Block() as block:

            @block.sync
            def _(sp):
                for n in range(3):
                    sp.dma_start(w[n][:], dram[f"w{n + 1}"]).then_inc(load_w, 16)
                    sp.dma_start(b[n][:], dram[f"b{n + 1}"].partition_broadcast(P)).then_inc(load_w, 16)
                sp.dma_start(affine[:], dram["affine"]).then_inc(load_w, 16)
                slots = dram["slots"].rearrange("(t p) d -> t p d", p=P)

                def store(i, slot, has):
                    if has(i):
                        sp.wait_ge(o_ready, i + 1)
                        sp.dma_start(slots[at(i)].squeeze(0), o[:, slot]).then_inc(stored[slot], 16)

                pipeline(sp, store)
                for slot in range(2):
                    sp.wait_ge(stored[slot], 8 * N)

            @block.gpsimd
            def _(pool):
                pool.memset(power[:], -0.5).then_inc(powered, 1)
                pool.wait_ge(powered, 1)

                def gather(i, slot):
                    need(pool, turned, i - 1)
                    pool.sem_inc(go, 1)
                    pool.tensor_copy(index[:, slot], t.token[:, at(i)]).then_inc(indexed, 1)
                    pool.wait_ge(indexed, i + 1)
                    pool.sem_inc(go, 1)
                    pool.indirect_dma_start(rows[:, slot], None, dram["tok"],
                                            bass.IndirectOffsetOnAxis(ap=index[:, slot], axis=0)).then_inc(gathered[slot], 16)

                def root(i, layer):
                    pool.wait_ge(ln[layer], 4 * i + 4)
                    pool.tensor_tensor(rstd[:, layer:layer + 1], var[:, layer:layer + 1], power[:], ALU.pow)\
                        .then_inc(rooted[layer], 1)

                def body(i, slot, has):
                    if has(i + 3):
                        gather(i + 3, 1 - slot)
                    if has(i):
                        root(i, 0)
                    if has(i - 1):
                        root(i - 1, 1)

                gather(0, 0)
                gather(1, 1)
                pipeline(pool, body)

            @block.vector
            def _(v):
                v.wait_ge(load_w, 7 * 16)

                def add_bias(i, layer):
                    e = expert_of(v, i)
                    v.wait_ge(h_done[layer], i + 1)
                    need(v, v_ready[layer], i)
                    v.tensor_tensor(h[layer][:], ps_h[layer][:, 0:H2], b[layer][:, at(e)].squeeze(1),
                                    ALU.add).then_inc(ln[layer], 1)

                def statistics(i, layer):
                    v.wait_ge(ln[layer], 4 * i + 1)
                    v.bn_stats(stats[:, layer], h[layer][:]).then_inc(ln[layer], 1)

                def moments_of(i, layer):
                    v.wait_ge(ln[layer], 4 * i + 2)
                    v.sem_inc(go, 1)
                    v.bn_aggr(moment[:, layer], stats[:, layer]).then_inc(ln[layer], 1)

                def guarded_variance(i, layer):
                    v.wait_ge(ln[layer], 4 * i + 3)
                    v.tensor_scalar(var[:, layer:layer + 1], moment[:, layer, 1:2], EPS, None, ALU.add).then_inc(ln[layer], 1)

                def normalize(i, layer):
                    v.wait_ge(rooted[layer], i + 1)
                    need(v, u_done[layer], i)
                    v.tensor_scalar(v_[layer][:], h[layer][:], moment[:, layer, 0:1], rstd[:, layer:layer + 1], ALU.subtract,
                                    ALU.mult).then_inc(v_ready[layer], 1)

                def finish(i, slot):
                    e = expert_of(v, i)
                    v.wait_ge(o_done, i + 1)
                    need(v, stored[slot], 8 * (i - slot))
                    v.tensor_tensor(o[:, slot], ps_o[slot][:], b[2][:, at(e)].squeeze(1), ALU.add).then_inc(o_ready, 1)

                def body(i, slot, has):
                    for layer in range(2):
                        if has(i - layer):
                            for part in (add_bias, statistics, moments_of, guarded_variance):
                                part(i - layer, layer)
                        if layer == 0 and has(i - 3):
                            finish(i - 3, 1 - slot)
                        if has(i - layer):
                            normalize(i - layer, layer)

                pipeline(v, body)

            @block.scalar
            def _(a):
                a.wait_ge(load_w, 7 * 16)

                def evacuate(i, slot):
                    a.wait_ge(turned, i + 1)
                    need(a, h_done[0], i - 1)
                    a.copy(xt[:, slot], ps_t[slot][:]).then_inc(xt_ready, 1)

                def gelu(i, layer):
                    e = expert_of(a, i)
                    a.wait_ge(u_done[layer], i + 1)
                    need(a, (h_done[1], o_done)[layer], i)
                    for k in range(KH):
                        cols = slice(k * P, (k + 1) * P)
                        a.activation(a_[layer][:, cols], ps_u[layer][:, cols], ACT.Gelu,
                                     bias=affine[:, layer, 1, k, at(e)], scale=affine[:, layer, 0, k, at(e)])\
                            .then_inc(a_ready[layer], 1)

                def body(i, slot, has):
                    if has(i - 1):
                        gelu(i - 1, 0)
                    if has(i - 2):
                        gelu(i - 2, 1)
                    if has(i + 1):
                        evacuate(i + 1, 1 - slot)

                pipeline(a, body)

            @block.tensor
            def _(pe):
                pe.wait_ge(load_w, 7 * 16)

                def turn_rows(i, slot):
                    pe.wait_ge(gathered[slot], 8 * (i - slot) + 16)
                    need(pe, xt_ready, i - 1)
                    for k in range(KD):
                        tr = pe.transpose(ps_t[slot][:, k * P:(k + 1) * P], rows[:, slot, k * P:(k + 1) * P], t.ident[:])
                    tr.then_inc(turned, 1)

                def turn(i, layer):
                    pe.wait_ge(v_ready[layer], i + 1)
                    need(pe, a_ready[layer], 2 * i)
                    for k in range(KH):
                        cols = slice(k * P, (k + 1) * P)
                        tr = pe.transpose(ps_u[layer][:, cols], v_[layer][:, cols], t.ident[:])
                    tr.then_inc(u_done[layer], 1)

                def layer1(i, slot):
                    e = expert_of(pe, i)
                    pe.wait_ge(xt_ready, i + 1)
                    need(pe, ln[0], 4 * i - 3)
                    for k in range(KD):
                        mm = pe.matmul(ps_h[0][:, 0:H2], xt[:, slot, k * P:(k + 1) * P], w[0][:, k, at(e)].squeeze(1),
                                       start=k == 0, stop=k == KD - 1)
                    mm.then_inc(h_done[0], 1)

                def layer2(i):
                    e = expert_of(pe, i)
                    pe.wait_ge(a_ready[0], 2 * i + 2)
                    need(pe, ln[1], 4 * i - 3)
                    for k in range(KH):
                        mm = pe.matmul(ps_h[1][:, 0:H2], a_[0][:, k * P:(k + 1) * P], w[1][:, k, at(e)].squeeze(1),
                                       start=k == 0, stop=k == KH - 1)
                    mm.then_inc(h_done[1], 1)

                def layer3(i, slot):
                    e = expert_of(pe, i)
                    pe.wait_ge(a_ready[1], 2 * i + 2)
                    need(pe, o_ready, i - 1)
                    for k in range(KH):
                        mm = pe.matmul(ps_o[slot][:], a_[1][:, k * P:(k + 1) * P], w[2][:, k, at(e)].squeeze(1),
                                       start=k == 0, stop=k == KH - 1)
                    mm.then_inc(o_done, 1)

                def body(i, slot, has):
                    if has(i):
                        layer1(i, slot)
                    if has(i - 1):
                        turn(i - 1, 0)
                    if has(i - 2):
                        turn(i - 2, 1)
                    if has(i + 1):
                        turn_rows(i + 1, 1 - slot)
                    if has(i - 1):
                        layer2(i - 1)
                    if has(i - 2):
                        layer3(i - 2, slot)

                pipeline(pe, body)


def combine(nc, s, t, dram):
    with ExitStack() as ctx:
        sb, ps, sem = allocate(nc, ctx, "combine", t.lasting)
        T = s.tiles
        index = sb("index", [P, 2, 2], I32)
        rows = sb("rows", [P, 2, 2, D])
        x1 = sb("x1", [P, 2, D])
        partial = sb("partial", [P, 2, D])
        out = sb("out", [P, 2, D])
        go = sem("go")
        indexed = sem("indexed")
        gathered = [[sem(f"gathered{i}{n}") for n in range(2)] for i in range(2)]
        load_x1 = [sem(f"load_x1{i}") for i in range(2)]
        half = sem("half")
        done = sem("done")
        stored = [sem(f"stored{i}") for i in range(2)]

        with nc.Block() as block:

            @block.gpsimd
            def _(pool):
                def gather(i, slot, first):
                    if not first:
                        pool.wait_ge(done, i - 1)
                        pool.sem_inc(go, 1)
                    pool.tensor_copy(index[:, slot], t.slot[:, at(i)].squeeze(1)).then_inc(indexed, 1)
                    pool.wait_ge(indexed, i + 1)
                    pool.sem_inc(go, 1)
                    for n in range(2):
                        pool.indirect_dma_start(rows[:, slot, n], None, dram["slots"],
                                                bass.IndirectOffsetOnAxis(ap=index[:, slot, n:n + 1], axis=0))\
                            .then_inc(gathered[slot][n], 16)

                by_pairs(pool, T, gather)

            @block.sync
            def _(sp):
                xv = dram["x1"].rearrange("(t p) d -> t p d", p=P)

                def load(i, slot, first):
                    if not first:
                        sp.wait_ge(half, i - 1)
                    sp.dma_start(x1[:, slot], xv[at(i)].squeeze(0)).then_inc(load_x1[slot], 16)

                by_pairs(sp, T, load)

            @block.vector
            def _(v):
                def add(i, slot, first):
                    v.wait_ge(load_x1[slot], 8 * (i - slot) + 16)
                    v.wait_ge(gathered[slot][0], 8 * (i - slot) + 16)
                    if not first:
                        v.wait_ge(done, i - 1)
                    v.scalar_tensor_tensor(partial[:, slot], rows[:, slot, 0], t.weight[:, at(i), 0], x1[:, slot], ALU.mult,
                                           ALU.add).then_inc(half, 1)
                    v.wait_ge(half, i + 1)
                    v.wait_ge(gathered[slot][1], 8 * (i - slot) + 16)
                    if not first:
                        v.wait_ge(stored[slot], 8 * (i - slot))
                    v.scalar_tensor_tensor(out[:, slot], rows[:, slot, 1], t.weight[:, at(i), 1], partial[:, slot], ALU.mult,
                                           ALU.add).then_inc(done, 1)

                by_pairs(v, T, add)

            @block.scalar
            def _(a):
                ov = dram["out"].rearrange("(t p) d -> t p d", p=P)

                def store(i, slot, first):
                    a.wait_ge(done, i + 1)
                    a.dma_start(ov[at(i)].squeeze(0), out[:, slot]).then_inc(stored[slot], 16)

                by_pairs(a, T, store)
                for slot, n in ((0, T // 2 + 1), (1, T // 2)):
                    a.wait_ge(stored[slot], 16 * n)


def build(nc, dram, sizes):
    s = shapes(*sizes)
    t = lambda: None
    with ExitStack() as ctx:
        t.lasting = ctx
        sb, ps, sem = allocate(nc, ctx, "all")
        t.ident = sb("ident", [P, P])
        t.iota = sb("iota", [P, P], F16)
        t.neg_block = sb("neg_block", [P, s.tiles])
        t.visits = sb("visits", [1, 3 * s.supers], I32)
        t.mean = sb("mean", [P, s.tiles])
        t.rstd = sb("rstd", [P, s.tiles])
        t.dis = sb("dis", [P, s.tiles])
        t.dis_table = sb("dis_table", [P, s.tiles])
        t.dis_back = sb("dis_back", [P, s.tiles])
        t.p = sb("p", [P, D])
        t.m = sb("m", [P, KD, D])
        t.gate = sb("gate", [P, s.tiles, GATE])
        t.weight = sb("weight", [P, s.tiles, 2])
        t.slot = sb("slot", [P, s.tiles, 2], I32)
        t.token = sb("token", [P, s.slot_tiles], I32)
        t.expert = sb("expert", [1, s.slot_tiles], I32)
        t.dis_col = lambda i, k: t.dis_table[:, at(i)]
        with ExitStack() as gathering:
            sb, ps, sem = allocate(nc, gathering, "graph", ctx)
            t.acc = sb("acc", [P, s.tiles, D])
            t.src = sb("src", [P, s.chunks], I32)
            t.dst = sb("dst", [P, s.chunks])
            prepare_edges(nc, s, t, dram)
            prepare_table(nc, s, t, dram)
            aggregate(nc, s, t, dram)
            fold(nc, s, t, dram)
            mix(nc, s, t, dram)
            gate_in(nc, s, t, dram)
        route(nc, s, t, dram)
        experts(nc, s, t, dram)
        combine(nc, s, t, dram)


def kernel(**inputs):
    import concourse.bacc as bacc
    from concourse.bass_utils import run_bass_kernel_spmd as run

    x, src, dst = (np.asarray(inputs[n]) for n in ("x", "src", "dst"))
    sizes = (x.shape[0], src.shape[0])
    s = shapes(*sizes)
    rows = s.tiles * P

    def edges(a):
        padded = np.concatenate([a, np.full(s.chunks * P - a.shape[0], rows - 1, a.dtype)])
        return np.ascontiguousarray(padded.reshape(s.chunks, P).T)

    def by_partition(a):
        experts, rows_in, columns = a.shape
        return np.ascontiguousarray(a.reshape(experts, rows_in // P, P, columns).transpose(2, 1, 0, 3))

    qkv = np.asarray(inputs["L0_mix_W_qkv"])
    cast = np.arange(P, dtype=np.float16)
    arrays = {
        "x": np.concatenate([x, np.zeros((rows - x.shape[0], D), x.dtype)]),
        "src": edges(src),
        "dst": edges(dst),
        "ident": np.eye(P, dtype=np.float32),
        "upper": np.triu(np.ones((P, P), np.float32), 1),
        "iota": np.tile(cast, (P, 1)),
        "w_q": np.ascontiguousarray(qkv[:D]),
        "w_out": np.ascontiguousarray(np.asarray(inputs["L0_mix_W_out"]).T),
        "b_out": np.asarray(inputs["L0_mix_b_out"]),
        "w_gnn": np.ascontiguousarray(np.asarray(inputs["L0_gnn_W"]).T),
        "b_gnn": np.asarray(inputs["L0_gnn_b"]),
        "w_gate1": np.asarray(inputs["L0_ffn_Wg1"]),
        "b_gate1": np.asarray(inputs["L0_ffn_bg1"]),
        "w_gate2": np.ascontiguousarray(np.asarray(inputs["L0_ffn_Wg2"]).T),
        "b_gate2": np.asarray(inputs["L0_ffn_bg2"]),
        "ids": np.ascontiguousarray(np.arange(rows, dtype=np.float32).reshape(s.tiles, P).T),
        **{f"w{n}": by_partition(np.asarray(inputs[f"L0_ffn_W{n}"])) for n in (1, 2, 3)},
        **{f"b{n}": np.asarray(inputs[f"L0_ffn_b{n}"]) for n in (1, 2, 3)},
        "affine": np.ascontiguousarray(np.stack([
            np.stack([np.asarray(inputs[f"L0_ffn_{kind}{n}"]).T.reshape(H2 // P, P, EXPERTS) for kind in ("g", "be")])
            for n in (1, 2)]).transpose(3, 0, 1, 2, 4)),
        "w_kv": np.ascontiguousarray(qkv[D:].T),
        "gamma_k": np.asarray(inputs["L0_mix_gamma_K"]).reshape(D),
        "beta_k": np.asarray(inputs["L0_mix_beta_K"]).reshape(D),
        "gamma_v": np.asarray(inputs["L0_mix_gamma_V"]).reshape(D),
        "beta_v": np.asarray(inputs["L0_mix_beta_V"]).reshape(D),
        "neg_block": np.tile(-P * np.arange(s.tiles, dtype=np.float32), (P, 1)),
    }
    nc = bacc.Bacc("TRN2", target_bir_lowering=False, num_devices=1)
    dram = {n: nc.dram_tensor(f"in_{n}", a.shape, mybir.dt.from_np(a.dtype), kind="ExternalInput").ap()
            for n, a in arrays.items()}
    dram["xt"] = nc.dram_tensor("xt_scratch", [s.tiles, P, D], F32, kind="Internal").ap()
    dram["table"] = nc.dram_tensor("table_scratch", [rows, 2 * D], F16, kind="Internal").ap()
    dram["x1"] = nc.dram_tensor("x1_scratch", [rows, D], F32, kind="Internal").ap()
    dram["tok"] = nc.dram_tensor("tok_scratch", [rows, D], F32, kind="Internal").ap()
    dram["slots"] = nc.dram_tensor("slots_scratch", [s.slot_tiles * P, D], F32, kind="Internal").ap()
    dram["out"] = nc.dram_tensor("out_rows", [rows, D], F32, kind="ExternalOutput").ap()
    build(nc, dram, sizes)
    r = run(nc, [{f"in_{n}": a for n, a in arrays.items()}], core_ids=[0])
    return r.results[0]["out_rows"][0:x.shape[0]]
```

```python
from contextlib import ExitStack

import concourse.bass as bass
import numpy as np
from concourse import mybir

P = 128
D = 512
KD = D // P
HEADS = 8
DH = 64
H2 = 256
EXPERTS = 8
GATE = 16
EPS = 1e-5

F32 = mybir.dt.float32
F16 = mybir.dt.float16
I32 = mybir.dt.int32
ALU = mybir.AluOpType
ACT = mybir.ActivationFunctionType
AX = mybir.AxisListType

SUPER = 8
TABLE_SCALE = 2.0 ** 10
LOW_SCALE = 2.0 ** 11


class Chain:

    def __init__(self, engine, sem, start=0):
        self.engine, self.sem, self.start, self.n = engine, sem, start, 0

    def mark(self, ins):
        ins.then_inc(self.sem, 1)
        self.n += 1

    def wait(self):
        self.engine.wait_ge(self.sem, self.start + self.n)

    def then(self, ins):
        self.mark(ins)
        self.wait()


def shapes(n_nodes, n_edges):
    s = lambda: None
    s.nodes = n_nodes
    s.tiles = -(-n_nodes // P)
    s.last = n_nodes - (s.tiles - 1) * P
    s.per_tile = -(-n_edges // P // s.tiles)
    s.chunks = s.per_tile * s.tiles
    s.supers = s.chunks // SUPER
    s.slot_tiles = (2 * s.tiles * P) // P + EXPERTS
    s.group = 7
    assert s.tiles % s.group == 0 and s.chunks % SUPER == 0 and s.supers == 2 * s.tiles
    assert s.tiles < 64 and s.supers <= P
    return s


def allocate(nc, ctx, stage, lasting=None):
    sb = lambda name, shape, dt=F32: ctx.enter_context(nc.sbuf_tensor(f"{stage}_{name}", shape, dt))
    ps = lambda name, shape, dt=F32: ctx.enter_context(nc.psum_tensor(f"{stage}_{name}", shape, dt))
    sem = lambda name: (lasting or ctx).enter_context(nc.semaphore(f"{stage}_{name}"))
    return sb, ps, sem


def at(i, n=1):
    return bass.ds(i, n)


def need(engine, semaphore, value):
    if not isinstance(value, int) or value > 0:
        engine.wait_ge(semaphore, value)


def by_pairs(engine, tiles, body):
    body(0, 0, True)
    body(1, 1, True)
    with engine.Fori(1, tiles // 2) as pair:
        body(2 * pair, 0, False)
        body(2 * pair + 1, 1, False)
    body(tiles - 1, 0, False)


def moments(v, step, stats, mean, var, half):
    step.mark(v.tensor_tensor(mean[:], stats[:, :, 1], stats[:, :, 4], ALU.add))
    step.mark(v.tensor_tensor(half[:], stats[:, :, 1], stats[:, :, 4], ALU.subtract))
    step.then(v.tensor_tensor(var[:], stats[:, :, 2], stats[:, :, 5], ALU.add))
    step.mark(v.tensor_scalar(mean[:], mean[:], 0.5, None, ALU.mult))
    step.mark(v.scalar_tensor_tensor(half[:], half[:], 0.25, half[:], ALU.mult, ALU.mult))
    step.then(v.tensor_scalar(var[:], var[:], 1.0 / D, None, ALU.mult))
    step.then(v.tensor_tensor(var[:], var[:], half[:], ALU.add))


def refine_root(v, step, r, a, spare):
    step.then(v.tensor_tensor(spare, r, r, ALU.mult))
    step.then(v.tensor_tensor(spare, spare, a, ALU.mult))
    step.then(v.tensor_scalar(spare, spare, -0.5, 1.5, ALU.mult, ALU.add))
    step.then(v.tensor_tensor(r, r, spare, ALU.mult))


def prepare_edges(nc, s, t, dram):
    with ExitStack() as ctx:
        sb, ps, sem = allocate(nc, ctx, "prepare_edges", t.lasting)
        T, C, U = s.tiles, s.chunks, s.supers
        low = sb("src_low_int", [P, C], I32)
        high = sb("src_high_int", [P, C], I32)
        dst_int = sb("dst_int", [P, C], I32)
        low_f = sb("src_low", [P, C])
        high_f = sb("src_high", [P, C])
        hot_low = sb("hot_low", [P, 2, s.per_tile, P], F16)
        hot_high = sb("hot_high", [P, 2, s.per_tile, T], F16)
        gap = sb("gap", [P, 2, s.per_tile, T], F16)
        gap2 = sb("gap2", [P, s.per_tile, T], F16)
        stats = sb("stats", [P, T, 6])
        var = sb("var", [P, T])
        half = sb("half", [P, T])
        ends = sb("ends", [U, 2])
        ends_int = sb("ends_int", [U, 2], I32)
        ends_block = sb("ends_block", [U, 2], I32)
        span = sb("span", [U, 4])
        parts = sb("parts", [1, 3, U], I32)
        deg = sb("deg", [P, T])
        root = sb("root", [P, T])
        sd = sb("sd", [P, T])
        upper = sb("upper", [P, P])
        zero = sb("zero", [P, P], F16)
        ps_dst = ps("ps_dst", [P, SUPER * P])
        ps_deg = ps("ps_deg", [P, 512])
        ps_rows = ps("ps_rows", [P, 512])

        load_small = sem("load_small")
        load_x = sem("load_x")
        split = sem("split")
        low_ready = sem("low_ready")
        gap_ready = sem("gap_ready")
        gap_squared = sem("gap_squared")
        high_ready = sem("high_ready")
        hot_used = sem("hot_used")
        dst_turned = sem("dst_turned")
        dve = sem("dve_steps")
        bn = sem("bn_steps")
        rows_in = sem("rows_in")
        rows_out = sem("rows_out")
        zeroed = sem("zeroed")
        deg_done = sem("deg_done")
        roots_in = sem("roots_in")
        roots_out = sem("roots_out")

        with nc.Block() as block:

            @block.sync
            def _(sp):
                sp.dma_start(t.src[:], dram["src"]).then_inc(load_small, 16)
                sp.dma_start(dst_int[:], dram["dst"]).then_inc(load_small, 16)
                sp.dma_start(t.ident[:], dram["ident"]).then_inc(load_small, 16)
                sp.dma_start(upper[:], dram["upper"]).then_inc(load_small, 16)
                sp.dma_start(t.iota[:], dram["iota"]).then_inc(load_small, 16)
                sp.dma_start(t.neg_block[:], dram["neg_block"]).then_inc(load_small, 16)
                xv = dram["x"].rearrange("(t p) d -> p t d", p=P)
                def load(g):
                    sp.dma_start(t.acc[:, at(g * s.group, s.group), :],
                                 xv[:, at(g * s.group, s.group), :]).then_inc(load_x, 16)

                load(0)
                with sp.Fori(1, T // s.group) as g:
                    sp.wait_ge(load_x, g * 16)
                    load(g)

            @block.gpsimd
            def _(pool):
                pool.memset(zero[:], 0.0).then_inc(zeroed, 1)
                pool.wait_ge(load_small, 96)
                pool.wait_ge(split, 4)
                shape = [P, s.per_tile, T]
                blocks = t.iota[:, 0:T].unsqueeze(1).to_broadcast(shape)

                def gaps(i, slot, first):
                    if not first:
                        pool.wait_ge(gap_squared, i - 1)
                    pool.tensor_tensor(gap[:, slot], high_f[:, at(i * s.per_tile, s.per_tile)].unsqueeze(2).to_broadcast(shape),
                                       blocks, ALU.subtract).then_inc(gap_ready, 1)

                gaps(0, 0, True)
                gaps(1, 1, True)
                with pool.Fori(1, T // 2) as pair:
                    i = 2 * pair
                    gaps(i, 0, False)
                    gaps(i + 1, 1, False)
                gaps(T - 1, 0, False)

            @block.vector
            def _(v):
                v.wait_ge(load_small, 96)
                v.tensor_copy(t.dst[:], dst_int[:]).then_inc(split, 1)
                v.tensor_single_scalar(high[:], t.src[:], 7, op=ALU.logical_shift_right).then_inc(split, 1)
                v.tensor_single_scalar(low[:], t.src[:], P - 1, op=ALU.bitwise_and).then_inc(split, 1)
                v.wait_ge(split, 3)
                v.tensor_copy(high_f[:], high[:]).then_inc(split, 1)
                v.tensor_copy(low_f[:], low[:]).then_inc(split, 1)
                v.wait_ge(split, 5)

                step = Chain(v, dve)
                v.wait_ge(dst_turned, 1)
                step.mark(v.tensor_reduce(ends[:, 0:1], ps_dst[0:U, :], AX.X, ALU.max))
                step.then(v.tensor_reduce(ends[:, 1:2], ps_dst[0:U, :], AX.X, ALU.min))
                step.then(v.tensor_copy(ends_int[:], ends[:]))
                step.then(v.tensor_single_scalar(ends_block[:], ends_int[:], 7, op=ALU.logical_shift_right))
                step.then(v.tensor_copy(span[:, 0:2], ends_block[:]))
                step.mark(v.tensor_scalar(span[:, 3:4], span[:, 1:2], -1.0, float(T), ALU.mult, ALU.add))
                v.tensor_tensor(span[:, 2:3], span[:, 0:1], span[:, 1:2], ALU.subtract).then_inc(rows_in, 1)
                v.wait_ge(rows_out, 1)
                step.wait()
                step.then(v.tensor_copy(parts[:].rearrange("p n u -> p (n u)"), ps_rows[0:1, 0:3 * U]))
                step.mark(v.tensor_single_scalar(parts[:, 1], parts[:, 1], 6, op=ALU.logical_shift_left))
                step.then(v.tensor_single_scalar(parts[:, 2], parts[:, 2], 12, op=ALU.logical_shift_left))
                step.then(v.tensor_tensor(parts[:, 1], parts[:, 1], parts[:, 2], ALU.bitwise_or))
                v.tensor_tensor(t.visits[:], parts[:, 0], parts[:, 1], ALU.bitwise_or)

                def low_hots(i, slot, first):
                    if not first:
                        v.wait_ge(hot_used, i - 1)
                    for c in range(s.per_tile):
                        hot = v.tensor_scalar(hot_low[:, slot, c, :], t.iota[:], low_f[:, at(i * s.per_tile + c)],
                                              None, ALU.is_equal)
                    hot.then_inc(low_ready, 1)

                low_hots(0, 0, True)
                low_hots(1, 1, True)
                with v.Fori(1, T // 2) as pair:
                    i = 2 * pair
                    low_hots(i, 0, False)
                    low_hots(i + 1, 1, False)
                low_hots(T - 1, 0, False)

                with v.Fori(0, T // s.group) as g:
                    v.wait_ge(load_x, g * 16 + 16)
                    for j in range(s.group):
                        v.bn_stats(stats[:, at(g * s.group + j)].squeeze(1),
                                   t.acc[:, at(g * s.group + j)].squeeze(1)).then_inc(bn, 1)
                v.wait_ge(bn, T)
                step = Chain(v, dve, step.n)
                moments(v, step, stats, t.mean, var, half)
                step.then(v.tensor_scalar(var[:], var[:], EPS, None, ALU.add))
                v.wait_ge(deg_done, 1)
                step.then(v.tensor_scalar(deg[:], ps_deg[:, 0:T], 1.0, None, ALU.add))
                v.sem_inc(roots_in, 1)
                v.wait_ge(roots_out, 2)
                step.mark(v.reciprocal(t.rstd[:], sd[:]))
                step.then(v.reciprocal(t.dis[:], root[:]))
                refine_root(v, step, t.rstd[:], var[:], sd[:])
                refine_root(v, step, t.dis[:], deg[:], root[:])
                v.tensor_scalar(t.dis_table[:], t.dis[:], TABLE_SCALE, None, ALU.mult)
                v.tensor_scalar(t.dis_back[:], t.dis[:], 1.0 / TABLE_SCALE, None, ALU.mult)

            @block.scalar
            def _(a):
                def high_hots(i, slot, first):
                    a.wait_ge(gap_ready, i + 1)
                    if not (first and slot == 0):
                        a.wait_ge(high_ready, i)
                    a.activation(gap2[:], gap[:, slot], ACT.Square).then_inc(gap_squared, 1)
                    a.wait_ge(gap_squared, i + 1)
                    if not first:
                        a.wait_ge(hot_used, i - 1)
                    a.activation(hot_high[:, slot], gap2[:], ACT.Relu, bias=1.0, scale=-1.0).then_inc(high_ready, 1)

                high_hots(0, 0, True)
                high_hots(1, 1, True)
                with a.Fori(1, T // 2) as pair:
                    i = 2 * pair
                    high_hots(i, 0, False)
                    high_hots(i + 1, 1, False)
                high_hots(T - 1, 0, False)
                a.wait_ge(roots_in, 1)
                a.activation(root[:], deg[:], ACT.Sqrt).then_inc(roots_out, 1)
                a.activation(sd[:], var[:], ACT.Sqrt).then_inc(roots_out, 1)

            @block.tensor
            def _(pe):
                pe.wait_ge(load_small, 96)
                pe.wait_ge(split, 1)
                for k in range(SUPER):
                    turn = pe.transpose(ps_dst[0:U, k * P:(k + 1) * P], t.dst[:, k::SUPER], t.ident[:])
                turn.then_inc(dst_turned, 1)
                pe.wait_ge(rows_in, 1)
                for n, column, square, start, stop in ((0, 1, t.ident, True, True), (1, 2, t.ident, True, True),
                                                       (2, 3, t.ident, True, False), (2, 2, upper, False, True)):
                    mm = pe.matmul(ps_rows[0:1, n * U:(n + 1) * U], span[:, column:column + 1], square[0:U, 0:U],
                                   start=start, stop=stop)
                mm.then_inc(rows_out, 1)
                pe.wait_ge(zeroed, 1)
                pe.matmul(ps_deg[:, 0:T], zero[:], t.iota[:, 0:T], start=True, stop=True)

                def count(i, slot):
                    pe.wait_ge(high_ready, i + 1)
                    pe.wait_ge(low_ready, i + 1)
                    for c in range(s.per_tile):
                        mm = pe.matmul(ps_deg[:, 0:T], hot_low[:, slot, c, :], hot_high[:, slot, c, :],
                                       start=False, stop=True, skip_group_check=True)
                    mm.then_inc(hot_used, 1)

                with pe.Fori(0, T // 2) as pair:
                    i = 2 * pair
                    count(i, 0)
                    count(i + 1, 1)
                count(T - 1, 0)
                pe.wait_ge(hot_used, T)
                pe.sem_inc(deg_done, 1)


def prepare_table(nc, s, t, dram):
    with ExitStack() as ctx:
        sb, ps, sem = allocate(nc, ctx, "prepare_table", t.lasting)
        T = s.tiles
        xn = sb("xn", [P, 2, D])
        xt = sb("xt", [P, 2, D])
        rest = sb("rest", [P, 2, D])
        halves = sb("halves", [P, 2, 2 * D], F16)
        ps_xt = [ps(f"ps_xt{i}", [P, D]) for i in range(2)]
        xn_ready = sem("xn_ready")
        turned = sem("turned")
        xt_ready = sem("xt_ready")
        scaled = sem("scaled")
        high_ready = sem("high_ready")
        rest_ready = sem("rest_ready")
        low_ready = sem("low_ready")
        xt_stored = [sem(f"xt_stored{i}") for i in range(2)]
        table_stored = [sem(f"table_stored{i}") for i in range(2)]
        table = dram["table"].rearrange("(t p) d -> t p d", p=P)

        def stores_before(i, slot):
            return 8 * (i - slot)

        with nc.Block() as block:

            @block.vector
            def _(v):
                def normalize(i, slot, first):
                    if not first:
                        v.wait_ge(turned, i - 1)
                        v.wait_ge(scaled, i - 1)
                    v.tensor_scalar(xn[:, slot], t.acc[:, at(i), :].squeeze(1), t.mean[:, at(i)], t.rstd[:, at(i)],
                                    ALU.subtract, ALU.mult).then_inc(xn_ready, 1)

                def halve(i, slot, first):
                    v.wait_ge(scaled, i + 1)
                    if not first:
                        v.wait_ge(table_stored[slot], stores_before(i, slot))
                    v.tensor_scalar(halves[:, slot, 0:D], t.acc[:, at(i), :].squeeze(1), 1.0, None,
                                    ALU.mult).then_inc(high_ready, 1)
                    v.wait_ge(high_ready, i + 1)
                    if not first:
                        v.wait_ge(low_ready, i - 1)
                    v.tensor_tensor(rest[:, slot], t.acc[:, at(i), :].squeeze(1), halves[:, slot, 0:D],
                                    ALU.subtract).then_inc(rest_ready, 1)

                normalize(0, 0, True)
                normalize(1, 1, True)
                halve(0, 0, True)
                normalize(2, 0, False)
                halve(1, 1, True)
                with v.Fori(1, T // 2) as pair:
                    i = 2 * pair
                    normalize(i + 1, 1, False)
                    halve(i, 0, False)
                    normalize(i + 2, 0, False)
                    halve(i + 1, 1, False)
                halve(T - 1, 0, False)

            @block.gpsimd
            def _(pool):
                def low(i, slot, first):
                    pool.wait_ge(rest_ready, i + 1)
                    if not first:
                        pool.wait_ge(table_stored[slot], stores_before(i, slot))
                    pool.sem_inc(held, 1)
                    pool.tensor_scalar(halves[:, slot, D:2 * D], rest[:, slot], LOW_SCALE, 1.0, ALU.mult,
                                       ALU.mult).then_inc(low_ready, 1)

                held = sem("held")
                by_pairs(pool, T, low)

            @block.scalar
            def _(a):
                def evacuate(i, slot, first):
                    a.wait_ge(xn_ready, i + 1)
                    a.activation(t.acc[:, at(i), :].squeeze(1), xn[:, slot], ACT.Identity,
                                 bias=t.dis_col(i, 0), scale=t.dis_col(i, 0)).then_inc(scaled, 1)
                    a.wait_ge(turned, i + 1)
                    if not first:
                        a.wait_ge(xt_stored[slot], stores_before(i, slot))
                    a.copy(xt[:, slot], ps_xt[slot][:]).then_inc(xt_ready, 1)

                by_pairs(a, T, evacuate)

            @block.tensor
            def _(pe):
                def turn(i, slot, first):
                    pe.wait_ge(xn_ready, i + 1)
                    if not first:
                        pe.wait_ge(xt_ready, i - 1)
                    for k in range(KD):
                        tr = pe.transpose(ps_xt[slot][:, k * P:(k + 1) * P], xn[:, slot, k * P:(k + 1) * P], t.ident[:])
                    tr.then_inc(turned, 1)

                by_pairs(pe, T, turn)

            @block.sync
            def _(sp):
                def store(i, slot, first):
                    sp.wait_ge(xt_ready, i + 1)
                    sp.dma_start(dram["xt"][at(i)].squeeze(0), xt[:, slot]).then_inc(xt_stored[slot], 16)
                    sp.wait_ge(low_ready, i + 1)
                    sp.dma_start(table[at(i)].squeeze(0), halves[:, slot]).then_inc(table_stored[slot], 16)

                by_pairs(sp, T, store)
                for slot, n in ((0, T // 2 + 1), (1, T // 2)):
                    sp.wait_ge(xt_stored[slot], 16 * n)
                    sp.wait_ge(table_stored[slot], 16 * n)


def aggregate(nc, s, t, dram):
    with ExitStack() as ctx:
        sb, ps, sem = allocate(nc, ctx, "aggregate", t.lasting)
        T, U = s.tiles, s.supers
        RING = 2 * SUPER
        rows = sb("rows", [P, RING, 2 * D], F16)
        index = sb("index", [P, 2, SUPER], I32)
        offsets = sb("offsets", [P, 3, SUPER])
        hot = sb("hot", [P, 3, SUPER, P], F16)
        hot_small = sb("hot_small", [P, 3, SUPER, P], F16)
        zero = sb("zero", [P, P])
        w = sb("w_kv", [P, KD, 2 * D])
        sums = sb("w_sums", [P, KD, 2 * HEADS])
        affine = sb("affine", [P, 4, D])
        xt = sb("xt_kv", [P, 2, D])
        square = sb("square", [P, 2, D])
        var = sb("var_kv", [P, 2, HEADS])
        rstd = sb("rstd_kv", [P, 2, HEADS])
        spare = sb("spare_kv", [P, HEADS])
        kv = sb("kv", [P, 2, 2, D])
        ps_sum = [ps("ps_sum0", [P, D]), ps("ps_sum1", [P, D]), ps("ps_sum2", [P, D])]
        ps_kv = [ps("ps_k", [P, D]), ps("ps_v", [P, D])]
        ps_p = ps("ps_p", [P, D])

        gathered = [sem(f"gathered{i}") for i in range(RING)]
        index_ready = sem("index_ready")
        go = sem("go")
        super_used = sem("super_used")
        placed, further_placed = sem("placed"), sem("further_placed")
        hot_ready, further_hot = sem("hot_ready"), sem("further_hot")
        small_ready, further_small = sem("small_ready"), sem("further_small")
        summed, further_summed = sem("summed"), sem("further_summed")
        added, further_added = sem("added"), sem("further_added")
        load_w = sem("load_w")
        w_ready = sem("w_ready")
        zeroed = sem("zeroed")
        loaded_xt = [sem(f"loaded_xt{i}") for i in range(2)]
        projected = [sem("projected_k"), sem("projected_v")]
        squared = [sem("squared_k"), sem("squared_v")]
        var_ready = [sem("var_ready_k"), sem("var_ready_v")]
        rooted = [sem("rooted_k"), sem("rooted_v")]
        kv_steps = [sem("kv_steps_k"), sem("kv_steps_v")]
        emptied = [sem("emptied_k"), sem("emptied_v")]
        normalized = [sem("normalized_k"), sem("normalized_v")]
        correlated = sem("correlated")
        w_steps = sem("w_steps")

        def span_of(engine, u):
            packed = engine.value_load(t.visits[0:1, at(u)], min_val=0, max_val=(T * U + T) * 4096 + 4095)
            first = (packed & 63).with_bounds(min_val=0, max_val=T - 1)
            end = (first + ((packed >> 6) & 63) + 1).with_bounds(min_val=1, max_val=T)
            offset = (packed >> 12).with_bounds(min_val=1, max_val=T * U + T)
            return first, end, offset

        with nc.Block() as block:

            @block.sync
            def _(sp):
                sp.dma_start(w[:], dram["w_kv"].rearrange("(k p) n -> p k n", p=P)).then_inc(load_w, 16)
                for n, name in enumerate(("gamma_k", "beta_k", "gamma_v", "beta_v")):
                    sp.dma_start(affine[:, n], dram[name].partition_broadcast(P)).then_inc(load_w, 16)

                def load(i, slot, first):
                    if not first:
                        sp.wait_ge(projected[1], i - 1)
                    sp.dma_start(xt[:, slot], dram["xt"][at(i)].squeeze(0)).then_inc(loaded_xt[slot], 16)

                load(0, 0, True)
                load(1, 1, True)
                with sp.Fori(1, T // 2) as pair:
                    load(2 * pair, 0, False)
                    load(2 * pair + 1, 1, False)
                load(T - 1, 0, False)

            @block.gpsimd
            def _(pool):
                pool.memset(zero[:], 0.0).then_inc(zeroed, 1)

                def gather(u, half, first):
                    if not first:
                        pool.wait_ge(super_used, u - 1)
                        pool.sem_inc(go, 1)
                    pool.tensor_copy(index[:, half], t.src[:, at(u * SUPER, SUPER)]).then_inc(index_ready, 1)
                    pool.wait_ge(index_ready, u + 1)
                    pool.sem_inc(go, 1)
                    for k in range(SUPER):
                        slot = half * SUPER + k
                        pool.indirect_dma_start(
                            rows[:, slot], None, dram["table"],
                            bass.IndirectOffsetOnAxis(ap=index[:, half, k:k + 1], axis=0)).then_inc(gathered[slot], 16)

                gather(0, 0, True)
                gather(1, 1, True)
                with pool.Fori(1, T) as i:
                    gather(2 * i, 0, False)
                    gather(2 * i + 1, 1, False)

            @block.vector
            def _(v):
                v.sem_inc(further_placed, T + 1)
                v.sem_inc(further_hot, T + 1)
                v.sem_inc(further_added, T + 1)
                v.wait_ge(load_w, 80)
                step = Chain(v, w_steps)
                grouped = w[:].rearrange("p k (h e) -> p k h e", e=DH)
                step.then(v.tensor_reduce(sums[:], grouped, AX.X, ALU.add))
                step.then(v.tensor_scalar(sums[:], sums[:], 1.0 / DH, None, ALU.mult))
                v.tensor_tensor(grouped, grouped, sums[:].unsqueeze(3).to_broadcast([P, KD, 2 * HEADS, DH]),
                                ALU.subtract).then_inc(w_ready, 1)

                def make_hots(u, b, buffer, done, ready, n):
                    v.tensor_scalar(offsets[:, buffer], t.dst[:, at(u * SUPER, SUPER)], t.neg_block[:, at(b)], None,
                                    ALU.add).then_inc(done, 1)
                    v.wait_ge(done, n + 1)
                    shape = [P, SUPER, P]
                    v.tensor_tensor(hot[:, buffer], t.iota[:].unsqueeze(1).to_broadcast(shape),
                                    offsets[:, buffer].unsqueeze(2).to_broadcast(shape), ALU.is_equal).then_inc(ready, 1)

                def first_hots(u, parity, opening=False):
                    first, _, _ = span_of(v, u)
                    if not opening:
                        v.wait_ge(summed, u - 1)
                    make_hots(u, first, parity, placed, hot_ready, u)

                def add_visits(u, parity):
                    first, end, offset = span_of(v, u)
                    acc = t.acc[:, at(first)].squeeze(1)
                    v.wait_ge(summed, u + 1)
                    v.wait_ge(further_added, offset + first + 1)
                    if not isinstance(u, int) or u > 0:
                        v.wait_ge(added, u)
                    v.tensor_tensor(acc, ps_sum[parity][:], acc, ALU.add).then_inc(added, 1)
                    with v.If(first + 1 < end), v.Fori(first + 1, end) as b:
                        n = offset + b
                        v.wait_ge(further_summed, n)
                        make_hots(u, b, 2, further_placed, further_hot, n)
                        acc = t.acc[:, at(b)].squeeze(1)
                        v.wait_ge(further_summed, n + 1)
                        v.wait_ge(further_added, n)
                        v.wait_ge(added, u + 1)
                        v.tensor_tensor(acc, ps_sum[2][:], acc, ALU.add).then_inc(further_added, 1)

                def post(i, slot, kind, first):
                    per_head = [P, HEADS, DH]
                    v.wait_ge(squared[kind], i + 1)
                    step = Chain(v, kv_steps[kind], 6 * i)
                    step.then(v.tensor_reduce(var[:, kind], square[:, kind].rearrange("p (h e) -> p h e", e=DH), AX.X, ALU.add))
                    v.tensor_scalar(var[:, kind], var[:, kind], 1.0 / DH, EPS, ALU.mult, ALU.add).then_inc(var_ready[kind], 1)
                    out = kv[:, kind, slot]
                    if not first:
                        v.wait_ge(correlated, i - 1)
                    v.tensor_tensor(out, ps_kv[kind][:], affine[:, 2 * kind], ALU.mult).then_inc(emptied[kind], 1)
                    v.wait_ge(var_ready[kind], i + 1)
                    v.wait_ge(rooted[kind], i + 1)
                    step.then(v.reciprocal(rstd[:, kind], rstd[:, kind]))
                    refine_root(v, step, rstd[:, kind], var[:, kind], spare[:])
                    v.wait_ge(emptied[kind], i + 1)
                    heads = out.rearrange("p (h e) -> p h e", e=DH)
                    v.tensor_tensor(heads, heads, rstd[:, kind].unsqueeze(2).to_broadcast(per_head),
                                    ALU.mult).then_inc(normalized[kind], 1)
                    v.wait_ge(normalized[kind], 2 * i + 1)
                    v.tensor_tensor(out, out, affine[:, 2 * kind + 1], ALU.add).then_inc(normalized[kind], 1)

                def beside(i, slot, last=False):
                    number = i if isinstance(i, int) else T
                    first_hots(2 * i + 1, 1, number == 0)
                    add_visits(2 * i, 0)
                    if number > 0:
                        post(i - 1, 1 - slot, 1, number < 3)
                    if not last:
                        first_hots(2 * i + 2, 0)
                    add_visits(2 * i + 1, 1)
                    post(i, slot, 0, number < 2)

                first_hots(0, 0, True)
                for i in range(3):
                    beside(i, i % 2)
                with v.Fori(1, T // 2 - 1) as pair:
                    beside(2 * pair + 1, 1)
                    beside(2 * pair + 2, 0)
                beside(T - 2, 1)
                beside(T - 1, 0, True)
                post(T - 1, 0, 1, False)
                v.memset(t.p[:], 0.0).then_inc(zeroed, 1)
                v.wait_ge(zeroed, 2)
                v.wait_ge(correlated, T)
                for head in range(HEADS):
                    rows = slice(head % 2 * DH, head % 2 * DH + DH)
                    cols = slice(head * DH, head * DH + DH)
                    v.tensor_scalar(t.p[rows, cols], ps_p[rows, cols], 1.0 / s.nodes, None, ALU.mult)

            @block.scalar
            def _(a):
                def first_small(u, parity):
                    a.wait_ge(hot_ready, u + 1)
                    a.activation(hot_small[:, parity], hot[:, parity], ACT.Copy, scale=1.0 / LOW_SCALE).then_inc(small_ready, 1)

                def further_smalls(u):
                    first, end, offset = span_of(a, u)
                    with a.If(first + 1 < end), a.Fori(first + 1, end) as b:
                        a.wait_ge(further_hot, offset + b + 1)
                        a.sem_inc(go, 1)
                        a.activation(hot_small[:, 2], hot[:, 2], ACT.Copy, scale=1.0 / LOW_SCALE).then_inc(further_small, 1)

                def squares(i, kind):
                    a.wait_ge(projected[kind], i + 1)
                    a.activation(square[:, kind], ps_kv[kind][:], ACT.Square).then_inc(squared[kind], 1)

                def root(i, kind):
                    a.wait_ge(var_ready[kind], i + 1)
                    a.activation(rstd[:, kind], var[:, kind], ACT.Sqrt).then_inc(rooted[kind], 1)

                def beside(i, opening=False, last=False):
                    first_small(2 * i + 1, 1)
                    further_smalls(2 * i)
                    squares(i, 0)
                    if not opening:
                        root(i - 1, 1)
                    if not last:
                        first_small(2 * i + 2, 0)
                    further_smalls(2 * i + 1)
                    squares(i, 1)
                    root(i, 0)

                a.sem_inc(further_small, T + 1)
                first_small(0, 0)
                beside(0, opening=True)
                with a.Fori(1, T - 1) as i:
                    beside(i)
                beside(T - 1, last=True)
                root(T - 1, 1)

            @block.tensor
            def _(pe):
                def products(bank, buffer, half, ready, small, n, done):
                    for part, (hots, signal) in enumerate(((hot, ready), (hot_small, small))):
                        pe.wait_ge(signal, n + 1)
                        for k in range(SUPER):
                            mm = pe.matmul(bank[:], hots[:, buffer, k], rows[:, half * SUPER + k, part * D:(part + 1) * D],
                                           start=part == 0 and k == 0, stop=part == 1 and k == SUPER - 1)
                    mm.then_inc(done, 1)

                def first_visit(u, i, half):
                    for k in range(SUPER):
                        pe.wait_ge(gathered[half * SUPER + k], (i + 1) * 16)
                    if not isinstance(u, int) or u > 1:
                        pe.wait_ge(added, u - 1)
                    products(ps_sum[half], half, half, hot_ready, small_ready, u, summed)

                def further_visits(u, half):
                    first, end, offset = span_of(pe, u)
                    with pe.If(first + 1 < end), pe.Fori(first + 1, end) as b:
                        n = offset + b
                        pe.wait_ge(further_added, n)
                        products(ps_sum[2], 2, half, further_hot, further_small, n, further_summed)
                    pe.wait_ge(summed, u + 1)
                    pe.wait_ge(further_summed, offset + end)
                    pe.sem_inc(super_used, 1)

                def project(i, slot, kind, first):
                    if kind == 0:
                        pe.wait_ge(loaded_xt[slot], 8 * (i - slot) + 16)
                    if not first:
                        pe.wait_ge(emptied[kind], i)
                    for k in range(KD):
                        mm = pe.matmul(ps_kv[kind][:], xt[:, slot, k * P:(k + 1) * P], w[:, k, kind * D:(kind + 1) * D],
                                       start=k == 0, stop=k == KD - 1)
                    mm.then_inc(projected[kind], 1)

                def correlate(i, slot, n=P):
                    pe.wait_ge(normalized[0], 2 * i + 2)
                    pe.wait_ge(normalized[1], 2 * i + 2)
                    for pair in range(HEADS // 2):
                        cols = slice(pair * P, (pair + 1) * P)
                        mm = pe.matmul(ps_p[:, cols], kv[0:n, 1, slot, cols], kv[0:n, 0, slot, cols],
                                       start=False, stop=True, skip_group_check=True)
                    mm.then_inc(correlated, 1)

                def beside(i, slot, first):
                    for half in range(2):
                        first_visit(2 * i + half, i, half)
                        project(i, slot, half, first)
                        further_visits(2 * i + half, half)
                    if not first:
                        correlate(i - 1, 1 - slot)

                pe.sem_inc(further_summed, T + 1)
                pe.wait_ge(zeroed, 1)
                pe.wait_ge(w_ready, 1)
                pe.matmul(ps_p[:], zero[:], w[:, 0, 0:D], start=True, stop=True)
                beside(0, 0, True)
                with pe.Fori(0, T // 2) as pair:
                    beside(2 * pair + 1, 1, False)
                    beside(2 * pair + 2, 0, False)
                correlate(T - 1, 0, s.last)


def fold(nc, s, t, dram):
    with ExitStack() as ctx:
        sb, ps, sem = allocate(nc, ctx, "fold", t.lasting)
        wq = sb("wq", [P, KD, D])
        wo = sb("wo", [P, KD, D])
        pw = sb("pw", [P, KD, D])
        ps_pw = [ps(f"ps_pw{i}", [P, D]) for i in range(KD)]
        ps_m = [ps(f"ps_m{i}", [P, D]) for i in range(KD)]
        loaded = sem("loaded")
        pw_done = sem("pw_done")
        pw_ready = sem("pw_ready")
        m_done = sem("m_done")

        with nc.Block() as block:

            @block.sync
            def _(sp):
                sp.dma_start(wo[:], dram["w_out"].rearrange("(k p) n -> p k n", p=P)).then_inc(loaded, 16)
                sp.dma_start(wq[:], dram["w_q"].rearrange("(k p) n -> p k n", p=P)).then_inc(loaded, 16)

            @block.tensor
            def _(pe):
                pe.wait_ge(loaded, 32)
                for j in range(KD):
                    pe.matmul(ps_pw[j][:], t.p[:, j * P:(j + 1) * P], wo[:, j], start=True, stop=True).then_inc(pw_done, 1)
                for m in range(KD):
                    for j in range(KD):
                        if m == 0:
                            pe.wait_ge(pw_ready, j + 1)
                        mm = pe.matmul(ps_m[m][:], wq[:, j, m * P:(m + 1) * P], pw[:, j], start=j == 0, stop=j == KD - 1)
                    mm.then_inc(m_done, 1)

            @block.vector
            def _(v):
                for j in range(KD):
                    v.wait_ge(pw_done, j + 1)
                    v.tensor_copy(pw[:, j], ps_pw[j][:]).then_inc(pw_ready, 1)
                for m in range(KD):
                    v.wait_ge(m_done, m + 1)
                    v.tensor_copy(t.m[:, m], ps_m[m][:])


def mix(nc, s, t, dram):
    with ExitStack() as ctx:
        sb, ps, sem = allocate(nc, ctx, "mix", t.lasting)
        T = s.tiles
        wg = sb("w_gnn", [P, KD, D])
        w_gate = sb("w_gate", [P, KD, GATE])
        b_gate = sb("b_gate", [P, GATE])
        b_gnn = sb("b_gnn", [P, D])
        b_out = sb("b_out", [P, D])
        power = sb("power", [P, 1])
        x = sb("x", [P, 2, D])
        xt = sb("xt", [P, 2, D])
        y = sb("y", [P, 2, D])
        yt = sb("yt", [P, 2, D])
        part = sb("part", [P, D])
        tok = sb("tok", [P, 2, D])
        tt = sb("tt", [P, 2, D])
        stats_y = sb("stats_y", [P, 6])
        stats_x1 = sb("stats_x1", [P, 6])
        moment_y = sb("moment_y", [P, 2, 2])
        moment_x1 = sb("moment_x1", [P, 2, 2])
        weight = sb("weight", [P, 2])
        var = sb("var", [P, 2])
        rstd = sb("rstd", [P, 2])
        ps_yt = ps("ps_yt", [P, D])
        ps_tt = ps("ps_tt", [P, D])
        ps_g = [ps(f"ps_g{i}", [P, D]) for i in range(2)]
        ps_a = [ps(f"ps_a{i}", [P, D]) for i in range(2)]
        ps_gate = [ps(f"ps_gate{i}", [P, D]) for i in range(2)]
        load_w = sem("load_w")
        load_x = [sem(f"load_x{i}") for i in range(2)]
        load_xt = [sem(f"load_xt{i}") for i in range(2)]
        powered = sem("powered")
        go = sem("go")
        x_biased = sem("x_biased")
        centring = sem("centring")
        y_ready = sem("y_ready")
        y_turned = sem("y_turned")
        yt_ready = sem("yt_ready")
        g_done = sem("g_done")
        a_done = sem("a_done")
        sums = sem("sums")
        ln = sem("ln")
        rooted = sem("rooted")
        tok_ready = sem("tok_ready")
        tok_turned = sem("tok_turned")
        tt_ready = sem("tt_ready")
        gated = sem("gated")
        gate_read = sem("gate_read")
        tok_stored = [sem(f"tok_stored{i}") for i in range(2)]
        x1_stored = sem("x1_stored")

        def pipeline(engine, body):
            has = lambda i: not isinstance(i, int) or 0 <= i < T
            for i in range(-1, 4):
                body(i, i % 2, has)
            with engine.Fori(2, (T - 1) // 2) as pair:
                body(2 * pair, 0, has)
                body(2 * pair + 1, 1, has)
            for i in range(T - 1, T + 3):
                body(i, i % 2, has)

        with nc.Block() as block:

            @block.sync
            def _(sp):
                sp.dma_start(wg[:], dram["w_gnn"].rearrange("(k p) n -> p k n", p=P)).then_inc(load_w, 16)
                sp.dma_start(b_gnn[:], dram["b_gnn"].partition_broadcast(P)).then_inc(load_w, 16)
                sp.dma_start(b_out[:], dram["b_out"].partition_broadcast(P)).then_inc(load_w, 16)
                sp.dma_start(w_gate[:], dram["w_gate1"].rearrange("(k p) n -> p k n", p=P)).then_inc(load_w, 16)
                sp.dma_start(b_gate[:], dram["b_gate1"].partition_broadcast(P)).then_inc(load_w, 16)
                xv = dram["x"].rearrange("(t p) d -> t p d", p=P)

                def load(i, slot, first):
                    if not first:
                        sp.wait_ge(a_done, i - 1)
                    sp.dma_start(xt[:, slot], dram["xt"][at(i)].squeeze(0)).then_inc(load_xt[slot], 16)
                    if not first:
                        sp.wait_ge(sums, 3 * i - 3)
                    sp.dma_start(x[:, slot], xv[at(i)].squeeze(0)).then_inc(load_x[slot], 16)

                by_pairs(sp, T, load)

            @block.gpsimd
            def _(pool):
                pool.memset(power[:], -0.5).then_inc(powered, 1)
                pool.wait_ge(powered, 1)
                pool.wait_ge(load_w, 5 * 16)

                def body(i, slot, has):
                    if has(i):
                        pool.wait_ge(load_x[slot], 8 * (i - slot) + 16)
                        pool.tensor_tensor(x[:, slot], x[:, slot], b_out[:], ALU.add).then_inc(x_biased, 1)
                    if has(i - 1):
                        last = slice(1 - slot, 2 - slot)
                        pool.wait_ge(ln, 3 * i)
                        pool.tensor_tensor(rstd[:, last], var[:, last], power[:], ALU.pow).then_inc(rooted, 1)

                pipeline(pool, body)

            @block.vector
            def _(v):
                v.wait_ge(load_w, 5 * 16)

                def centre(i, slot):
                    acc = t.acc[:, at(i)].squeeze(1)
                    need(v, centring, 3 * i)
                    need(v, sums, 3 * i - 3)
                    v.sem_inc(go, 1)
                    v.bn_stats(stats_y[:], acc).then_inc(centring, 1)
                    v.wait_ge(centring, 3 * i + 1)
                    need(v, y_ready, i - 1)
                    v.sem_inc(go, 1)
                    v.bn_aggr(moment_y[:, slot], stats_y[:]).then_inc(centring, 1)
                    v.wait_ge(centring, 3 * i + 2)
                    v.tensor_scalar(weight[:, slot:slot + 1], moment_y[:, slot, 0:1], t.dis_back[:, at(i)], None,
                                    ALU.mult).then_inc(centring, 1)
                    need(v, y_turned, i - 1)
                    v.tensor_scalar(y[:, slot], acc, moment_y[:, slot, 0:1], t.dis_back[:, at(i)], ALU.subtract,
                                    ALU.mult).then_inc(y_ready, 1)

                def add(i, slot):
                    v.wait_ge(g_done, i + 1)
                    v.wait_ge(centring, 3 * i + 3)
                    need(v, sums, 3 * i)
                    v.scalar_tensor_tensor(part[:], b_gnn[:], weight[:, slot:slot + 1], ps_g[slot][:], ALU.mult,
                                           ALU.add).then_inc(sums, 1)
                    v.wait_ge(sums, 3 * i + 1)
                    v.wait_ge(a_done, i + 1)
                    v.scalar_tensor_tensor(part[:], part[:], 0.0, ps_a[slot][:], ALU.max, ALU.add).then_inc(sums, 1)
                    v.wait_ge(sums, 3 * i + 2)
                    v.wait_ge(x_biased, i + 1)
                    v.wait_ge(y_ready, i + 1)
                    v.tensor_tensor(t.acc[:, at(i)].squeeze(1), part[:], x[:, slot], ALU.add).then_inc(sums, 1)

                def statistics(i, slot):
                    v.wait_ge(sums, 3 * i + 3)
                    need(v, ln, 3 * i)
                    v.sem_inc(go, 1)
                    v.bn_stats(stats_x1[:], t.acc[:, at(i)].squeeze(1)).then_inc(ln, 1)
                    v.wait_ge(ln, 3 * i + 1)
                    need(v, tok_ready, i - 1)
                    v.sem_inc(go, 1)
                    v.bn_aggr(moment_x1[:, slot], stats_x1[:]).then_inc(ln, 1)
                    v.wait_ge(ln, 3 * i + 2)
                    v.tensor_scalar(var[:, slot:slot + 1], moment_x1[:, slot, 1:2], EPS, None, ALU.add).then_inc(ln, 1)

                def normalize(i, slot):
                    v.wait_ge(rooted, i + 1)
                    v.wait_ge(ln, 3 * i + 2)
                    need(v, tok_turned, i - 1)
                    need(v, tok_stored[slot], 8 * (i - slot))
                    v.tensor_scalar(tok[:, slot], t.acc[:, at(i)].squeeze(1), moment_x1[:, slot, 0:1], rstd[:, slot:slot + 1],
                                    ALU.subtract, ALU.mult).then_inc(tok_ready, 1)

                def keep(i, slot):
                    v.wait_ge(gated, i + 1)
                    v.tensor_tensor(t.gate[:, at(i)].squeeze(1), ps_gate[slot][:, 0:GATE], b_gate[:], ALU.add).then_inc(gate_read, 1)

                def body(i, slot, has):
                    if has(i - 1):
                        add(i - 1, 1 - slot)
                        statistics(i - 1, 1 - slot)
                    if has(i + 1):
                        centre(i + 1, 1 - slot)
                    if has(i - 1):
                        normalize(i - 1, 1 - slot)
                    if has(i - 3):
                        keep(i - 3, 1 - slot)

                pipeline(v, body)

            @block.scalar
            def _(a):
                x1_rows = dram["x1"].rearrange("(t p) d -> t p d", p=P)
                tok_rows = dram["tok"].rearrange("(t p) d -> t p d", p=P)

                def body(i, slot, has):
                    if has(i - 1):
                        a.wait_ge(sums, 3 * i)
                        need(a, x1_stored, 16 * (i - 1))
                        a.dma_start(x1_rows[at(i - 1)].squeeze(0), t.acc[:, at(i - 1)].squeeze(1)).then_inc(x1_stored, 16)
                    if has(i + 1):
                        a.wait_ge(y_turned, i + 2)
                        need(a, g_done, i)
                        a.copy(yt[:, 1 - slot], ps_yt[:]).then_inc(yt_ready, 1)
                    if has(i - 1):
                        a.wait_ge(tok_ready, i)
                        a.dma_start(tok_rows[at(i - 1)].squeeze(0), tok[:, 1 - slot]).then_inc(tok_stored[1 - slot], 16)
                        a.wait_ge(tok_turned, i)
                        need(a, gated, i - 2)
                        a.copy(tt[:, 1 - slot], ps_tt[:]).then_inc(tt_ready, 1)

                pipeline(a, body)
                a.wait_ge(x1_stored, 16 * T)
                for slot, n in ((0, T // 2 + 1), (1, T // 2)):
                    a.wait_ge(tok_stored[slot], 16 * n)

            @block.tensor
            def _(pe):
                pe.wait_ge(load_w, 5 * 16)

                def attention(i, slot):
                    pe.wait_ge(load_xt[slot], 8 * (i - slot) + 16)
                    need(pe, sums, 3 * i - 4)
                    for k in range(KD):
                        mm = pe.matmul(ps_a[slot][:], xt[:, slot, k * P:(k + 1) * P], t.m[:, k], start=k == 0, stop=k == KD - 1)
                    mm.then_inc(a_done, 1)

                def gnn(i, slot):
                    pe.wait_ge(yt_ready, i + 1)
                    need(pe, sums, 3 * i - 5)
                    for k in range(KD):
                        mm = pe.matmul(ps_g[slot][:], yt[:, slot, k * P:(k + 1) * P], wg[:, k], start=k == 0, stop=k == KD - 1)
                    mm.then_inc(g_done, 1)

                def turn(i, slot, rows, ready, bank, emptied, turned):
                    pe.wait_ge(ready, i + 1)
                    need(pe, emptied, i)
                    for k in range(KD):
                        tr = pe.transpose(bank[:, k * P:(k + 1) * P], rows[:, slot, k * P:(k + 1) * P], t.ident[:])
                    tr.then_inc(turned, 1)

                def gate(i, slot):
                    pe.wait_ge(tt_ready, i + 1)
                    need(pe, gate_read, i - 1)
                    for k in range(KD):
                        mm = pe.matmul(ps_gate[slot][:, 0:GATE], tt[:, slot, k * P:(k + 1) * P], w_gate[:, k], start=k == 0,
                                       stop=k == KD - 1)
                    mm.then_inc(gated, 1)

                def body(i, slot, has):
                    if has(i):
                        attention(i, slot)
                    if has(i - 2):
                        gate(i - 2, slot)
                    if has(i):
                        gnn(i, slot)
                    if has(i + 1):
                        turn(i + 1, 1 - slot, y, y_ready, ps_yt, yt_ready, y_turned)
                    if has(i - 1):
                        turn(i - 1, 1 - slot, tok, tok_ready, ps_tt, tt_ready, tok_turned)

                pipeline(pe, body)


def route(nc, s, t, dram):
    with ExitStack() as ctx:
        sb, ps, sem = allocate(nc, ctx, "route", t.lasting)
        T, E, S = s.tiles, EXPERTS, s.slot_tiles
        w = sb("w", [P, E, GATE])
        b = sb("b", [P, E])
        ids = sb("ids", [P, T])
        upper = sb("upper", [P, P])
        ones = sb("ones", [P, P])
        products = sb("products", [P, T, E, GATE])
        logits = sb("logits", [P, T, E])
        order = sb("order", [P, E])
        top = sb("top", [P, 2, T])
        same = sb("same", [P, T, E])
        pick = sb("pick", [P, T])
        hot = sb("hot", [P, 2, T, E])
        mask = sb("mask", [P, T, E])
        down = sb("down", [P, T])
        rank = sb("rank", [P, T, E])
        total = sb("total", [P, T, E])
        run = [sb("run0", [P, T, E]), sb("run1", [P, T, E])]
        count = sb("count", [P, E])
        count_int = sb("count_int", [P, 2, E], I32)
        tiles_of = sb("tiles_of", [P, E])
        ends = [sb("ends0", [P, E]), sb("ends1", [P, E])]
        base = sb("base", [P, E])
        slot = sb("slot", [P, T, 2])
        slot_low = sb("slot_low", [P, T, 2], I32)
        slot_high = sb("slot_high", [P, T, 2], I32)
        low = sb("low", [P, T, 2])
        high = sb("high", [P, T, 2])
        reached = sb("reached", [1, S, E])
        expert = sb("expert", [1, S])
        hot_low = sb("hot_low", [P, 2, P])
        hot_high = sb("hot_high", [P, 2, S])
        ps_rank = ps("ps_rank", [P, 512])
        ps_total = ps("ps_total", [P, 512])
        ps_list = ps("ps_list", [P, 512])
        loaded = sem("loaded")
        gelu = sem("gelu")
        steps = sem("steps")
        one = sem("one")
        exp_in = sem("exp_in")
        exp_out = sem("exp_out")
        masked = sem("masked")
        ranked = sem("ranked")
        hots = sem("hots")
        listed = sem("listed")
        opened = sem("opened")

        with nc.Block() as block:

            @block.sync
            def _(sp):
                sp.dma_start(w[:], dram["w_gate2"].partition_broadcast(P)).then_inc(loaded, 16)
                sp.dma_start(b[:], dram["b_gate2"].partition_broadcast(P)).then_inc(loaded, 16)
                sp.dma_start(ids[:], dram["ids"]).then_inc(loaded, 16)
                sp.dma_start(upper[:], dram["upper"]).then_inc(loaded, 16)

            @block.gpsimd
            def _(pool):
                pool.memset(ones[:], 1.0).then_inc(one, 1)

            @block.scalar
            def _(a):
                a.activation(t.gate[:], t.gate[:], ACT.Gelu).then_inc(gelu, 1)
                a.wait_ge(exp_in, 1)
                a.activation(down[:], down[:], ACT.Exp).then_inc(exp_out, 1)

            @block.vector
            def _(v):
                step = Chain(v, steps)
                over_t = lambda a: a.unsqueeze(1).to_broadcast([P, T, E])
                over_e = lambda a: a.unsqueeze(2).to_broadcast([P, T, E])
                v.wait_ge(loaded, 64)
                step.mark(v.tensor_scalar(order[:], t.iota[:, 0:E], -1.0, float(E), ALU.mult, ALU.add))
                v.wait_ge(gelu, 1)
                step.then(v.tensor_tensor(products[:], t.gate[:].unsqueeze(2).to_broadcast([P, T, E, GATE]),
                                          w[:].unsqueeze(1).to_broadcast([P, T, E, GATE]), ALU.mult))
                step.then(v.tensor_reduce(logits[:], products[:], AX.X, ALU.add))
                step.then(v.tensor_tensor(logits[:], logits[:], over_t(b[:]), ALU.add))
                for n in range(2):
                    step.then(v.tensor_reduce(top[:, n], logits[:], AX.X, ALU.max))
                    step.then(v.tensor_tensor(same[:], logits[:], over_e(top[:, n]), ALU.is_equal))
                    step.then(v.tensor_tensor(same[:], same[:], over_t(order[:]), ALU.mult))
                    step.then(v.tensor_reduce(pick[:], same[:], AX.X, ALU.max))
                    step.then(v.tensor_tensor(hot[:, n], over_t(order[:]), over_e(pick[:]), ALU.is_equal))
                    if n == 0:
                        step.then(v.scalar_tensor_tensor(logits[:], hot[:, 0], -3.0e38, logits[:], ALU.mult, ALU.add))
                step.then(v.tensor_tensor(down[:], top[:, 1], top[:, 0], ALU.subtract))
                v.sem_inc(exp_in, 1)
                step.then(v.tensor_tensor(mask[:], hot[:, 0], hot[:, 1], ALU.add))
                v.sem_inc(masked, 1)
                v.wait_ge(exp_out, 1)
                step.then(v.tensor_scalar(pick[:], down[:], 1.0, None, ALU.add))
                step.then(v.reciprocal(t.weight[:, :, 0], pick[:]))
                step.mark(v.tensor_tensor(t.weight[:, :, 1], t.weight[:, :, 0], down[:], ALU.mult))
                v.wait_ge(ranked, 1)
                step.mark(v.tensor_copy(rank[:], ps_rank[:, 0:T * E]))
                step.mark(v.tensor_copy(total[:], ps_total[:, 0:T * E]))
                step.then(v.tensor_copy(run[0][:], ps_total[:, 0:T * E]))
                now, shift = 0, 1
                while shift < T:
                    old, new = run[now], run[1 - now]
                    step.mark(v.tensor_copy(new[:, 0:shift], old[:, 0:shift]))
                    step.then(v.tensor_tensor(new[:, shift:], old[:, shift:], old[:, 0:T - shift], ALU.add))
                    now, shift = 1 - now, 2 * shift
                step.mark(v.tensor_copy(count_int[:, 0], run[now][:, T - 1]))
                step.then(v.tensor_tensor(rank[:], rank[:], run[now][:], ALU.add))
                step.then(v.tensor_tensor(rank[:], rank[:], total[:], ALU.subtract))
                step.then(v.tensor_scalar(count[:], count_int[:, 0], float(P - 1), None, ALU.add))
                step.then(v.tensor_copy(count_int[:, 0], count[:]))
                step.then(v.tensor_single_scalar(count_int[:, 1], count_int[:, 0], 7, op=ALU.logical_shift_right))
                step.mark(v.tensor_copy(tiles_of[:], count_int[:, 1]))
                step.then(v.tensor_copy(ends[0][:], count_int[:, 1]))
                now, shift = 0, 1
                while shift < E:
                    old, new = ends[now], ends[1 - now]
                    step.mark(v.tensor_copy(new[:, 0:shift], old[:, 0:shift]))
                    step.then(v.tensor_tensor(new[:, shift:], old[:, shift:], old[:, 0:E - shift], ALU.add))
                    now, shift = 1 - now, 2 * shift
                end = ends[now]
                step.then(v.tensor_tensor(base[:], end[:], tiles_of[:], ALU.subtract))
                step.then(v.tensor_scalar(base[:], base[:], float(P), None, ALU.mult))
                step.then(v.tensor_tensor(rank[:], rank[:], over_t(base[:]), ALU.add))
                for n in range(2):
                    step.then(v.tensor_tensor(same[:], hot[:, n], rank[:], ALU.mult))
                    step.then(v.tensor_reduce(slot[:, :, n], same[:], AX.X, ALU.add))
                step.then(v.tensor_copy(t.slot[:], slot[:]))
                step.mark(v.tensor_single_scalar(slot_low[:], t.slot[:], P - 1, op=ALU.bitwise_and))
                step.then(v.tensor_single_scalar(slot_high[:], t.slot[:], 7, op=ALU.logical_shift_right))
                step.mark(v.tensor_copy(low[:], slot_low[:]))
                step.mark(v.tensor_copy(high[:], slot_high[:]))
                steps_row = [1, S, E]
                step.then(v.tensor_tensor(reached[:], t.iota[0:1, 0:S].unsqueeze(2).to_broadcast(steps_row),
                                          end[0:1].unsqueeze(1).to_broadcast(steps_row), ALU.is_ge))
                step.then(v.tensor_reduce(expert[:], reached[:], AX.X, ALU.add))
                step.then(v.tensor_scalar(expert[:], expert[:], float(E - 1), None, ALU.min))
                step.then(v.tensor_copy(t.expert[:], expert[:]))

                def spot(i, first):
                    for n in range(2):
                        if not first:
                            v.wait_ge(listed, 2 * i + n - 1)
                        v.tensor_scalar(hot_low[:, n], t.iota[:], low[:, at(i), n], None, ALU.is_equal).then_inc(hots, 1)
                        v.tensor_scalar(hot_high[:, n], t.iota[:, 0:S], high[:, at(i), n], ids[:, at(i)], ALU.is_equal,
                                        ALU.mult).then_inc(hots, 1)

                spot(0, True)
                with v.Fori(1, T) as i:
                    spot(i, False)
                v.wait_ge(listed, 2 * T)
                v.tensor_copy(t.token[:], ps_list[:, 0:S])

            @block.tensor
            def _(pe):
                pe.wait_ge(loaded, 64)
                pe.wait_ge(one, 1)
                pe.wait_ge(masked, 1)
                pe.matmul(ps_rank[:, 0:T * E], upper[:], mask[:].rearrange("p t e -> p (t e)"), start=True, stop=True)
                pe.matmul(ps_total[:, 0:T * E], ones[:], mask[:].rearrange("p t e -> p (t e)"), start=True,
                          stop=True).then_inc(ranked, 1)

                def place(i, opening):
                    for n in range(2):
                        pe.wait_ge(hots, 4 * i + 2 * n + 2)
                        pe.matmul(ps_list[:, 0:S], hot_low[:, n], hot_high[:, n], start=opening and n == 0, stop=True,
                                  skip_group_check=True).then_inc(listed, 1)

                place(0, True)
                with pe.Fori(1, T) as i:
                    place(i, False)


def experts(nc, s, t, dram):
    with ExitStack() as ctx:
        sb, ps, sem = allocate(nc, ctx, "experts", t.lasting)
        E, N = EXPERTS, s.slot_tiles
        KH = H2 // P
        w = [sb("w1", [P, KD, E, H2]), sb("w2", [P, KH, E, H2]), sb("w3", [P, KH, E, D])]
        b = [sb("b1", [P, E, H2]), sb("b2", [P, E, H2]), sb("b3", [P, E, D])]
        affine = sb("affine", [P, 2, 2, KH, E])
        index = sb("index", [P, 2, 1], I32)
        rows = sb("rows", [P, 2, D])
        xt = sb("xt", [P, 2, D])
        h = [sb("h1", [P, H2]), sb("h2", [P, H2])]
        stats = sb("stats", [P, 2, 6])
        moment = sb("moment", [P, 2, 2])
        var = sb("var", [P, 2])
        power = sb("power", [P, 1])
        rstd = sb("rstd", [P, 2])
        v_ = [sb("v1", [P, H2]), sb("v2", [P, H2])]
        a_ = [sb("a1", [P, H2]), sb("a2", [P, H2])]
        o = sb("o", [P, 2, D])
        ps_t = [ps(f"ps_t{i}", [P, D]) for i in range(2)]
        ps_h = [ps(f"ps_h{i}", [P, D]) for i in range(2)]
        ps_u = [ps(f"ps_u{i}", [P, D]) for i in range(2)]
        ps_o = [ps(f"ps_o{i}", [P, D]) for i in range(2)]
        load_w = sem("load_w")
        indexed = sem("indexed")
        powered = sem("powered")
        go = sem("go")
        gathered = [sem(f"gathered{i}") for i in range(2)]
        turned = sem("turned")
        xt_ready = sem("xt_ready")
        h_done = [sem("h1_done"), sem("h2_done")]
        ln = [sem("ln1"), sem("ln2")]
        rooted = [sem("rooted1"), sem("rooted2")]
        v_ready = [sem("v1_ready"), sem("v2_ready")]
        u_done = [sem("u1_done"), sem("u2_done")]
        a_ready = [sem("a1_ready"), sem("a2_ready")]
        o_done = sem("o_done")
        o_ready = sem("o_ready")
        stored = [sem(f"stored{i}") for i in range(2)]

        def pipeline(engine, body):
            has = lambda i: not isinstance(i, int) or 0 <= i < N
            for i in range(-1, 4):
                body(i, i % 2, has)
            with engine.Fori(2, (N - 4) // 2) as pair:
                body(2 * pair, 0, lambda i: True)
                body(2 * pair + 1, 1, lambda i: True)
            for i in range(N - 4, N + 3):
                body(i, i % 2, has)

        def expert_of(engine, i):
            return engine.value_load(t.expert[0:1, at(i)], min_val=0, max_val=E - 1)

        with nc.Block() as block:

            @block.sync
            def _(sp):
                for n in range(3):
                    sp.dma_start(w[n][:], dram[f"w{n + 1}"]).then_inc(load_w, 16)
                    sp.dma_start(b[n][:], dram[f"b{n + 1}"].partition_broadcast(P)).then_inc(load_w, 16)
                sp.dma_start(affine[:], dram["affine"]).then_inc(load_w, 16)
                slots = dram["slots"].rearrange("(t p) d -> t p d", p=P)

                def store(i, slot, has):
                    if has(i):
                        sp.wait_ge(o_ready, i + 1)
                        sp.dma_start(slots[at(i)].squeeze(0), o[:, slot]).then_inc(stored[slot], 16)

                pipeline(sp, store)
                for slot in range(2):
                    sp.wait_ge(stored[slot], 8 * N)

            @block.gpsimd
            def _(pool):
                pool.memset(power[:], -0.5).then_inc(powered, 1)
                pool.wait_ge(powered, 1)

                def gather(i, slot):
                    need(pool, turned, i - 1)
                    pool.sem_inc(go, 1)
                    pool.tensor_copy(index[:, slot], t.token[:, at(i)]).then_inc(indexed, 1)
                    pool.wait_ge(indexed, i + 1)
                    pool.sem_inc(go, 1)
                    pool.indirect_dma_start(rows[:, slot], None, dram["tok"],
                                            bass.IndirectOffsetOnAxis(ap=index[:, slot], axis=0)).then_inc(gathered[slot], 16)

                def root(i, layer):
                    pool.wait_ge(ln[layer], 4 * i + 4)
                    pool.tensor_tensor(rstd[:, layer:layer + 1], var[:, layer:layer + 1], power[:], ALU.pow)\
                        .then_inc(rooted[layer], 1)

                def body(i, slot, has):
                    if has(i + 3):
                        gather(i + 3, 1 - slot)
                    if has(i):
                        root(i, 0)
                    if has(i - 1):
                        root(i - 1, 1)

                gather(0, 0)
                gather(1, 1)
                pipeline(pool, body)

            @block.vector
            def _(v):
                v.wait_ge(load_w, 7 * 16)

                def add_bias(i, layer):
                    e = expert_of(v, i)
                    v.wait_ge(h_done[layer], i + 1)
                    need(v, v_ready[layer], i)
                    v.tensor_tensor(h[layer][:], ps_h[layer][:, 0:H2], b[layer][:, at(e)].squeeze(1),
                                    ALU.add).then_inc(ln[layer], 1)

                def statistics(i, layer):
                    v.wait_ge(ln[layer], 4 * i + 1)
                    v.bn_stats(stats[:, layer], h[layer][:]).then_inc(ln[layer], 1)

                def moments_of(i, layer):
                    v.wait_ge(ln[layer], 4 * i + 2)
                    v.sem_inc(go, 1)
                    v.bn_aggr(moment[:, layer], stats[:, layer]).then_inc(ln[layer], 1)

                def guarded_variance(i, layer):
                    v.wait_ge(ln[layer], 4 * i + 3)
                    v.tensor_scalar(var[:, layer:layer + 1], moment[:, layer, 1:2], EPS, None, ALU.add).then_inc(ln[layer], 1)

                def normalize(i, layer):
                    v.wait_ge(rooted[layer], i + 1)
                    need(v, u_done[layer], i)
                    v.tensor_scalar(v_[layer][:], h[layer][:], moment[:, layer, 0:1], rstd[:, layer:layer + 1], ALU.subtract,
                                    ALU.mult).then_inc(v_ready[layer], 1)

                def finish(i, slot):
                    e = expert_of(v, i)
                    v.wait_ge(o_done, i + 1)
                    need(v, stored[slot], 8 * (i - slot))
                    v.tensor_tensor(o[:, slot], ps_o[slot][:], b[2][:, at(e)].squeeze(1), ALU.add).then_inc(o_ready, 1)

                def body(i, slot, has):
                    for layer in range(2):
                        if has(i - layer):
                            for part in (add_bias, statistics, moments_of, guarded_variance):
                                part(i - layer, layer)
                        if layer == 0 and has(i - 3):
                            finish(i - 3, 1 - slot)
                        if has(i - layer):
                            normalize(i - layer, layer)

                pipeline(v, body)

            @block.scalar
            def _(a):
                a.wait_ge(load_w, 7 * 16)

                def evacuate(i, slot):
                    a.wait_ge(turned, i + 1)
                    need(a, h_done[0], i - 1)
                    a.copy(xt[:, slot], ps_t[slot][:]).then_inc(xt_ready, 1)

                def gelu(i, layer):
                    e = expert_of(a, i)
                    a.wait_ge(u_done[layer], i + 1)
                    need(a, (h_done[1], o_done)[layer], i)
                    for k in range(KH):
                        cols = slice(k * P, (k + 1) * P)
                        a.activation(a_[layer][:, cols], ps_u[layer][:, cols], ACT.Gelu,
                                     bias=affine[:, layer, 1, k, at(e)], scale=affine[:, layer, 0, k, at(e)])\
                            .then_inc(a_ready[layer], 1)

                def body(i, slot, has):
                    if has(i - 1):
                        gelu(i - 1, 0)
                    if has(i - 2):
                        gelu(i - 2, 1)
                    if has(i + 1):
                        evacuate(i + 1, 1 - slot)

                pipeline(a, body)

            @block.tensor
            def _(pe):
                pe.wait_ge(load_w, 7 * 16)

                def turn_rows(i, slot):
                    pe.wait_ge(gathered[slot], 8 * (i - slot) + 16)
                    need(pe, xt_ready, i - 1)
                    for k in range(KD):
                        tr = pe.transpose(ps_t[slot][:, k * P:(k + 1) * P], rows[:, slot, k * P:(k + 1) * P], t.ident[:])
                    tr.then_inc(turned, 1)

                def turn(i, layer):
                    pe.wait_ge(v_ready[layer], i + 1)
                    need(pe, a_ready[layer], 2 * i)
                    for k in range(KH):
                        cols = slice(k * P, (k + 1) * P)
                        tr = pe.transpose(ps_u[layer][:, cols], v_[layer][:, cols], t.ident[:])
                    tr.then_inc(u_done[layer], 1)

                def layer1(i, slot):
                    e = expert_of(pe, i)
                    pe.wait_ge(xt_ready, i + 1)
                    need(pe, ln[0], 4 * i - 3)
                    for k in range(KD):
                        mm = pe.matmul(ps_h[0][:, 0:H2], xt[:, slot, k * P:(k + 1) * P], w[0][:, k, at(e)].squeeze(1),
                                       start=k == 0, stop=k == KD - 1)
                    mm.then_inc(h_done[0], 1)

                def layer2(i):
                    e = expert_of(pe, i)
                    pe.wait_ge(a_ready[0], 2 * i + 2)
                    need(pe, ln[1], 4 * i - 3)
                    for k in range(KH):
                        mm = pe.matmul(ps_h[1][:, 0:H2], a_[0][:, k * P:(k + 1) * P], w[1][:, k, at(e)].squeeze(1),
                                       start=k == 0, stop=k == KH - 1)
                    mm.then_inc(h_done[1], 1)

                def layer3(i, slot):
                    e = expert_of(pe, i)
                    pe.wait_ge(a_ready[1], 2 * i + 2)
                    need(pe, o_ready, i - 1)
                    for k in range(KH):
                        mm = pe.matmul(ps_o[slot][:], a_[1][:, k * P:(k + 1) * P], w[2][:, k, at(e)].squeeze(1),
                                       start=k == 0, stop=k == KH - 1)
                    mm.then_inc(o_done, 1)

                def body(i, slot, has):
                    if has(i):
                        layer1(i, slot)
                    if has(i - 1):
                        turn(i - 1, 0)
                    if has(i - 2):
                        turn(i - 2, 1)
                    if has(i + 1):
                        turn_rows(i + 1, 1 - slot)
                    if has(i - 1):
                        layer2(i - 1)
                    if has(i - 2):
                        layer3(i - 2, slot)

                pipeline(pe, body)


def combine(nc, s, t, dram):
    with ExitStack() as ctx:
        sb, ps, sem = allocate(nc, ctx, "combine", t.lasting)
        T = s.tiles
        index = sb("index", [P, 2, 2], I32)
        rows = sb("rows", [P, 2, 2, D])
        x1 = sb("x1", [P, 2, D])
        partial = sb("partial", [P, 2, D])
        out = sb("out", [P, 2, D])
        go = sem("go")
        indexed = sem("indexed")
        gathered = [[sem(f"gathered{i}{n}") for n in range(2)] for i in range(2)]
        load_x1 = [sem(f"load_x1{i}") for i in range(2)]
        half = sem("half")
        done = sem("done")
        stored = [sem(f"stored{i}") for i in range(2)]

        with nc.Block() as block:

            @block.gpsimd
            def _(pool):
                def gather(i, slot, first):
                    if not first:
                        pool.wait_ge(done, i - 1)
                        pool.sem_inc(go, 1)
                    pool.tensor_copy(index[:, slot], t.slot[:, at(i)].squeeze(1)).then_inc(indexed, 1)
                    pool.wait_ge(indexed, i + 1)
                    pool.sem_inc(go, 1)
                    for n in range(2):
                        pool.indirect_dma_start(rows[:, slot, n], None, dram["slots"],
                                                bass.IndirectOffsetOnAxis(ap=index[:, slot, n:n + 1], axis=0))\
                            .then_inc(gathered[slot][n], 16)

                by_pairs(pool, T, gather)

            @block.sync
            def _(sp):
                xv = dram["x1"].rearrange("(t p) d -> t p d", p=P)

                def load(i, slot, first):
                    if not first:
                        sp.wait_ge(half, i - 1)
                    sp.dma_start(x1[:, slot], xv[at(i)].squeeze(0)).then_inc(load_x1[slot], 16)

                by_pairs(sp, T, load)

            @block.vector
            def _(v):
                def add(i, slot, first):
                    v.wait_ge(load_x1[slot], 8 * (i - slot) + 16)
                    v.wait_ge(gathered[slot][0], 8 * (i - slot) + 16)
                    if not first:
                        v.wait_ge(done, i - 1)
                    v.scalar_tensor_tensor(partial[:, slot], rows[:, slot, 0], t.weight[:, at(i), 0], x1[:, slot], ALU.mult,
                                           ALU.add).then_inc(half, 1)
                    v.wait_ge(half, i + 1)
                    v.wait_ge(gathered[slot][1], 8 * (i - slot) + 16)
                    if not first:
                        v.wait_ge(stored[slot], 8 * (i - slot))
                    v.scalar_tensor_tensor(out[:, slot], rows[:, slot, 1], t.weight[:, at(i), 1], partial[:, slot], ALU.mult,
                                           ALU.add).then_inc(done, 1)

                by_pairs(v, T, add)

            @block.scalar
            def _(a):
                ov = dram["out"].rearrange("(t p) d -> t p d", p=P)

                def store(i, slot, first):
                    a.wait_ge(done, i + 1)
                    a.dma_start(ov[at(i)].squeeze(0), out[:, slot]).then_inc(stored[slot], 16)

                by_pairs(a, T, store)
                for slot, n in ((0, T // 2 + 1), (1, T // 2)):
                    a.wait_ge(stored[slot], 16 * n)


def build(nc, dram, sizes):
    s = shapes(*sizes)
    t = lambda: None
    with ExitStack() as ctx:
        t.lasting = ctx
        sb, ps, sem = allocate(nc, ctx, "all")
        t.ident = sb("ident", [P, P])
        t.iota = sb("iota", [P, P], F16)
        t.neg_block = sb("neg_block", [P, s.tiles])
        t.visits = sb("visits", [1, s.supers], I32)
        t.mean = sb("mean", [P, s.tiles])
        t.rstd = sb("rstd", [P, s.tiles])
        t.dis = sb("dis", [P, s.tiles])
        t.dis_table = sb("dis_table", [P, s.tiles])
        t.dis_back = sb("dis_back", [P, s.tiles])
        t.p = sb("p", [P, D])
        t.m = sb("m", [P, KD, D])
        t.gate = sb("gate", [P, s.tiles, GATE])
        t.weight = sb("weight", [P, s.tiles, 2])
        t.slot = sb("slot", [P, s.tiles, 2], I32)
        t.token = sb("token", [P, s.slot_tiles], I32)
        t.expert = sb("expert", [1, s.slot_tiles], I32)
        t.dis_col = lambda i, k: t.dis_table[:, at(i)]
        with ExitStack() as gathering:
            sb, ps, sem = allocate(nc, gathering, "graph", ctx)
            t.acc = sb("acc", [P, s.tiles, D])
            t.src = sb("src", [P, s.chunks], I32)
            t.dst = sb("dst", [P, s.chunks])
            prepare_edges(nc, s, t, dram)
            prepare_table(nc, s, t, dram)
            aggregate(nc, s, t, dram)
            fold(nc, s, t, dram)
            mix(nc, s, t, dram)
        route(nc, s, t, dram)
        experts(nc, s, t, dram)
        combine(nc, s, t, dram)


def kernel(**inputs):
    import concourse.bacc as bacc
    from concourse.bass_utils import run_bass_kernel_spmd as run

    x, src, dst = (np.asarray(inputs[n]) for n in ("x", "src", "dst"))
    sizes = (x.shape[0], src.shape[0])
    s = shapes(*sizes)
    rows = s.tiles * P

    def edges(a):
        padded = np.concatenate([a, np.full(s.chunks * P - a.shape[0], rows - 1, a.dtype)])
        return np.ascontiguousarray(padded.reshape(s.chunks, P).T)

    def by_partition(a):
        experts, rows_in, columns = a.shape
        return np.ascontiguousarray(a.reshape(experts, rows_in // P, P, columns).transpose(2, 1, 0, 3))

    qkv = np.asarray(inputs["L0_mix_W_qkv"])
    cast = np.arange(P, dtype=np.float16)
    arrays = {
        "x": np.concatenate([x, np.zeros((rows - x.shape[0], D), x.dtype)]),
        "src": edges(src),
        "dst": edges(dst),
        "ident": np.eye(P, dtype=np.float32),
        "upper": np.triu(np.ones((P, P), np.float32), 1),
        "iota": np.tile(cast, (P, 1)),
        "w_q": np.ascontiguousarray(qkv[:D]),
        "w_out": np.ascontiguousarray(np.asarray(inputs["L0_mix_W_out"]).T),
        "b_out": np.asarray(inputs["L0_mix_b_out"]),
        "w_gnn": np.ascontiguousarray(np.asarray(inputs["L0_gnn_W"]).T),
        "b_gnn": np.asarray(inputs["L0_gnn_b"]),
        "w_gate1": np.asarray(inputs["L0_ffn_Wg1"]),
        "b_gate1": np.asarray(inputs["L0_ffn_bg1"]),
        "w_gate2": np.ascontiguousarray(np.asarray(inputs["L0_ffn_Wg2"]).T),
        "b_gate2": np.asarray(inputs["L0_ffn_bg2"]),
        "ids": np.ascontiguousarray(np.arange(rows, dtype=np.float32).reshape(s.tiles, P).T),
        **{f"w{n}": by_partition(np.asarray(inputs[f"L0_ffn_W{n}"])) for n in (1, 2, 3)},
        **{f"b{n}": np.asarray(inputs[f"L0_ffn_b{n}"]) for n in (1, 2, 3)},
        "affine": np.ascontiguousarray(np.stack([
            np.stack([np.asarray(inputs[f"L0_ffn_{kind}{n}"]).T.reshape(H2 // P, P, EXPERTS) for kind in ("g", "be")])
            for n in (1, 2)]).transpose(3, 0, 1, 2, 4)),
        "w_kv": np.ascontiguousarray(qkv[D:].T),
        "gamma_k": np.asarray(inputs["L0_mix_gamma_K"]).reshape(D),
        "beta_k": np.asarray(inputs["L0_mix_beta_K"]).reshape(D),
        "gamma_v": np.asarray(inputs["L0_mix_gamma_V"]).reshape(D),
        "beta_v": np.asarray(inputs["L0_mix_beta_V"]).reshape(D),
        "neg_block": np.tile(-P * np.arange(s.tiles, dtype=np.float32), (P, 1)),
    }
    nc = bacc.Bacc("TRN2", target_bir_lowering=False, num_devices=1)
    dram = {n: nc.dram_tensor(f"in_{n}", a.shape, mybir.dt.from_np(a.dtype), kind="ExternalInput").ap()
            for n, a in arrays.items()}
    dram["xt"] = nc.dram_tensor("xt_scratch", [s.tiles, P, D], F32, kind="Internal").ap()
    dram["table"] = nc.dram_tensor("table_scratch", [rows, 2 * D], F16, kind="Internal").ap()
    dram["x1"] = nc.dram_tensor("x1_scratch", [rows, D], F32, kind="Internal").ap()
    dram["tok"] = nc.dram_tensor("tok_scratch", [rows, D], F32, kind="Internal").ap()
    dram["slots"] = nc.dram_tensor("slots_scratch", [s.slot_tiles * P, D], F32, kind="Internal").ap()
    dram["out"] = nc.dram_tensor("out_rows", [rows, D], F32, kind="ExternalOutput").ap()
    build(nc, dram, sizes)
    r = run(nc, [{f"in_{n}": a for n, a in arrays.items()}], core_ids=[0])
    return r.results[0]["out_rows"][0:x.shape[0]]
```

```python
from contextlib import ExitStack

import concourse.bass as bass
import numpy as np
from concourse import mybir

P = 128
D = 512
KD = D // P
HEADS = 8
DH = 64
H2 = 256
EXPERTS = 8
GATE = 16
EPS = 1e-5

F32 = mybir.dt.float32
F16 = mybir.dt.float16
I32 = mybir.dt.int32
ALU = mybir.AluOpType
ACT = mybir.ActivationFunctionType
AX = mybir.AxisListType

SUPER = 8
TABLE_SCALE = 2.0 ** 10
LOW_SCALE = 2.0 ** 11


class Chain:

    def __init__(self, engine, sem, start=0):
        self.engine, self.sem, self.start, self.n = engine, sem, start, 0

    def mark(self, ins):
        ins.then_inc(self.sem, 1)
        self.n += 1

    def wait(self):
        self.engine.wait_ge(self.sem, self.start + self.n)

    def then(self, ins):
        self.mark(ins)
        self.wait()


def shapes(n_nodes, n_edges):
    s = lambda: None
    s.nodes = n_nodes
    s.tiles = -(-n_nodes // P)
    s.last = n_nodes - (s.tiles - 1) * P
    s.per_tile = -(-n_edges // P // s.tiles)
    s.chunks = s.per_tile * s.tiles
    s.supers = s.chunks // SUPER
    s.slot_tiles = (2 * s.tiles * P) // P + EXPERTS
    s.group = 7
    assert s.tiles % s.group == 0 and s.chunks % SUPER == 0 and s.supers == 2 * s.tiles
    assert s.tiles < 64 and s.supers <= P
    return s


def allocate(nc, ctx, stage, lasting=None):
    sb = lambda name, shape, dt=F32: ctx.enter_context(nc.sbuf_tensor(f"{stage}_{name}", shape, dt))
    ps = lambda name, shape, dt=F32: ctx.enter_context(nc.psum_tensor(f"{stage}_{name}", shape, dt))
    sem = lambda name: (lasting or ctx).enter_context(nc.semaphore(f"{stage}_{name}"))
    return sb, ps, sem


def at(i, n=1):
    return bass.ds(i, n)


def need(engine, semaphore, value):
    if not isinstance(value, int) or value > 0:
        engine.wait_ge(semaphore, value)


SLOTS = 4


def by_rounds(engine, tiles, body, slots=SLOTS):
    for i in range(slots):
        body(i, i, 0)
    with engine.Fori(1, tiles // slots) as r:
        for slot in range(slots):
            body(slots * r + slot, slot, r)
    for i in range(tiles // slots * slots, tiles):
        body(i, i % slots, i // slots)


def by_pairs(engine, tiles, body):
    body(0, 0, True)
    body(1, 1, True)
    with engine.Fori(1, tiles // 2) as pair:
        body(2 * pair, 0, False)
        body(2 * pair + 1, 1, False)
    body(tiles - 1, 0, False)


def moments(v, step, stats, mean, var, half):
    step.mark(v.tensor_tensor(mean[:], stats[:, :, 1], stats[:, :, 4], ALU.add))
    step.mark(v.tensor_tensor(half[:], stats[:, :, 1], stats[:, :, 4], ALU.subtract))
    step.then(v.tensor_tensor(var[:], stats[:, :, 2], stats[:, :, 5], ALU.add))
    step.mark(v.tensor_scalar(mean[:], mean[:], 0.5, None, ALU.mult))
    step.mark(v.scalar_tensor_tensor(half[:], half[:], 0.25, half[:], ALU.mult, ALU.mult))
    step.then(v.tensor_scalar(var[:], var[:], 1.0 / D, None, ALU.mult))
    step.then(v.tensor_tensor(var[:], var[:], half[:], ALU.add))


def refine_root(v, step, r, a, spare):
    step.then(v.tensor_tensor(spare, r, r, ALU.mult))
    step.then(v.tensor_tensor(spare, spare, a, ALU.mult))
    step.then(v.tensor_scalar(spare, spare, -0.5, 1.5, ALU.mult, ALU.add))
    step.then(v.tensor_tensor(r, r, spare, ALU.mult))


def prepare_edges(nc, s, t, dram):
    with ExitStack() as ctx:
        sb, ps, sem = allocate(nc, ctx, "prepare_edges", t.lasting)
        T, C, U = s.tiles, s.chunks, s.supers
        low = sb("src_low_int", [P, C], I32)
        high = sb("src_high_int", [P, C], I32)
        dst_int = sb("dst_int", [P, C], I32)
        low_f = sb("src_low", [P, C])
        high_f = sb("src_high", [P, C])
        hot_low = sb("hot_low", [P, 2, s.per_tile, P], F16)
        hot_high = sb("hot_high", [P, 2, s.per_tile, T], F16)
        gap = sb("gap", [P, 2, s.per_tile, T], F16)
        gap2 = sb("gap2", [P, s.per_tile, T], F16)
        stats = sb("stats", [P, T, 6])
        var = sb("var", [P, T])
        half = sb("half", [P, T])
        ends = sb("ends", [U, 2, 2])
        ends_int = sb("ends_int", [U, 2, 2], I32)
        ends_block = sb("ends_block", [U, 2, 2], I32)
        reach = sb("reach", [U, 2, 2])
        span = sb("span", [U, 4])
        alone = sb("alone", [U, 2])
        fields = sb("fields", [U, 1])
        parts = sb("parts", [1, 2, U], I32)
        deg = sb("deg", [P, T])
        root = sb("root", [P, T])
        sd = sb("sd", [P, T])
        upper = sb("upper", [P, P])
        zero = sb("zero", [P, P], F16)
        ps_dst = ps("ps_dst", [P, SUPER * P])
        ps_deg = ps("ps_deg", [P, 512])
        ps_rows = ps("ps_rows", [P, 512])

        load_small = sem("load_small")
        load_x = sem("load_x")
        split = sem("split")
        low_ready = sem("low_ready")
        gap_ready = sem("gap_ready")
        gap_squared = sem("gap_squared")
        high_ready = sem("high_ready")
        hot_used = sem("hot_used")
        dst_turned = sem("dst_turned")
        dve = sem("dve_steps")
        bn = sem("bn_steps")
        rows_in = sem("rows_in")
        rows_out = sem("rows_out")
        zeroed = sem("zeroed")
        deg_done = sem("deg_done")
        roots_in = sem("roots_in")
        roots_out = sem("roots_out")

        with nc.Block() as block:

            @block.sync
            def _(sp):
                sp.dma_start(t.src[:], dram["src"]).then_inc(load_small, 16)
                sp.dma_start(dst_int[:], dram["dst"]).then_inc(load_small, 16)
                sp.dma_start(t.ident[:], dram["ident"]).then_inc(load_small, 16)
                sp.dma_start(upper[:], dram["upper"]).then_inc(load_small, 16)
                sp.dma_start(t.iota[:], dram["iota"]).then_inc(load_small, 16)
                sp.dma_start(t.neg_block[:], dram["neg_block"]).then_inc(load_small, 16)
                xv = dram["x"].rearrange("(t p) d -> p t d", p=P)
                def load(g):
                    sp.dma_start(t.acc[:, at(g * s.group, s.group), :],
                                 xv[:, at(g * s.group, s.group), :]).then_inc(load_x, 16)

                load(0)
                with sp.Fori(1, T // s.group) as g:
                    sp.wait_ge(load_x, g * 16)
                    load(g)

            @block.gpsimd
            def _(pool):
                pool.memset(zero[:], 0.0).then_inc(zeroed, 1)
                pool.wait_ge(load_small, 96)
                pool.wait_ge(split, 4)
                shape = [P, s.per_tile, T]
                blocks = t.iota[:, 0:T].unsqueeze(1).to_broadcast(shape)

                def gaps(i, slot, first):
                    if not first:
                        pool.wait_ge(gap_squared, i - 1)
                    pool.tensor_tensor(gap[:, slot], high_f[:, at(i * s.per_tile, s.per_tile)].unsqueeze(2).to_broadcast(shape),
                                       blocks, ALU.subtract).then_inc(gap_ready, 1)

                gaps(0, 0, True)
                gaps(1, 1, True)
                with pool.Fori(1, T // 2) as pair:
                    i = 2 * pair
                    gaps(i, 0, False)
                    gaps(i + 1, 1, False)
                gaps(T - 1, 0, False)

            @block.vector
            def _(v):
                v.wait_ge(load_small, 96)
                v.tensor_copy(t.dst[:], dst_int[:]).then_inc(split, 1)
                v.tensor_single_scalar(high[:], t.src[:], 7, op=ALU.logical_shift_right).then_inc(split, 1)
                v.tensor_single_scalar(low[:], t.src[:], P - 1, op=ALU.bitwise_and).then_inc(split, 1)
                v.wait_ge(split, 3)
                v.tensor_copy(high_f[:], high[:]).then_inc(split, 1)
                v.tensor_copy(low_f[:], low[:]).then_inc(split, 1)
                v.wait_ge(split, 5)

                step = Chain(v, dve)
                v.wait_ge(dst_turned, 1)
                halves = ps_dst[0:U, :].rearrange("u (h c) -> u h c", h=2)
                step.mark(v.tensor_reduce(ends[:, 0], halves, AX.X, ALU.max))
                step.then(v.tensor_reduce(ends[:, 1], halves, AX.X, ALU.min))
                step.then(v.tensor_copy(ends_int[:], ends[:]))
                step.then(v.tensor_single_scalar(ends_block[:], ends_int[:], 7, op=ALU.logical_shift_right))
                step.then(v.tensor_copy(reach[:], ends_block[:]))
                step.mark(v.tensor_tensor(span[:, 0:1], reach[:, 0, 0:1], reach[:, 0, 1:2], ALU.max))
                step.then(v.tensor_tensor(span[:, 1:2], reach[:, 1, 0:1], reach[:, 1, 1:2], ALU.min))
                step.mark(v.tensor_tensor(alone[:, 0:1], reach[:, 1, 1:2], span[:, 1:2], ALU.is_gt))
                step.mark(v.tensor_tensor(alone[:, 1:2], reach[:, 0, 0:1], span[:, 1:2], ALU.is_le))
                step.mark(v.tensor_scalar(span[:, 3:4], span[:, 1:2], -1.0, float(T), ALU.mult, ALU.add))
                step.then(v.tensor_tensor(span[:, 2:3], span[:, 0:1], span[:, 1:2], ALU.subtract))
                step.then(v.scalar_tensor_tensor(fields[:], span[:, 2:3], 64.0, span[:, 1:2], ALU.mult, ALU.add))
                for n in range(2):
                    step.then(v.scalar_tensor_tensor(fields[:], alone[:, n:n + 1], 4096.0 * (1 + n), fields[:], ALU.mult, ALU.add))
                v.sem_inc(rows_in, 1)
                v.wait_ge(rows_out, 1)
                step.then(v.tensor_copy(parts[:].rearrange("p n u -> p (n u)"), ps_rows[0:1, 0:2 * U]))
                step.then(v.tensor_single_scalar(parts[:, 1], parts[:, 1], 14, op=ALU.logical_shift_left))
                v.tensor_tensor(t.visits[:], parts[:, 0], parts[:, 1], ALU.bitwise_or)

                def low_hots(i, slot, first):
                    if not first:
                        v.wait_ge(hot_used, i - 1)
                    shape = [P, s.per_tile, P]
                    v.tensor_tensor(hot_low[:, slot], t.iota[:].unsqueeze(1).to_broadcast(shape),
                                    low_f[:, at(i * s.per_tile, s.per_tile)].unsqueeze(2).to_broadcast(shape),
                                    ALU.is_equal).then_inc(low_ready, 1)

                low_hots(0, 0, True)
                low_hots(1, 1, True)
                with v.Fori(1, T // 2) as pair:
                    i = 2 * pair
                    low_hots(i, 0, False)
                    low_hots(i + 1, 1, False)
                low_hots(T - 1, 0, False)

                with v.Fori(0, T // s.group) as g:
                    v.wait_ge(load_x, g * 16 + 16)
                    for j in range(s.group):
                        v.bn_stats(stats[:, at(g * s.group + j)].squeeze(1),
                                   t.acc[:, at(g * s.group + j)].squeeze(1)).then_inc(bn, 1)
                v.wait_ge(bn, T)
                step = Chain(v, dve, step.n)
                moments(v, step, stats, t.mean, var, half)
                step.then(v.tensor_scalar(var[:], var[:], EPS, None, ALU.add))
                v.wait_ge(deg_done, 1)
                step.then(v.tensor_scalar(deg[:], ps_deg[:, 0:T], 1.0, None, ALU.add))
                v.sem_inc(roots_in, 1)
                v.wait_ge(roots_out, 2)
                step.mark(v.reciprocal(t.rstd[:], sd[:]))
                step.then(v.reciprocal(t.dis[:], root[:]))
                refine_root(v, step, t.rstd[:], var[:], sd[:])
                refine_root(v, step, t.dis[:], deg[:], root[:])
                v.tensor_scalar(t.dis_table[:], t.dis[:], TABLE_SCALE, None, ALU.mult)
                v.tensor_scalar(t.dis_back[:], t.dis[:], 1.0 / TABLE_SCALE, None, ALU.mult)

            @block.scalar
            def _(a):
                def high_hots(i, slot, first):
                    a.wait_ge(gap_ready, i + 1)
                    if not (first and slot == 0):
                        a.wait_ge(high_ready, i)
                    a.activation(gap2[:], gap[:, slot], ACT.Square).then_inc(gap_squared, 1)
                    a.wait_ge(gap_squared, i + 1)
                    if not first:
                        a.wait_ge(hot_used, i - 1)
                    a.activation(hot_high[:, slot], gap2[:], ACT.Relu, bias=1.0, scale=-1.0).then_inc(high_ready, 1)

                high_hots(0, 0, True)
                high_hots(1, 1, True)
                with a.Fori(1, T // 2) as pair:
                    i = 2 * pair
                    high_hots(i, 0, False)
                    high_hots(i + 1, 1, False)
                high_hots(T - 1, 0, False)
                a.wait_ge(roots_in, 1)
                a.activation(root[:], deg[:], ACT.Sqrt).then_inc(roots_out, 1)
                a.activation(sd[:], var[:], ACT.Sqrt).then_inc(roots_out, 1)

            @block.tensor
            def _(pe):
                pe.wait_ge(load_small, 96)
                pe.wait_ge(split, 1)
                for k in range(SUPER):
                    turn = pe.transpose(ps_dst[0:U, k * P:(k + 1) * P], t.dst[:, k::SUPER], t.ident[:])
                turn.then_inc(dst_turned, 1)
                pe.wait_ge(rows_in, 1)
                pe.matmul(ps_rows[0:1, 0:U], fields[:], t.ident[0:U, 0:U], start=True, stop=True)
                pe.matmul(ps_rows[0:1, U:2 * U], span[:, 3:4], t.ident[0:U, 0:U], start=True, stop=False)
                mm = pe.matmul(ps_rows[0:1, U:2 * U], span[:, 2:3], upper[0:U, 0:U], start=False, stop=True)
                mm.then_inc(rows_out, 1)
                pe.wait_ge(zeroed, 1)
                pe.matmul(ps_deg[:, 0:T], zero[:], t.iota[:, 0:T], start=True, stop=True)

                def count(i, slot):
                    pe.wait_ge(high_ready, i + 1)
                    pe.wait_ge(low_ready, i + 1)
                    for c in range(s.per_tile):
                        mm = pe.matmul(ps_deg[:, 0:T], hot_low[:, slot, c, :], hot_high[:, slot, c, :],
                                       start=False, stop=True, skip_group_check=True)
                    mm.then_inc(hot_used, 1)

                with pe.Fori(0, T // 2) as pair:
                    i = 2 * pair
                    count(i, 0)
                    count(i + 1, 1)
                count(T - 1, 0)
                pe.wait_ge(hot_used, T)
                pe.sem_inc(deg_done, 1)


def prepare_table(nc, s, t, dram):
    with ExitStack() as ctx:
        sb, ps, sem = allocate(nc, ctx, "prepare_table", t.lasting)
        T = s.tiles
        xn = sb("xn", [P, SLOTS, D])
        xt = sb("xt", [P, SLOTS, D])
        rest = sb("rest", [P, SLOTS, D])
        halves = sb("halves", [P, SLOTS, 2 * D], F16)
        ps_xt = [ps(f"ps_xt{i}", [P, D]) for i in range(SLOTS)]
        xn_ready = sem("xn_ready")
        turned = sem("turned")
        xt_ready = sem("xt_ready")
        scaled = sem("scaled")
        high_ready = sem("high_ready")
        rest_ready = sem("rest_ready")
        low_ready = sem("low_ready")
        go = sem("go")
        xt_stored = [sem(f"xt_stored{i}") for i in range(SLOTS)]
        table_stored = [sem(f"table_stored{i}") for i in range(SLOTS)]
        table = dram["table"].rearrange("(t p) d -> t p d", p=P)

        with nc.Block() as block:

            @block.vector
            def _(v):
                def normalize(i, slot):
                    need(v, turned, i - SLOTS + 1)
                    need(v, scaled, i - SLOTS + 1)
                    v.tensor_scalar(xn[:, slot], t.acc[:, at(i), :].squeeze(1), t.mean[:, at(i)], t.rstd[:, at(i)],
                                    ALU.subtract, ALU.mult).then_inc(xn_ready, 1)

                def halve(i, slot, r):
                    v.wait_ge(scaled, i + 1)
                    need(v, table_stored[slot], 16 * r)
                    v.tensor_scalar(halves[:, slot, 0:D], t.acc[:, at(i), :].squeeze(1), 1.0, None,
                                    ALU.mult).then_inc(high_ready, 1)
                    v.wait_ge(high_ready, i + 1)
                    need(v, low_ready, i - SLOTS + 1)
                    v.tensor_tensor(rest[:, slot], t.acc[:, at(i), :].squeeze(1), halves[:, slot, 0:D],
                                    ALU.subtract).then_inc(rest_ready, 1)

                def body(i, slot, r):
                    if not isinstance(i, int) or i + 1 < T:
                        normalize(i + 1, (slot + 1) % SLOTS)
                    halve(i, slot, r)

                normalize(0, 0)
                by_rounds(v, T, body)

            @block.gpsimd
            def _(pool):
                def low(i, slot, r):
                    pool.wait_ge(rest_ready, i + 1)
                    need(pool, table_stored[slot], 16 * r)
                    pool.sem_inc(go, 1)
                    pool.tensor_scalar(halves[:, slot, D:2 * D], rest[:, slot], LOW_SCALE, 1.0, ALU.mult,
                                       ALU.mult).then_inc(low_ready, 1)

                by_rounds(pool, T, low)

            @block.scalar
            def _(a):
                def evacuate(i, slot, r):
                    a.wait_ge(xn_ready, i + 1)
                    a.activation(t.acc[:, at(i), :].squeeze(1), xn[:, slot], ACT.Identity,
                                 bias=t.dis_table[:, at(i)], scale=t.dis_table[:, at(i)]).then_inc(scaled, 1)
                    a.wait_ge(turned, i + 1)
                    need(a, xt_stored[slot], 16 * r)
                    a.copy(xt[:, slot], ps_xt[slot][:]).then_inc(xt_ready, 1)

                by_rounds(a, T, evacuate)

            @block.tensor
            def _(pe):
                def turn(i, slot, r):
                    pe.wait_ge(xn_ready, i + 1)
                    need(pe, xt_ready, i - SLOTS + 1)
                    for k in range(KD):
                        tr = pe.transpose(ps_xt[slot][:, k * P:(k + 1) * P], xn[:, slot, k * P:(k + 1) * P], t.ident[:])
                    tr.then_inc(turned, 1)

                by_rounds(pe, T, turn)

            @block.sync
            def _(sp):
                def store(i, slot, r):
                    sp.wait_ge(xt_ready, i + 1)
                    sp.dma_start(dram["xt"][at(i)].squeeze(0), xt[:, slot]).then_inc(xt_stored[slot], 16)
                    sp.wait_ge(low_ready, i + 1)
                    sp.dma_start(table[at(i)].squeeze(0), halves[:, slot]).then_inc(table_stored[slot], 16)

                by_rounds(sp, T, store)
                for slot in range(SLOTS):
                    for stored in (xt_stored, table_stored):
                        sp.wait_ge(stored[slot], 16 * len(range(slot, T, SLOTS)))


def aggregate(nc, s, t, dram):
    with ExitStack() as ctx:
        sb, ps, sem = allocate(nc, ctx, "aggregate", t.lasting)
        T, U = s.tiles, s.supers
        RING = 2 * SUPER
        rows = sb("rows", [P, RING, 2 * D], F16)
        index = sb("index", [P, 2, SUPER], I32)
        offsets = sb("offsets", [P, 3, SUPER])
        hot = sb("hot", [P, 3, SUPER, P], F16)
        hot_small = sb("hot_small", [P, 3, SUPER, P], F16)
        zero = sb("zero", [P, P])
        w = sb("w_kv", [P, KD, 2 * D])
        sums = sb("w_sums", [P, KD, 2 * HEADS])
        affine = sb("affine", [P, 2, 2 * D])
        xt = sb("xt_kv", [P, 2, D])
        square = sb("square", [P, 2, 2 * D])
        var = sb("var_kv", [P, 2 * HEADS])
        rstd = sb("rstd_kv", [P, 2 * HEADS])
        spare = sb("spare_kv", [P, 2 * HEADS])
        kv = sb("kv", [P, 2, 2 * D])
        ps_sum = [ps("ps_sum0", [P, D]), ps("ps_sum1", [P, D]), ps("ps_sum2", [P, D])]
        ps_kv = [ps("ps_kv0", [P, 2 * D]), ps("ps_kv1", [P, 2 * D])]
        ps_p = ps("ps_p", [P, D])

        gathered = [sem(f"gathered{i}") for i in range(RING // 2)]
        index_ready = sem("index_ready")
        go = sem("go")
        super_used = sem("super_used")
        placed, further_placed = sem("placed"), sem("further_placed")
        hot_ready, further_hot = sem("hot_ready"), sem("further_hot")
        small_ready, further_small = sem("small_ready"), sem("further_small")
        summed, further_summed = sem("summed"), sem("further_summed")
        added, further_added = sem("added"), sem("further_added")
        load_w = sem("load_w")
        w_ready = sem("w_ready")
        zeroed = sem("zeroed")
        loaded_xt = [sem(f"loaded_xt{i}") for i in range(2)]
        projected = sem("projected")
        squared = sem("squared")
        var_ready = sem("var_ready")
        rooted = sem("rooted")
        kv_steps = sem("kv_steps")
        kv_scaled = sem("kv_scaled")
        kv_ready = sem("kv_ready")
        correlated = sem("correlated")
        w_steps = sem("w_steps")

        def span_of(engine, u, halves=False):
            packed = engine.value_load(t.visits[0:1, at(u)], min_val=0, max_val=(T * U + T) * 16384 + 16383)
            first = (packed & 63).with_bounds(min_val=0, max_val=T - 1)
            end = (first + ((packed >> 6) & 63) + 1).with_bounds(min_val=1, max_val=T)
            offset = (packed >> 14).with_bounds(min_val=1, max_val=T * U + T)
            if halves:
                return first, end, offset, (packed >> 12) & 1, (packed >> 13) & 1
            return first, end, offset

        def pipeline(engine, body):
            has = lambda i: not isinstance(i, int) or 0 <= i < T
            for i in range(4):
                body(i, i % 2, has)
            with engine.Fori(2, (T - 1) // 2) as pair:
                body(2 * pair, 0, has)
                body(2 * pair + 1, 1, has)
            for i in range(T - 1, T + 3):
                body(i, i % 2, has)

        with nc.Block() as block:

            @block.sync
            def _(sp):
                sp.dma_start(w[:], dram["w_kv"].rearrange("(k p) n -> p k n", p=P)).then_inc(load_w, 16)
                for n, name in enumerate(("gamma_k", "gamma_v", "beta_k", "beta_v")):
                    half = slice(n % 2 * D, n % 2 * D + D)
                    sp.dma_start(affine[:, n // 2, half], dram[name].partition_broadcast(P)).then_inc(load_w, 16)

                def load(i, slot, first):
                    if not first:
                        sp.wait_ge(projected, 2 * i - 2)
                    sp.dma_start(xt[:, slot], dram["xt"][at(i)].squeeze(0)).then_inc(loaded_xt[slot], 16)

                load(0, 0, True)
                load(1, 1, True)
                with sp.Fori(1, T // 2) as pair:
                    load(2 * pair, 0, False)
                    load(2 * pair + 1, 1, False)
                load(T - 1, 0, False)

            @block.gpsimd
            def _(pool):
                pool.memset(zero[:], 0.0).then_inc(zeroed, 1)

                def gather(u, half, first):
                    if not first:
                        pool.wait_ge(super_used, u - 1)
                        pool.sem_inc(go, 1)
                    pool.tensor_copy(index[:, half], t.src[:, at(u * SUPER, SUPER)]).then_inc(index_ready, 1)
                    pool.wait_ge(index_ready, u + 1)
                    pool.sem_inc(go, 1)
                    for k in range(SUPER):
                        slot = half * SUPER + k
                        pool.indirect_dma_start(
                            rows[:, slot], None, dram["table"],
                            bass.IndirectOffsetOnAxis(ap=index[:, half, k:k + 1], axis=0)).then_inc(gathered[slot // 2], 16)

                gather(0, 0, True)
                gather(1, 1, True)
                with pool.Fori(1, T) as i:
                    gather(2 * i, 0, False)
                    gather(2 * i + 1, 1, False)

            @block.vector
            def _(v):
                v.sem_inc(further_placed, T + 1)
                v.sem_inc(further_hot, T + 1)
                v.sem_inc(further_added, T + 1)
                v.wait_ge(load_w, 80)
                step = Chain(v, w_steps)
                grouped = w[:].rearrange("p k (h e) -> p k h e", e=DH)
                step.then(v.tensor_reduce(sums[:], grouped, AX.X, ALU.add))
                step.then(v.tensor_scalar(sums[:], sums[:], 1.0 / DH, None, ALU.mult))
                v.tensor_tensor(grouped, grouped, sums[:].unsqueeze(3).to_broadcast([P, KD, 2 * HEADS, DH]),
                                ALU.subtract).then_inc(w_ready, 1)

                def make_hots(u, b, buffer, done, ready, n):
                    v.tensor_scalar(offsets[:, buffer], t.dst[:, at(u * SUPER, SUPER)], t.neg_block[:, at(b)], None,
                                    ALU.add).then_inc(done, 1)
                    v.wait_ge(done, n + 1)
                    shape = [P, SUPER, P]
                    v.tensor_tensor(hot[:, buffer], t.iota[:].unsqueeze(1).to_broadcast(shape),
                                    offsets[:, buffer].unsqueeze(2).to_broadcast(shape), ALU.is_equal).then_inc(ready, 1)

                def first_hots(u, parity, opening=False):
                    first, _, _ = span_of(v, u)
                    if not opening:
                        v.wait_ge(summed, 2 * u - 2)
                    make_hots(u, first, parity, placed, hot_ready, u)

                def further_hots(u, b, offset):
                    n = offset + b
                    v.wait_ge(further_summed, 2 * n)
                    make_hots(u, b, 2, further_placed, further_hot, n)

                def add_visits(u, parity, next_first):
                    first, end, offset = span_of(v, u)
                    with v.If(first + 1 < end):
                        further_hots(u, (first + 1).with_bounds(min_val=1, max_val=T - 1), offset)
                    if next_first:
                        first_hots(u + 1, 1 - parity, isinstance(u, int) and u == 0)
                    acc = t.acc[:, at(first)].squeeze(1)
                    v.wait_ge(summed, 2 * u + 2)
                    v.wait_ge(further_added, offset + first + 1)
                    if not isinstance(u, int) or u > 0:
                        v.wait_ge(added, u)
                    v.tensor_tensor(acc, ps_sum[parity][:], acc, ALU.add).then_inc(added, 1)
                    with v.If(first + 1 < end), v.Fori(first + 1, end) as b:
                        n = offset + b
                        acc = t.acc[:, at(b)].squeeze(1)
                        v.wait_ge(further_summed, 2 * n + 2)
                        v.wait_ge(further_added, n)
                        v.wait_ge(added, u + 1)
                        v.tensor_tensor(acc, ps_sum[2][:], acc, ALU.add).then_inc(further_added, 1)
                        with v.If(b + 1 < end):
                            further_hots(u, (b + 1).with_bounds(min_val=1, max_val=T - 1), offset)

                def statistics(i, slot):
                    step = Chain(v, kv_steps, 6 * i)
                    v.wait_ge(squared, 2 * i + 2)
                    need(v, kv_steps, 6 * i)
                    need(v, rooted, i)
                    step.then(v.tensor_reduce(var[:], square[:, slot].rearrange("p (h e) -> p h e", e=DH), AX.X, ALU.add))
                    v.tensor_scalar(var[:], var[:], 1.0 / DH, EPS, ALU.mult, ALU.add).then_inc(var_ready, 1)
                    v.wait_ge(var_ready, i + 1)
                    v.wait_ge(rooted, i + 1)
                    step.then(v.reciprocal(rstd[:], rstd[:]))
                    refine_root(v, step, rstd[:], var[:], spare[:])

                def gain_and_bias(i, slot):
                    v.wait_ge(kv_scaled, i + 1)
                    v.tensor_tensor(kv[:, slot], kv[:, slot], affine[:, 0], ALU.mult).then_inc(kv_ready, 1)
                    v.wait_ge(kv_ready, 2 * i + 1)
                    v.tensor_tensor(kv[:, slot], kv[:, slot], affine[:, 1], ALU.add).then_inc(kv_ready, 1)

                def body(i, slot, has):
                    if has(i):
                        add_visits(2 * i, 0, True)
                    if has(i - 1):
                        statistics(i - 1, 1 - slot)
                        v.sem_inc(go, 1)
                    if has(i):
                        add_visits(2 * i + 1, 1, has(i + 1))
                    if has(i - 2):
                        gain_and_bias(i - 2, slot)

                first_hots(0, 0, True)
                pipeline(v, body)
                v.memset(t.p[:], 0.0).then_inc(zeroed, 1)
                v.wait_ge(zeroed, 2)
                v.wait_ge(correlated, T)
                for head in range(HEADS):
                    rows = slice(head % 2 * DH, head % 2 * DH + DH)
                    cols = slice(head * DH, head * DH + DH)
                    v.tensor_scalar(t.p[rows, cols], ps_p[rows, cols], 1.0 / s.nodes, None, ALU.mult)

            @block.scalar
            def _(a):
                def first_small(u, parity):
                    a.wait_ge(hot_ready, u + 1)
                    a.activation(hot_small[:, parity], hot[:, parity], ACT.Copy, scale=1.0 / LOW_SCALE).then_inc(small_ready, 1)

                def further_smalls(u):
                    first, end, offset = span_of(a, u)
                    with a.If(first + 1 < end), a.Fori(first + 1, end) as b:
                        a.wait_ge(further_hot, offset + b + 1)
                        a.sem_inc(go, 1)
                        a.activation(hot_small[:, 2], hot[:, 2], ACT.Copy, scale=1.0 / LOW_SCALE).then_inc(further_small, 1)

                def squares(i, slot, kind):
                    cols = slice(kind * D, kind * D + D)
                    a.wait_ge(projected, 2 * i + kind + 1)
                    need(a, var_ready, i - 1)
                    a.activation(square[:, slot, cols], ps_kv[slot][:, cols], ACT.Square).then_inc(squared, 1)

                def root(i):
                    a.wait_ge(var_ready, i + 1)
                    need(a, kv_scaled, i)
                    a.activation(rstd[:], var[:], ACT.Sqrt).then_inc(rooted, 1)

                def scale(i, slot):
                    a.wait_ge(kv_steps, 6 * i + 6)
                    need(a, correlated, i - 1)
                    for head in range(2 * HEADS):
                        cols = slice(head * DH, head * DH + DH)
                        scaled = a.activation(kv[:, slot, cols], ps_kv[slot][:, cols], ACT.Copy, scale=rstd[:, head:head + 1])
                    scaled.then_inc(kv_scaled, 1)

                def body(i, slot, has):
                    if has(i):
                        further_smalls(2 * i)
                        first_small(2 * i + 1, 1)
                    if has(i - 1):
                        root(i - 1)
                    if has(i):
                        squares(i, slot, 0)
                        further_smalls(2 * i + 1)
                    if has(i + 1):
                        first_small(2 * i + 2, 0)
                    if has(i - 1):
                        scale(i - 1, 1 - slot)
                    if has(i):
                        squares(i, slot, 1)

                a.sem_inc(further_small, T + 1)
                first_small(0, 0)
                pipeline(a, body)

            @block.tensor
            def _(pe):
                def products(bank, buffer, ring, ready, small, n, done, always, skip):
                    def chunks(half, opening, closing):
                        for part, hots in enumerate((hot, hot_small)):
                            if opening:
                                pe.wait_ge((ready, small)[part], n + 1)
                            for k in range(SUPER // 2):
                                chunk = half * SUPER // 2 + k
                                mm = pe.matmul(bank[:], hots[:, buffer, chunk],
                                               rows[:, ring * SUPER + chunk, part * D:(part + 1) * D],
                                               start=opening and part == 0 and k == 0, stop=True, skip_group_check=True)
                        mm.then_inc(done, 1)

                    chunks(always, True, False)
                    with pe.If(skip < 1):
                        chunks(1 - always, False, True)
                    with pe.If(skip > 0):
                        pe.sem_inc(done, 1)

                def visits(u, i, ring):
                    first, end, offset, alone, within = span_of(pe, u, True)
                    for k in range(0, SUPER, 2):
                        pe.wait_ge(gathered[(ring * SUPER + k) // 2], (i + 1) * 32)
                    if not isinstance(u, int) or u > 1:
                        pe.wait_ge(added, u - 1)
                    products(ps_sum[ring], ring, ring, hot_ready, small_ready, u, summed, 0, alone)
                    with pe.If(first + 1 < end), pe.Fori(first + 1, end) as b:
                        n = offset + b
                        pe.wait_ge(further_added, n)
                        products(ps_sum[2], 2, ring, further_hot, further_small, n, further_summed, 1, within)
                    pe.wait_ge(summed, 2 * u + 2)
                    pe.wait_ge(further_summed, 2 * (offset + end))
                    pe.sem_inc(super_used, 1)

                def project(i, slot, kind):
                    if kind == 0:
                        pe.wait_ge(loaded_xt[slot], 8 * (i - slot) + 16)
                        need(pe, kv_scaled, i - 1)
                    cols = slice(kind * D, kind * D + D)
                    for k in range(KD):
                        mm = pe.matmul(ps_kv[slot][:, cols], xt[:, slot, k * P:(k + 1) * P], w[:, k, cols],
                                       start=k == 0, stop=k == KD - 1)
                    mm.then_inc(projected, 1)

                def correlate(i, slot, n=P):
                    pe.wait_ge(kv_ready, 2 * i + 2)
                    for pair in range(HEADS // 2):
                        cols = slice(pair * P, (pair + 1) * P)
                        values = slice(D + pair * P, D + (pair + 1) * P)
                        mm = pe.matmul(ps_p[:, cols], kv[0:n, slot, values], kv[0:n, slot, cols],
                                       start=False, stop=True, skip_group_check=True)
                    mm.then_inc(correlated, 1)

                def body(i, slot, has):
                    for half in range(2):
                        if has(i):
                            visits(2 * i + half, i, half)
                            project(i, slot, half)
                        if half == 0 and has(i - 3):
                            correlate(i - 3, 1 - slot, s.last if isinstance(i, int) and i - 3 == T - 1 else P)

                pe.sem_inc(further_summed, 2 * T + 2)
                pe.wait_ge(zeroed, 1)
                pe.wait_ge(w_ready, 1)
                pe.matmul(ps_p[:], zero[:], w[:, 0, 0:D], start=True, stop=True)
                pipeline(pe, body)


def fold(nc, s, t, dram):
    with ExitStack() as ctx:
        sb, ps, sem = allocate(nc, ctx, "fold", t.lasting)
        wq = sb("wq", [P, KD, D])
        wo = sb("wo", [P, KD, D])
        pw = sb("pw", [P, KD, D])
        ps_pw = [ps(f"ps_pw{i}", [P, D]) for i in range(KD)]
        ps_m = [ps(f"ps_m{i}", [P, D]) for i in range(KD)]
        loaded = sem("loaded")
        pw_done = sem("pw_done")
        pw_ready = sem("pw_ready")
        m_done = sem("m_done")

        with nc.Block() as block:

            @block.sync
            def _(sp):
                sp.dma_start(wo[:], dram["w_out"].rearrange("(k p) n -> p k n", p=P)).then_inc(loaded, 16)
                sp.dma_start(wq[:], dram["w_q"].rearrange("(k p) n -> p k n", p=P)).then_inc(loaded, 16)

            @block.tensor
            def _(pe):
                pe.wait_ge(loaded, 32)
                for j in range(KD):
                    pe.matmul(ps_pw[j][:], t.p[:, j * P:(j + 1) * P], wo[:, j], start=True, stop=True).then_inc(pw_done, 1)
                for m in range(KD):
                    for j in range(KD):
                        if m == 0:
                            pe.wait_ge(pw_ready, j + 1)
                        mm = pe.matmul(ps_m[m][:], wq[:, j, m * P:(m + 1) * P], pw[:, j], start=j == 0, stop=j == KD - 1)
                    mm.then_inc(m_done, 1)

            @block.vector
            def _(v):
                for j in range(KD):
                    v.wait_ge(pw_done, j + 1)
                    v.tensor_copy(pw[:, j], ps_pw[j][:]).then_inc(pw_ready, 1)
                for m in range(KD):
                    v.wait_ge(m_done, m + 1)
                    v.tensor_copy(t.m[:, m], ps_m[m][:])


def mix(nc, s, t, dram):
    with ExitStack() as ctx:
        sb, ps, sem = allocate(nc, ctx, "mix", t.lasting)
        T = s.tiles
        wg = sb("w_gnn", [P, KD, D])
        w_gate = sb("w_gate", [P, KD, GATE])
        b_gate = sb("b_gate", [P, GATE])
        b_gnn = sb("b_gnn", [P, D])
        b_out = sb("b_out", [P, D])
        power = sb("power", [P, 1])
        x = sb("x", [P, 2, D])
        xt = sb("xt", [P, 2, D])
        y = sb("y", [P, 2, D])
        yt = sb("yt", [P, 2, D])
        part = sb("part", [P, D])
        tok = sb("tok", [P, 2, D])
        tt = sb("tt", [P, 2, D])
        stats_y = sb("stats_y", [P, 6])
        stats_x1 = sb("stats_x1", [P, 6])
        moment_y = sb("moment_y", [P, 2, 2])
        moment_x1 = sb("moment_x1", [P, 2, 2])
        weight = sb("weight", [P, 2])
        var = sb("var", [P, 2])
        rstd = sb("rstd", [P, 2])
        ps_yt = ps("ps_yt", [P, D])
        ps_tt = ps("ps_tt", [P, D])
        ps_g = [ps(f"ps_g{i}", [P, D]) for i in range(2)]
        ps_a = [ps(f"ps_a{i}", [P, D]) for i in range(2)]
        ps_gate = [ps(f"ps_gate{i}", [P, D]) for i in range(2)]
        load_w = sem("load_w")
        load_x = [sem(f"load_x{i}") for i in range(2)]
        load_xt = [sem(f"load_xt{i}") for i in range(2)]
        powered = sem("powered")
        go = sem("go")
        x_biased = sem("x_biased")
        centring = sem("centring")
        y_ready = sem("y_ready")
        y_turned = sem("y_turned")
        yt_ready = sem("yt_ready")
        g_done = sem("g_done")
        a_done = sem("a_done")
        sums = sem("sums")
        ln = sem("ln")
        rooted = sem("rooted")
        tok_ready = sem("tok_ready")
        tok_turned = sem("tok_turned")
        tt_ready = sem("tt_ready")
        gated = sem("gated")
        gate_read = sem("gate_read")
        tok_stored = [sem(f"tok_stored{i}") for i in range(2)]
        x1_stored = sem("x1_stored")

        def pipeline(engine, body):
            has = lambda i: not isinstance(i, int) or 0 <= i < T
            for i in range(-1, 4):
                body(i, i % 2, has)
            with engine.Fori(2, (T - 1) // 2) as pair:
                body(2 * pair, 0, has)
                body(2 * pair + 1, 1, has)
            for i in range(T - 1, T + 3):
                body(i, i % 2, has)

        with nc.Block() as block:

            @block.sync
            def _(sp):
                sp.dma_start(wg[:], dram["w_gnn"].rearrange("(k p) n -> p k n", p=P)).then_inc(load_w, 16)
                sp.dma_start(b_gnn[:], dram["b_gnn"].partition_broadcast(P)).then_inc(load_w, 16)
                sp.dma_start(b_out[:], dram["b_out"].partition_broadcast(P)).then_inc(load_w, 16)
                sp.dma_start(w_gate[:], dram["w_gate1"].rearrange("(k p) n -> p k n", p=P)).then_inc(load_w, 16)
                sp.dma_start(b_gate[:], dram["b_gate1"].partition_broadcast(P)).then_inc(load_w, 16)
                xv = dram["x"].rearrange("(t p) d -> t p d", p=P)

                def load(i, slot, first):
                    if not first:
                        sp.wait_ge(a_done, i - 1)
                    sp.dma_start(xt[:, slot], dram["xt"][at(i)].squeeze(0)).then_inc(load_xt[slot], 16)
                    if not first:
                        sp.wait_ge(sums, 3 * i - 3)
                    sp.dma_start(x[:, slot], xv[at(i)].squeeze(0)).then_inc(load_x[slot], 16)

                by_pairs(sp, T, load)

            @block.gpsimd
            def _(pool):
                pool.memset(power[:], -0.5).then_inc(powered, 1)
                pool.wait_ge(powered, 1)
                pool.wait_ge(load_w, 5 * 16)

                def body(i, slot, has):
                    if has(i):
                        pool.wait_ge(load_x[slot], 8 * (i - slot) + 16)
                        pool.tensor_tensor(x[:, slot], x[:, slot], b_out[:], ALU.add).then_inc(x_biased, 1)
                    if has(i - 1):
                        last = slice(1 - slot, 2 - slot)
                        pool.wait_ge(ln, 3 * i)
                        pool.tensor_tensor(rstd[:, last], var[:, last], power[:], ALU.pow).then_inc(rooted, 1)

                pipeline(pool, body)

            @block.vector
            def _(v):
                v.wait_ge(load_w, 5 * 16)

                def centre(i, slot):
                    acc = t.acc[:, at(i)].squeeze(1)
                    need(v, centring, 3 * i)
                    need(v, sums, 3 * i - 3)
                    v.sem_inc(go, 1)
                    v.bn_stats(stats_y[:], acc).then_inc(centring, 1)
                    v.wait_ge(centring, 3 * i + 1)
                    need(v, y_ready, i - 1)
                    v.sem_inc(go, 1)
                    v.bn_aggr(moment_y[:, slot], stats_y[:]).then_inc(centring, 1)
                    v.wait_ge(centring, 3 * i + 2)
                    v.tensor_scalar(weight[:, slot:slot + 1], moment_y[:, slot, 0:1], t.dis_back[:, at(i)], None,
                                    ALU.mult).then_inc(centring, 1)
                    need(v, y_turned, i - 1)
                    v.tensor_scalar(y[:, slot], acc, moment_y[:, slot, 0:1], t.dis_back[:, at(i)], ALU.subtract,
                                    ALU.mult).then_inc(y_ready, 1)

                def add(i, slot):
                    v.wait_ge(g_done, i + 1)
                    v.wait_ge(centring, 3 * i + 3)
                    need(v, sums, 3 * i)
                    v.scalar_tensor_tensor(part[:], b_gnn[:], weight[:, slot:slot + 1], ps_g[slot][:], ALU.mult,
                                           ALU.add).then_inc(sums, 1)
                    v.wait_ge(sums, 3 * i + 1)
                    v.wait_ge(a_done, i + 1)
                    v.scalar_tensor_tensor(part[:], part[:], 0.0, ps_a[slot][:], ALU.max, ALU.add).then_inc(sums, 1)
                    v.wait_ge(sums, 3 * i + 2)
                    v.wait_ge(x_biased, i + 1)
                    v.wait_ge(y_ready, i + 1)
                    v.tensor_tensor(t.acc[:, at(i)].squeeze(1), part[:], x[:, slot], ALU.add).then_inc(sums, 1)

                def statistics(i, slot):
                    v.wait_ge(sums, 3 * i + 3)
                    need(v, ln, 3 * i)
                    v.sem_inc(go, 1)
                    v.bn_stats(stats_x1[:], t.acc[:, at(i)].squeeze(1)).then_inc(ln, 1)
                    v.wait_ge(ln, 3 * i + 1)
                    need(v, tok_ready, i - 1)
                    v.sem_inc(go, 1)
                    v.bn_aggr(moment_x1[:, slot], stats_x1[:]).then_inc(ln, 1)
                    v.wait_ge(ln, 3 * i + 2)
                    v.tensor_scalar(var[:, slot:slot + 1], moment_x1[:, slot, 1:2], EPS, None, ALU.add).then_inc(ln, 1)

                def normalize(i, slot):
                    v.wait_ge(rooted, i + 1)
                    v.wait_ge(ln, 3 * i + 2)
                    need(v, tok_turned, i - 1)
                    need(v, tok_stored[slot], 8 * (i - slot))
                    v.tensor_scalar(tok[:, slot], t.acc[:, at(i)].squeeze(1), moment_x1[:, slot, 0:1], rstd[:, slot:slot + 1],
                                    ALU.subtract, ALU.mult).then_inc(tok_ready, 1)

                def keep(i, slot):
                    v.wait_ge(gated, i + 1)
                    v.tensor_tensor(t.gate[:, at(i)].squeeze(1), ps_gate[slot][:, 0:GATE], b_gate[:], ALU.add).then_inc(gate_read, 1)

                def body(i, slot, has):
                    if has(i - 1):
                        add(i - 1, 1 - slot)
                        statistics(i - 1, 1 - slot)
                    if has(i + 1):
                        centre(i + 1, 1 - slot)
                    if has(i - 1):
                        normalize(i - 1, 1 - slot)
                    if has(i - 3):
                        keep(i - 3, 1 - slot)

                pipeline(v, body)

            @block.scalar
            def _(a):
                x1_rows = dram["x1"].rearrange("(t p) d -> t p d", p=P)
                tok_rows = dram["tok"].rearrange("(t p) d -> t p d", p=P)

                def body(i, slot, has):
                    if has(i - 1):
                        a.wait_ge(sums, 3 * i)
                        need(a, x1_stored, 16 * (i - 1))
                        a.dma_start(x1_rows[at(i - 1)].squeeze(0), t.acc[:, at(i - 1)].squeeze(1)).then_inc(x1_stored, 16)
                    if has(i + 1):
                        a.wait_ge(y_turned, i + 2)
                        need(a, g_done, i)
                        a.copy(yt[:, 1 - slot], ps_yt[:]).then_inc(yt_ready, 1)
                    if has(i - 1):
                        a.wait_ge(tok_ready, i)
                        a.dma_start(tok_rows[at(i - 1)].squeeze(0), tok[:, 1 - slot]).then_inc(tok_stored[1 - slot], 16)
                        a.wait_ge(tok_turned, i)
                        need(a, gated, i - 2)
                        a.copy(tt[:, 1 - slot], ps_tt[:]).then_inc(tt_ready, 1)

                pipeline(a, body)
                a.wait_ge(x1_stored, 16 * T)
                for slot, n in ((0, T // 2 + 1), (1, T // 2)):
                    a.wait_ge(tok_stored[slot], 16 * n)

            @block.tensor
            def _(pe):
                pe.wait_ge(load_w, 5 * 16)

                def attention(i, slot):
                    pe.wait_ge(load_xt[slot], 8 * (i - slot) + 16)
                    need(pe, sums, 3 * i - 4)
                    for k in range(KD):
                        mm = pe.matmul(ps_a[slot][:], xt[:, slot, k * P:(k + 1) * P], t.m[:, k], start=k == 0, stop=k == KD - 1)
                    mm.then_inc(a_done, 1)

                def gnn(i, slot):
                    pe.wait_ge(yt_ready, i + 1)
                    need(pe, sums, 3 * i - 5)
                    for k in range(KD):
                        mm = pe.matmul(ps_g[slot][:], yt[:, slot, k * P:(k + 1) * P], wg[:, k], start=k == 0, stop=k == KD - 1)
                    mm.then_inc(g_done, 1)

                def turn(i, slot, rows, ready, bank, emptied, turned):
                    pe.wait_ge(ready, i + 1)
                    need(pe, emptied, i)
                    for k in range(KD):
                        tr = pe.transpose(bank[:, k * P:(k + 1) * P], rows[:, slot, k * P:(k + 1) * P], t.ident[:])
                    tr.then_inc(turned, 1)

                def gate(i, slot):
                    pe.wait_ge(tt_ready, i + 1)
                    need(pe, gate_read, i - 1)
                    for k in range(KD):
                        mm = pe.matmul(ps_gate[slot][:, 0:GATE], tt[:, slot, k * P:(k + 1) * P], w_gate[:, k], start=k == 0,
                                       stop=k == KD - 1)
                    mm.then_inc(gated, 1)

                def body(i, slot, has):
                    if has(i):
                        attention(i, slot)
                    if has(i - 2):
                        gate(i - 2, slot)
                    if has(i):
                        gnn(i, slot)
                    if has(i + 1):
                        turn(i + 1, 1 - slot, y, y_ready, ps_yt, yt_ready, y_turned)
                    if has(i - 1):
                        turn(i - 1, 1 - slot, tok, tok_ready, ps_tt, tt_ready, tok_turned)

                pipeline(pe, body)


def route(nc, s, t, dram):
    with ExitStack() as ctx:
        sb, ps, sem = allocate(nc, ctx, "route", t.lasting)
        T, E, S = s.tiles, EXPERTS, s.slot_tiles
        w = sb("w", [P, E, GATE])
        b = sb("b", [P, E])
        ids = sb("ids", [P, T])
        upper = sb("upper", [P, P])
        ones = sb("ones", [P, P])
        products = sb("products", [P, T, E, GATE])
        logits = sb("logits", [P, T, E])
        order = sb("order", [P, E])
        top = sb("top", [P, 2, T])
        same = sb("same", [P, T, E])
        pick = sb("pick", [P, T])
        hot = sb("hot", [P, 2, T, E])
        mask = sb("mask", [P, T, E])
        down = sb("down", [P, T])
        rank = sb("rank", [P, T, E])
        total = sb("total", [P, T, E])
        run = [sb("run0", [P, T, E]), sb("run1", [P, T, E])]
        count = sb("count", [P, E])
        count_int = sb("count_int", [P, 2, E], I32)
        tiles_of = sb("tiles_of", [P, E])
        ends = [sb("ends0", [P, E]), sb("ends1", [P, E])]
        base = sb("base", [P, E])
        slot = sb("slot", [P, T, 2])
        slot_low = sb("slot_low", [P, T, 2], I32)
        slot_high = sb("slot_high", [P, T, 2], I32)
        low = sb("low", [P, T, 2])
        high = sb("high", [P, T, 2])
        reached = sb("reached", [1, S, E])
        expert = sb("expert", [1, S + 9])
        packed = sb("packed", [1, S + 4])
        B = s.group
        hot_low = sb("hot_low", [P, 2, 2 * B, P])
        hot_high = sb("hot_high", [P, 2, 2 * B, S])
        ps_rank = ps("ps_rank", [P, 512])
        ps_total = ps("ps_total", [P, 512])
        ps_list = ps("ps_list", [P, 512])
        loaded = sem("loaded")
        gelu = sem("gelu")
        steps = sem("steps")
        one = sem("one")
        exp_in = sem("exp_in")
        exp_out = sem("exp_out")
        masked = sem("masked")
        ranked = sem("ranked")
        low_hot = sem("low_hot")
        high_hot = sem("high_hot")
        high_ids = sem("high_ids")
        listed = sem("listed")
        opened = sem("opened")

        with nc.Block() as block:

            @block.sync
            def _(sp):
                sp.dma_start(w[:], dram["w_gate2"].partition_broadcast(P)).then_inc(loaded, 16)
                sp.dma_start(b[:], dram["b_gate2"].partition_broadcast(P)).then_inc(loaded, 16)
                sp.dma_start(ids[:], dram["ids"]).then_inc(loaded, 16)
                sp.dma_start(upper[:], dram["upper"]).then_inc(loaded, 16)
                for n in range(3):
                    sp.dma_start(t.expert_w[n][:], dram[f"w{n + 1}"]).then_inc(t.expert_loaded, 16)
                    sp.dma_start(t.expert_b[n][:], dram[f"b{n + 1}"].partition_broadcast(P)).then_inc(t.expert_loaded, 16)
                sp.dma_start(t.expert_affine[:], dram["affine"]).then_inc(t.expert_loaded, 16)

            @block.gpsimd
            def _(pool):
                pool.memset(expert[:], 0.0).then_inc(one, 1)
                pool.memset(ones[:], 1.0).then_inc(one, 1)
                pool.wait_ge(loaded, 64)
                for g in range(T // B):
                    hots = hot_high[:, g % 2].rearrange("p (t n) s -> p t (n s)", n=2)
                    pool.wait_ge(high_hot, g + 1)
                    pool.tensor_tensor(hots, hots, ids[:, g * B:(g + 1) * B].unsqueeze(2).to_broadcast([P, B, 2 * S]),
                                       ALU.mult).then_inc(high_ids, 1)

            @block.scalar
            def _(a):
                a.activation(t.gate[:], t.gate[:], ACT.Gelu).then_inc(gelu, 1)
                a.wait_ge(exp_in, 1)
                a.activation(down[:], down[:], ACT.Exp).then_inc(exp_out, 1)

            @block.vector
            def _(v):
                step = Chain(v, steps)
                over_t = lambda a: a.unsqueeze(1).to_broadcast([P, T, E])
                over_e = lambda a: a.unsqueeze(2).to_broadcast([P, T, E])
                v.wait_ge(loaded, 64)
                step.mark(v.tensor_scalar(order[:], t.iota[:, 0:E], -1.0, float(E), ALU.mult, ALU.add))
                v.wait_ge(gelu, 1)
                step.then(v.tensor_tensor(products[:], t.gate[:].unsqueeze(2).to_broadcast([P, T, E, GATE]),
                                          w[:].unsqueeze(1).to_broadcast([P, T, E, GATE]), ALU.mult))
                step.then(v.tensor_reduce(logits[:], products[:], AX.X, ALU.add))
                step.then(v.tensor_tensor(logits[:], logits[:], over_t(b[:]), ALU.add))
                for n in range(2):
                    step.then(v.tensor_reduce(top[:, n], logits[:], AX.X, ALU.max))
                    step.then(v.tensor_tensor(same[:], logits[:], over_e(top[:, n]), ALU.is_equal))
                    step.then(v.tensor_tensor(same[:], same[:], over_t(order[:]), ALU.mult))
                    step.then(v.tensor_reduce(pick[:], same[:], AX.X, ALU.max))
                    step.then(v.tensor_tensor(hot[:, n], over_t(order[:]), over_e(pick[:]), ALU.is_equal))
                    if n == 0:
                        step.then(v.scalar_tensor_tensor(logits[:], hot[:, 0], -3.0e38, logits[:], ALU.mult, ALU.add))
                step.then(v.tensor_tensor(down[:], top[:, 1], top[:, 0], ALU.subtract))
                v.sem_inc(exp_in, 1)
                step.then(v.tensor_tensor(mask[:], hot[:, 0], hot[:, 1], ALU.add))
                v.sem_inc(masked, 1)
                v.wait_ge(exp_out, 1)
                step.then(v.tensor_scalar(pick[:], down[:], 1.0, None, ALU.add))
                step.then(v.reciprocal(t.weight[:, :, 0], pick[:]))
                step.mark(v.tensor_tensor(t.weight[:, :, 1], t.weight[:, :, 0], down[:], ALU.mult))
                v.wait_ge(ranked, 1)
                step.mark(v.tensor_copy(rank[:], ps_rank[:, 0:T * E]))
                step.mark(v.tensor_copy(total[:], ps_total[:, 0:T * E]))
                step.then(v.tensor_copy(run[0][:], ps_total[:, 0:T * E]))
                now, shift = 0, 1
                while shift < T:
                    old, new = run[now], run[1 - now]
                    step.mark(v.tensor_copy(new[:, 0:shift], old[:, 0:shift]))
                    step.then(v.tensor_tensor(new[:, shift:], old[:, shift:], old[:, 0:T - shift], ALU.add))
                    now, shift = 1 - now, 2 * shift
                step.mark(v.tensor_copy(count_int[:, 0], run[now][:, T - 1]))
                step.then(v.tensor_tensor(rank[:], rank[:], run[now][:], ALU.add))
                step.then(v.tensor_tensor(rank[:], rank[:], total[:], ALU.subtract))
                step.then(v.tensor_scalar(count[:], count_int[:, 0], float(P - 1), None, ALU.add))
                step.then(v.tensor_copy(count_int[:, 0], count[:]))
                step.then(v.tensor_single_scalar(count_int[:, 1], count_int[:, 0], 7, op=ALU.logical_shift_right))
                step.mark(v.tensor_copy(tiles_of[:], count_int[:, 1]))
                step.then(v.tensor_copy(ends[0][:], count_int[:, 1]))
                now, shift = 0, 1
                while shift < E:
                    old, new = ends[now], ends[1 - now]
                    step.mark(v.tensor_copy(new[:, 0:shift], old[:, 0:shift]))
                    step.then(v.tensor_tensor(new[:, shift:], old[:, shift:], old[:, 0:E - shift], ALU.add))
                    now, shift = 1 - now, 2 * shift
                end = ends[now]
                step.then(v.tensor_tensor(base[:], end[:], tiles_of[:], ALU.subtract))
                step.then(v.tensor_scalar(base[:], base[:], float(P), None, ALU.mult))
                step.then(v.tensor_tensor(rank[:], rank[:], over_t(base[:]), ALU.add))
                for n in range(2):
                    step.then(v.tensor_tensor(same[:], hot[:, n], rank[:], ALU.mult))
                    step.then(v.tensor_reduce(slot[:, :, n], same[:], AX.X, ALU.add))
                step.then(v.tensor_copy(t.slot[:], slot[:]))
                step.mark(v.tensor_single_scalar(slot_low[:], t.slot[:], P - 1, op=ALU.bitwise_and))
                step.then(v.tensor_single_scalar(slot_high[:], t.slot[:], 7, op=ALU.logical_shift_right))
                step.mark(v.tensor_copy(low[:], slot_low[:]))
                step.mark(v.tensor_copy(high[:], slot_high[:]))
                steps_row = [1, S, E]
                step.then(v.tensor_tensor(reached[:], t.iota[0:1, 0:S].unsqueeze(2).to_broadcast(steps_row),
                                          end[0:1].unsqueeze(1).to_broadcast(steps_row), ALU.is_ge))
                v.wait_ge(one, 1)
                tiles = expert[:, 4:4 + S]
                step.then(v.tensor_reduce(tiles, reached[:], AX.X, ALU.add))
                step.then(v.tensor_scalar(tiles, tiles, float(E - 1), None, ALU.min))
                step.then(v.tensor_copy(packed[:], expert[:, 5:]))
                for k in range(1, 6):
                    step.then(v.scalar_tensor_tensor(packed[:], expert[:, 5 - k:S + 9 - k], float(1 << 4 * k), packed[:],
                                                     ALU.mult, ALU.add))
                step.then(v.tensor_copy(t.expert[:], packed[:]))

                for g in range(T // B):
                    if g > 1:
                        v.wait_ge(listed, g - 1)
                    for hots, width, which, done in ((hot_high, S, high, high_hot), (hot_low, P, low, low_hot)):
                        shape = [P, 2 * B, width]
                        v.tensor_tensor(hots[:, g % 2], t.iota[:, 0:width].unsqueeze(1).to_broadcast(shape),
                                        which[:, g * B:(g + 1) * B].rearrange("p t n -> p (t n)").unsqueeze(2).to_broadcast(shape),
                                        ALU.is_equal).then_inc(done, 1)
                v.wait_ge(listed, T // B)
                v.tensor_copy(t.token[:], ps_list[:, 0:S])

            @block.tensor
            def _(pe):
                pe.wait_ge(loaded, 64)
                pe.wait_ge(one, 2)
                pe.wait_ge(masked, 1)
                pe.matmul(ps_rank[:, 0:T * E], upper[:], mask[:].rearrange("p t e -> p (t e)"), start=True, stop=True)
                pe.matmul(ps_total[:, 0:T * E], ones[:], mask[:].rearrange("p t e -> p (t e)"), start=True,
                          stop=True).then_inc(ranked, 1)

                for g in range(T // B):
                    pe.wait_ge(low_hot, g + 1)
                    pe.wait_ge(high_ids, g + 1)
                    for k in range(2 * B):
                        mm = pe.matmul(ps_list[:, 0:S], hot_low[:, g % 2, k], hot_high[:, g % 2, k], start=g == 0 and k == 0,
                                       stop=g == T // B - 1 and k == 2 * B - 1)
                    mm.then_inc(listed, 1)


def experts(nc, s, t, dram):
    with ExitStack() as ctx:
        sb, ps, sem = allocate(nc, ctx, "experts", t.lasting)
        E, N = EXPERTS, s.slot_tiles
        KH = H2 // P
        w, b, affine, load_w = t.expert_w, t.expert_b, t.expert_affine, t.expert_loaded
        index = sb("index", [P, 2, 1], I32)
        rows = sb("rows", [P, 2, D])
        xt = sb("xt", [P, 2, D])
        h = [sb("h1", [P, H2]), sb("h2", [P, H2])]
        stats = sb("stats", [P, 2, 6])
        moment = sb("moment", [P, 2, 2])
        var = sb("var", [P, 2])
        power = sb("power", [P, 1])
        rstd = sb("rstd", [P, 2])
        v_ = [sb("v1", [P, H2]), sb("v2", [P, H2])]
        a_ = [sb("a1", [P, 1, H2]), sb("a2", [P, 2, H2])]
        product = sb("product", [P, 2, D])
        o = sb("o", [P, 2, D])
        ps_t = [ps(f"ps_t{i}", [P, D]) for i in range(2)]
        ps_h = [ps(f"ps_h{i}", [P, D]) for i in range(2)]
        ps_u = [ps(f"ps_u{i}", [P, D]) for i in range(2)]
        ps_o = [ps(f"ps_o{i}", [P, D]) for i in range(2)]
        indexed = sem("indexed")
        powered = sem("powered")
        go = sem("go")
        gathered = [sem(f"gathered{i}") for i in range(2)]
        turned = sem("turned")
        xt_ready = sem("xt_ready")
        h_done = [sem("h1_done"), sem("h2_done")]
        ln = [sem("ln1"), sem("ln2")]
        rooted = [sem("rooted1"), sem("rooted2")]
        v_ready = [sem("v1_ready"), sem("v2_ready")]
        u_done = [sem("u1_done"), sem("u2_done")]
        a_ready = [sem("a1_ready"), sem("a2_ready")]
        o_done = sem("o_done")
        o_copied = sem("o_copied")
        o_ready = sem("o_ready")
        stored = [sem(f"stored{i}") for i in range(2)]

        def pipeline(engine, body):
            has = lambda i: not isinstance(i, int) or 0 <= i < N
            for i in range(-1, 6):
                body(i, i % 2, has)
            with engine.Fori(3, (N - 4) // 2) as pair:
                body(2 * pair, 0, lambda i: True)
                body(2 * pair + 1, 1, lambda i: True)
            for i in range(N - 4, N + 4):
                body(i, i % 2, has)

        def experts_of(engine, i, slot, tiles, has, held):
            if not any(has(i - k) for k in tiles):
                return {}
            if slot == 0 or isinstance(i, int):
                held["packed"] = engine.value_load(t.expert[0:1, at(i - slot)], min_val=0, max_val=(1 << 24) - 1)
            return {k: (held["packed"] >> 4 * (k + 1 - slot)) & (E - 1) for k in tiles if has(i - k)}

        with nc.Block() as block:

            @block.sync
            def _(sp):
                slots = dram["slots"].rearrange("(t p) d -> t p d", p=P)

                def store(i, slot, has):
                    if has(i):
                        sp.wait_ge(o_ready, i + 1)
                        sp.dma_start(slots[at(i)].squeeze(0), o[:, slot]).then_inc(stored[slot], 16)

                pipeline(sp, store)
                for slot in range(2):
                    sp.wait_ge(stored[slot], 8 * N)

            @block.gpsimd
            def _(pool):
                held = {}
                pool.wait_ge(load_w, 7 * 16)
                pool.memset(power[:], -0.5).then_inc(powered, 1)
                pool.wait_ge(powered, 1)

                def gather(i, slot):
                    need(pool, turned, i - 1)
                    pool.sem_inc(go, 1)
                    pool.tensor_copy(index[:, slot], t.token[:, at(i)]).then_inc(indexed, 1)
                    pool.wait_ge(indexed, i + 1)
                    pool.sem_inc(go, 1)
                    pool.indirect_dma_start(rows[:, slot], None, dram["tok"],
                                            bass.IndirectOffsetOnAxis(ap=index[:, slot], axis=0)).then_inc(gathered[slot], 16)

                def root(i, layer):
                    pool.wait_ge(ln[layer], 4 * i + 4)
                    pool.tensor_tensor(rstd[:, layer:layer + 1], var[:, layer:layer + 1], power[:], ALU.pow)\
                        .then_inc(rooted[layer], 1)

                def finish(i, slot, e):
                    pool.wait_ge(o_copied, i + 1)
                    need(pool, stored[slot], 8 * (i - slot))
                    pool.tensor_tensor(o[:, slot], product[:, slot], b[2][:, at(e)].squeeze(1), ALU.add).then_inc(o_ready, 1)

                def body(i, slot, has):
                    e = experts_of(pool, i, slot, (4,), has, held)
                    if has(i - 2):
                        root(i - 2, 1)
                    if not isinstance(i, int) or 0 <= i < N - 2:
                        gather(i + 2, slot)
                    if has(i):
                        root(i, 0)
                    if has(i - 4):
                        finish(i - 4, slot, e[4])

                gather(0, 0)
                gather(1, 1)
                pipeline(pool, body)

            @block.vector
            def _(v):
                held = {}
                v.wait_ge(load_w, 7 * 16)

                def add_bias(i, layer, e):
                    v.wait_ge(h_done[layer], i + 1)
                    need(v, v_ready[layer], i)
                    v.tensor_tensor(h[layer][:], ps_h[layer][:, 0:H2], b[layer][:, at(e)].squeeze(1),
                                    ALU.add).then_inc(ln[layer], 1)

                def statistics(i, layer):
                    v.wait_ge(ln[layer], 4 * i + 1)
                    v.bn_stats(stats[:, layer], h[layer][:]).then_inc(ln[layer], 1)

                def moments_of(i, layer):
                    v.wait_ge(ln[layer], 4 * i + 2)
                    v.sem_inc(go, 1)
                    v.bn_aggr(moment[:, layer], stats[:, layer]).then_inc(ln[layer], 1)

                def guarded_variance(i, layer):
                    v.wait_ge(ln[layer], 4 * i + 3)
                    v.tensor_scalar(var[:, layer:layer + 1], moment[:, layer, 1:2], EPS, None, ALU.add).then_inc(ln[layer], 1)

                def normalize(i, layer):
                    v.wait_ge(rooted[layer], i + 1)
                    need(v, u_done[layer], i)
                    v.tensor_scalar(v_[layer][:], h[layer][:], moment[:, layer, 0:1], rstd[:, layer:layer + 1], ALU.subtract,
                                    ALU.mult).then_inc(v_ready[layer], 1)

                def body(i, slot, has):
                    e = experts_of(v, i, slot, (0, 2), has, held)
                    for tile, layer in ((i - 2, 1), (i, 0)):
                        if has(tile):
                            add_bias(tile, layer, e[2 * layer])
                            for part in (statistics, moments_of, guarded_variance):
                                part(tile, layer)
                        if has(tile):
                            normalize(tile, layer)

                pipeline(v, body)

            @block.scalar
            def _(a):
                held = {}
                a.wait_ge(load_w, 7 * 16)

                def evacuate(i, slot):
                    a.wait_ge(turned, i + 1)
                    need(a, h_done[0], i - 1)
                    a.copy(xt[:, slot], ps_t[slot][:]).then_inc(xt_ready, 1)

                def copy_product(i, slot):
                    a.wait_ge(o_done, i + 1)
                    need(a, o_ready, i - 1)
                    a.copy(product[:, slot], ps_o[slot][:]).then_inc(o_copied, 1)

                def gelu(i, layer, e, buffer):
                    a.wait_ge(u_done[layer], i + 1)
                    need(a, *((h_done[1], i), (o_done, i - 1))[layer])
                    for k in range(KH):
                        cols = slice(k * P, (k + 1) * P)
                        a.activation(a_[layer][:, buffer, cols], ps_u[layer][:, cols], ACT.Gelu,
                                     bias=affine[:, layer, 1, k, at(e)], scale=affine[:, layer, 0, k, at(e)])\
                            .then_inc(a_ready[layer], 1)

                def body(i, slot, has):
                    e = experts_of(a, i, slot, (1, 2), has, held)
                    if has(i - 1):
                        gelu(i - 1, 0, e[1], 0)
                    if has(i - 2):
                        gelu(i - 2, 1, e[2], slot)
                    if has(i + 1):
                        evacuate(i + 1, 1 - slot)
                    if has(i - 4):
                        copy_product(i - 4, slot)

                pipeline(a, body)

            @block.tensor
            def _(pe):
                held = {}
                pe.wait_ge(load_w, 7 * 16)

                def turn_rows(i, slot):
                    pe.wait_ge(gathered[slot], 8 * (i - slot) + 16)
                    need(pe, xt_ready, i - 1)
                    for k in range(KD):
                        tr = pe.transpose(ps_t[slot][:, k * P:(k + 1) * P], rows[:, slot, k * P:(k + 1) * P], t.ident[:])
                    tr.then_inc(turned, 1)

                def turn(i, layer):
                    pe.wait_ge(v_ready[layer], i + 1)
                    need(pe, a_ready[layer], 2 * i)
                    for k in range(KH):
                        cols = slice(k * P, (k + 1) * P)
                        tr = pe.transpose(ps_u[layer][:, cols], v_[layer][:, cols], t.ident[:])
                    tr.then_inc(u_done[layer], 1)

                def layer1(i, slot, e):
                    pe.wait_ge(xt_ready, i + 1)
                    need(pe, ln[0], 4 * i - 3)
                    for k in range(KD):
                        mm = pe.matmul(ps_h[0][:, 0:H2], xt[:, slot, k * P:(k + 1) * P], w[0][:, k, at(e)].squeeze(1),
                                       start=k == 0, stop=k == KD - 1)
                    mm.then_inc(h_done[0], 1)

                def layer2(i, e):
                    pe.wait_ge(a_ready[0], 2 * i + 2)
                    need(pe, ln[1], 4 * i - 3)
                    for k in range(KH):
                        mm = pe.matmul(ps_h[1][:, 0:H2], a_[0][:, 0, k * P:(k + 1) * P], w[1][:, k, at(e)].squeeze(1),
                                       start=k == 0, stop=k == KH - 1)
                    mm.then_inc(h_done[1], 1)

                def layer3(i, slot, e):
                    pe.wait_ge(a_ready[1], 2 * i + 2)
                    need(pe, o_copied, i - 1)
                    for k in range(KH):
                        mm = pe.matmul(ps_o[slot][:], a_[1][:, slot, k * P:(k + 1) * P], w[2][:, k, at(e)].squeeze(1),
                                       start=k == 0, stop=k == KH - 1)
                    mm.then_inc(o_done, 1)

                def body(i, slot, has):
                    e = experts_of(pe, i, slot, (0, 1, 3), has, held)
                    if has(i - 1):
                        turn(i - 1, 0)
                    if has(i):
                        layer1(i, slot, e[0])
                    if has(i - 1):
                        layer2(i - 1, e[1])
                    if has(i - 2):
                        turn(i - 2, 1)
                    if has(i + 1):
                        turn_rows(i + 1, 1 - slot)
                    if has(i - 3):
                        layer3(i - 3, 1 - slot, e[3])

                pipeline(pe, body)


def combine(nc, s, t, dram):
    with ExitStack() as ctx:
        sb, ps, sem = allocate(nc, ctx, "combine", t.lasting)
        T, ROWS = s.tiles, 6
        index = sb("index", [P, 2, ROWS, 2], I32)
        rows = sb("rows", [P, ROWS, 2, D])
        x1 = sb("x1", [P, ROWS, D])
        partial = sb("partial", [P, ROWS, D])
        out = sb("out", [P, ROWS, D])
        go = sem("go")
        indexed = sem("indexed")
        gathered = [sem(f"gathered{i}") for i in range(ROWS)]
        load_x1 = [sem(f"load_x1{i}") for i in range(ROWS)]
        half = sem("half")
        done = sem("done")
        stored = [sem(f"stored{i}") for i in range(ROWS)]

        with nc.Block() as block:

            @block.gpsimd
            def _(pool):
                def gather(first, parity, tiles):
                    need(pool, done, first - ROWS)
                    pool.sem_inc(go, 1)
                    pool.tensor_copy(index[:, parity, 0:tiles], t.slot[:, at(first, tiles)]).then_inc(indexed, ROWS)
                    pool.wait_ge(indexed, first + ROWS)
                    for slot in range(tiles):
                        need(pool, done, first + slot - ROWS + 1)
                        pool.sem_inc(go, 1)
                        for n in range(2):
                            pool.indirect_dma_start(rows[:, slot, n], None, dram["slots"],
                                                    bass.IndirectOffsetOnAxis(ap=index[:, parity, slot, n:n + 1], axis=0))\
                                .then_inc(gathered[slot], 16)

                gather(0, 0, ROWS)
                gather(ROWS, 1, ROWS)
                with pool.Fori(1, T // (2 * ROWS)) as r:
                    gather(2 * ROWS * r, 0, ROWS)
                    gather(2 * ROWS * r + ROWS, 1, ROWS)
                for first in range(T // (2 * ROWS) * 2 * ROWS, T, ROWS):
                    gather(first, first // ROWS % 2, min(ROWS, T - first))

            @block.sync
            def _(sp):
                xv = dram["x1"].rearrange("(t p) d -> t p d", p=P)

                def load(i, slot, r):
                    need(sp, half, i - ROWS + 1)
                    sp.dma_start(x1[:, slot], xv[at(i)].squeeze(0)).then_inc(load_x1[slot], 16)

                by_rounds(sp, T, load, ROWS)

            @block.vector
            def _(v):
                def add(i, slot, r):
                    v.wait_ge(load_x1[slot], 16 * r + 16)
                    v.wait_ge(gathered[slot], 32 * r + 32)
                    need(v, done, i - ROWS + 1)
                    v.scalar_tensor_tensor(partial[:, slot], rows[:, slot, 0], t.weight[:, at(i), 0], x1[:, slot], ALU.mult,
                                           ALU.add).then_inc(half, 1)
                    v.wait_ge(half, i + 1)
                    need(v, stored[slot], 16 * r)
                    v.scalar_tensor_tensor(out[:, slot], rows[:, slot, 1], t.weight[:, at(i), 1], partial[:, slot], ALU.mult,
                                           ALU.add).then_inc(done, 1)

                by_rounds(v, T, add, ROWS)

            @block.scalar
            def _(a):
                ov = dram["out"].rearrange("(t p) d -> t p d", p=P)

                def store(i, slot, r):
                    a.wait_ge(done, i + 1)
                    a.dma_start(ov[at(i)].squeeze(0), out[:, slot]).then_inc(stored[slot], 16)

                by_rounds(a, T, store, ROWS)
                for slot in range(ROWS):
                    a.wait_ge(stored[slot], 16 * len(range(slot, T, ROWS)))


def build(nc, dram, sizes):
    s = shapes(*sizes)
    t = lambda: None
    with ExitStack() as ctx:
        t.lasting = ctx
        sb, ps, sem = allocate(nc, ctx, "all")
        t.ident = sb("ident", [P, P])
        t.iota = sb("iota", [P, P], F16)
        t.neg_block = sb("neg_block", [P, s.tiles])
        t.visits = sb("visits", [1, s.supers], I32)
        t.mean = sb("mean", [P, s.tiles])
        t.rstd = sb("rstd", [P, s.tiles])
        t.dis = sb("dis", [P, s.tiles])
        t.dis_table = sb("dis_table", [P, s.tiles])
        t.dis_back = sb("dis_back", [P, s.tiles])
        t.p = sb("p", [P, D])
        t.gate = sb("gate", [P, s.tiles, GATE])
        t.weight = sb("weight", [P, s.tiles, 2])
        t.slot = sb("slot", [P, s.tiles, 2], I32)
        t.token = sb("token", [P, s.slot_tiles], I32)
        t.expert = sb("expert", [1, s.slot_tiles + 4], I32)
        with ExitStack() as gathering:
            sb, ps, sem = allocate(nc, gathering, "graph", ctx)
            t.acc = sb("acc", [P, s.tiles, D])
            t.src = sb("src", [P, s.chunks], I32)
            t.dst = sb("dst", [P, s.chunks])
            prepare_edges(nc, s, t, dram)
            prepare_table(nc, s, t, dram)
            aggregate(nc, s, t, dram)
            t.m = sb("m", [P, KD, D])
            fold(nc, s, t, dram)
            mix(nc, s, t, dram)
        with ExitStack() as routing:
            sb, ps, sem = allocate(nc, routing, "expert", ctx)
            KH = H2 // P
            t.expert_w = [sb("w1", [P, KD, EXPERTS, H2]), sb("w2", [P, KH, EXPERTS, H2]), sb("w3", [P, KH, EXPERTS, D])]
            t.expert_b = [sb("b1", [P, EXPERTS, H2]), sb("b2", [P, EXPERTS, H2]), sb("b3", [P, EXPERTS, D])]
            t.expert_affine = sb("affine", [P, 2, 2, KH, EXPERTS])
            t.expert_loaded = sem("loaded")
            route(nc, s, t, dram)
            experts(nc, s, t, dram)
        combine(nc, s, t, dram)


def kernel(**inputs):
    import concourse.bacc as bacc
    from concourse.bass_utils import run_bass_kernel_spmd as run

    x, src, dst = (np.asarray(inputs[n]) for n in ("x", "src", "dst"))
    sizes = (x.shape[0], src.shape[0])
    s = shapes(*sizes)
    rows = s.tiles * P

    def edges(a):
        padded = np.concatenate([a, np.full(s.chunks * P - a.shape[0], rows - 1, a.dtype)])
        return np.ascontiguousarray(padded.reshape(s.chunks, P).T)

    def by_partition(a):
        experts, rows_in, columns = a.shape
        return np.ascontiguousarray(a.reshape(experts, rows_in // P, P, columns).transpose(2, 1, 0, 3))

    qkv = np.asarray(inputs["L0_mix_W_qkv"])
    cast = np.arange(P, dtype=np.float16)
    arrays = {
        "x": np.concatenate([x, np.zeros((rows - x.shape[0], D), x.dtype)]),
        "src": edges(src),
        "dst": edges(dst),
        "ident": np.eye(P, dtype=np.float32),
        "upper": np.triu(np.ones((P, P), np.float32), 1),
        "iota": np.tile(cast, (P, 1)),
        "w_q": np.ascontiguousarray(qkv[:D]),
        "w_out": np.ascontiguousarray(np.asarray(inputs["L0_mix_W_out"]).T),
        "b_out": np.asarray(inputs["L0_mix_b_out"]),
        "w_gnn": np.ascontiguousarray(np.asarray(inputs["L0_gnn_W"]).T),
        "b_gnn": np.asarray(inputs["L0_gnn_b"]),
        "w_gate1": np.asarray(inputs["L0_ffn_Wg1"]),
        "b_gate1": np.asarray(inputs["L0_ffn_bg1"]),
        "w_gate2": np.ascontiguousarray(np.asarray(inputs["L0_ffn_Wg2"]).T),
        "b_gate2": np.asarray(inputs["L0_ffn_bg2"]),
        "ids": np.ascontiguousarray(np.arange(rows, dtype=np.float32).reshape(s.tiles, P).T),
        **{f"w{n}": by_partition(np.asarray(inputs[f"L0_ffn_W{n}"])) for n in (1, 2, 3)},
        **{f"b{n}": np.asarray(inputs[f"L0_ffn_b{n}"]) for n in (1, 2, 3)},
        "affine": np.ascontiguousarray(np.stack([
            np.stack([np.asarray(inputs[f"L0_ffn_{kind}{n}"]).T.reshape(H2 // P, P, EXPERTS) for kind in ("g", "be")])
            for n in (1, 2)]).transpose(3, 0, 1, 2, 4)),
        "w_kv": np.ascontiguousarray(qkv[D:].T),
        "gamma_k": np.asarray(inputs["L0_mix_gamma_K"]).reshape(D),
        "beta_k": np.asarray(inputs["L0_mix_beta_K"]).reshape(D),
        "gamma_v": np.asarray(inputs["L0_mix_gamma_V"]).reshape(D),
        "beta_v": np.asarray(inputs["L0_mix_beta_V"]).reshape(D),
        "neg_block": np.tile(-P * np.arange(s.tiles, dtype=np.float32), (P, 1)),
    }
    nc = bacc.Bacc("TRN2", target_bir_lowering=False, num_devices=1)
    dram = {n: nc.dram_tensor(f"in_{n}", a.shape, mybir.dt.from_np(a.dtype), kind="ExternalInput").ap()
            for n, a in arrays.items()}
    dram["xt"] = nc.dram_tensor("xt_scratch", [s.tiles, P, D], F32, kind="Internal").ap()
    dram["table"] = nc.dram_tensor("table_scratch", [rows, 2 * D], F16, kind="Internal").ap()
    dram["x1"] = nc.dram_tensor("x1_scratch", [rows, D], F32, kind="Internal").ap()
    dram["tok"] = nc.dram_tensor("tok_scratch", [rows, D], F32, kind="Internal").ap()
    dram["slots"] = nc.dram_tensor("slots_scratch", [s.slot_tiles * P, D], F32, kind="Internal").ap()
    dram["out"] = nc.dram_tensor("out_rows", [rows, D], F32, kind="ExternalOutput").ap()
    build(nc, dram, sizes)
    r = run(nc, [{f"in_{n}": a for n, a in arrays.items()}], core_ids=[0])
    return r.results[0]["out_rows"][0:x.shape[0]]
```
